# Optimizing a Trainium2 kernel written in Bass

```python
import numpy as np
import jax
import jax.numpy as jnp

def _softmax(x, axis=-1):
    return jax.nn.softmax(x, axis=axis)

def _gelu(x):
    return jax.nn.gelu(x, approximate=True)

def _silu(x):
    return jax.nn.silu(x)

def _sigmoid(x):
    return jax.nn.sigmoid(x)

def _layernorm(x, axis=-1, eps=1e-05):
    m = jnp.mean(x, axis=axis, keepdims=True)
    v = jnp.var(x, axis=axis, keepdims=True)
    return (x - m) / jnp.sqrt(v + eps)

def _scatter_add(tgt, idx, src, axis=0):
    return tgt.at[idx].add(src)

def _segment_sum(src, seg, n):
    return jax.ops.segment_sum(src, seg, n)
kernel_name = 'mk_conv_attn_hybrid_d2_conv_nchw256_r2_5ba38e'

def setup_inputs(seed: int=0):
    np.random.seed(seed)
    _w = jnp.asarray

    def _rec_inputs():
        import jax
        import jax.numpy as jnp
        _gk = jax.random.key(seed)
        x = -0.0005207 + 1.001 * jax.random.normal(jax.random.fold_in(_gk, 1), (2, 128, 32, 32), jnp.float32)
        return x
    x = _rec_inputs()

    def _L0_conv_setup():
        import jax, jax.numpy as jnp
        import numpy as np
        KS = 7
        P = 3
        EPS = 1e-05

        def _unfold(xp, H, W, ks):
            i = jnp.arange(H)[:, None, None, None] + jnp.arange(ks)[None, None, :, None]
            j = jnp.arange(W)[None, :, None, None] + jnp.arange(ks)[None, None, None, :]
            return xp[:, :, i, j]
        key = jax.random.key(seed)
        ks = jax.random.split(key, 9)
        B, Cin, Cout, H, W = (2, 128, 128, 32, 32)
        s = 1.0 / np.sqrt(Cin)
        return {'x': jax.random.normal(ks[0], (B, Cin, H, W), dtype=jnp.float32), 'wq': jax.random.normal(ks[1], (Cout, Cin), dtype=jnp.float32) * s, 'bq': jax.random.normal(ks[2], (Cout,), dtype=jnp.float32) * 0.01, 'wk': jax.random.normal(ks[3], (Cout, Cin), dtype=jnp.float32) * s, 'bk': jax.random.normal(ks[4], (Cout,), dtype=jnp.float32) * 0.01, 'wv': jax.random.normal(ks[5], (Cout, Cin), dtype=jnp.float32) * s, 'bv': jax.random.normal(ks[6], (Cout,), dtype=jnp.float32) * 0.01, 'gamma': jnp.ones((Cout,), dtype=jnp.float32), 'beta': jnp.zeros((Cout,), dtype=jnp.float32)}
    _L0_conv_all = _L0_conv_setup()
    _L0_conv_in = {k: v for k, v in _L0_conv_all.items() if k in ('wq', 'bq', 'wk', 'bk', 'wv', 'bv', 'gamma', 'beta')}
    del _L0_conv_all

    def _L1_attn_setup():
        import jax, jax.numpy as jnp
        import numpy as np
        B, N, D, H = (4, 512, 128, 8)
        key = jax.random.key(seed)
        k1, k2, k3 = jax.random.split(key, 3)
        x = jax.random.normal(k1, (B, N, D), dtype=jnp.float32)
        Wqkv = jax.random.normal(k2, (D, 3 * D * H), dtype=jnp.float32) * 0.02
        bqkv = jnp.zeros((3 * D * H,), dtype=jnp.float32)
        W0 = jax.random.normal(k3, (D * H, D), dtype=jnp.float32) * 0.02
        b0 = jnp.zeros((D,), dtype=jnp.float32)
        return {'x': x, 'Wqkv': Wqkv, 'bqkv': bqkv, 'W0': W0, 'b0': b0}
    _L1_attn_all = _L1_attn_setup()
    _L1_attn_in = {k: v for k, v in _L1_attn_all.items() if k in ('Wqkv', 'bqkv', 'W0', 'b0')}
    del _L1_attn_all

    def _L1_ffn_setup():
        import math
        import jax, jax.numpy as jnp
        import numpy as np
        CAPACITY_FACTOR = 1.25
        TOP_K = 2
        LN_EPS = 1e-05

        def _layer_norm(x, gamma, beta):
            mu = jnp.mean(x, axis=-1, keepdims=True)
            var = jnp.var(x, axis=-1, keepdims=True)
            return (x - mu) * jax.lax.rsqrt(var + LN_EPS) * gamma + beta
        key = jax.random.key(seed)
        ks = jax.random.split(key, 4)
        B, S, D, F, E = (8, 2048, 128, 256, 8)
        x = jax.random.normal(ks[0], (B, S, D), dtype=jnp.float32)
        Wr = jax.random.normal(ks[1], (D, E), dtype=jnp.float32) / np.sqrt(D)
        br = jnp.zeros((E,), jnp.float32)
        W1 = jax.random.normal(ks[2], (E, D, F), dtype=jnp.float32) / np.sqrt(D)
        b1 = jnp.zeros((E, F), jnp.float32)
        W2 = jax.random.normal(ks[3], (E, F, D), dtype=jnp.float32) / np.sqrt(F)
        b2 = jnp.zeros((E, D), jnp.float32)
        gamma = jnp.ones((D,), jnp.float32)
        beta = jnp.zeros((D,), jnp.float32)
        return {'x': x, 'Wr': Wr, 'br': br, 'W1': W1, 'b1': b1, 'W2': W2, 'b2': b2, 'gamma': gamma, 'beta': beta}
    _L1_ffn_all = _L1_ffn_setup()
    _L1_ffn_in = {k: v for k, v in _L1_ffn_all.items() if k in ('Wr', 'br', 'W1', 'b1', 'W2', 'b2', 'gamma', 'beta')}
    del _L1_ffn_all
    return {'x': x, 'L0_conv_wq': _L0_conv_in['wq'], 'L0_conv_bq': _L0_conv_in['bq'], 'L0_conv_wk': _L0_conv_in['wk'], 'L0_conv_bk': _L0_conv_in['bk'], 'L0_conv_wv': _L0_conv_in['wv'], 'L0_conv_bv': _L0_conv_in['bv'], 'L0_conv_gamma': _L0_conv_in['gamma'], 'L0_conv_beta': _L0_conv_in['beta'], 'L1_attn_Wqkv': _L1_attn_in['Wqkv'], 'L1_attn_bqkv': _L1_attn_in['bqkv'], 'L1_attn_W0': _L1_attn_in['W0'], 'L1_attn_b0': _L1_attn_in['b0'], 'L1_ffn_Wr': _L1_ffn_in['Wr'], 'L1_ffn_br': _L1_ffn_in['br'], 'L1_ffn_W1': _L1_ffn_in['W1'], 'L1_ffn_b1': _L1_ffn_in['b1'], 'L1_ffn_W2': _L1_ffn_in['W2'], 'L1_ffn_b2': _L1_ffn_in['b2'], 'L1_ffn_gamma': _L1_ffn_in['gamma'], 'L1_ffn_beta': _L1_ffn_in['beta']}

def reference(x, L0_conv_wq, L0_conv_bq, L0_conv_wk, L0_conv_bk, L0_conv_wv, L0_conv_bv, L0_conv_gamma, L0_conv_beta, L1_attn_Wqkv, L1_attn_bqkv, L1_attn_W0, L1_attn_b0, L1_ffn_Wr, L1_ffn_br, L1_ffn_W1, L1_ffn_b1, L1_ffn_W2, L1_ffn_b2, L1_ffn_gamma, L1_ffn_beta):
    import jax
    import jax.numpy as jnp

    def _L0_conv_ref(x, wq, bq, wk, bk, wv, bv, gamma, beta):
        import jax, jax.numpy as jnp
        import numpy as np
        KS = 7
        P = 3
        EPS = 1e-05

        def _unfold(xp, H, W, ks):
            i = jnp.arange(H)[:, None, None, None] + jnp.arange(ks)[None, None, :, None]
            j = jnp.arange(W)[None, :, None, None] + jnp.arange(ks)[None, None, None, :]
            return xp[:, :, i, j]
        B, Cin, H, W = x.shape
        C = wq.shape[0]
        k2 = KS * KS
        q = jnp.einsum('bchw,oc->bohw', x, wq) + bq[None, :, None, None]
        k = jnp.einsum('bchw,oc->bohw', x, wk) + bk[None, :, None, None]
        v = jnp.einsum('bchw,oc->bohw', x, wv) + bv[None, :, None, None]
        pad = ((0, 0), (0, 0), (P, P), (P, P))
        kp = jnp.pad(k, pad)
        vp = jnp.pad(v, pad)
        ku = _unfold(kp, H, W, KS).reshape(B, C, k2, H, W)
        vu = _unfold(vp, H, W, KS).reshape(B, C, k2, H, W)
        frac = jnp.einsum('bchw,bcphw->bhwp', q, ku)
        frac = jnp.where(frac != 0, frac, -jnp.inf)
        attn = jax.nn.softmax(frac, axis=-1)
        out = jnp.einsum('bhwp,bcphw->bchw', attn, vu)
        mean = out.mean(axis=(0, 2, 3), keepdims=True)
        var = out.var(axis=(0, 2, 3), keepdims=True)
        out = (out - mean) * jax.lax.rsqrt(var + EPS)
        out = out * gamma[None, :, None, None] + beta[None, :, None, None]
        return jax.nn.relu(out)

    def _L1_attn_ref(x, Wqkv, bqkv, W0, b0):
        import jax, jax.numpy as jnp
        import numpy as np
        B, N, D, H = (4, 512, 128, 8)
        b, n, d = x.shape
        h = Wqkv.shape[1] // (3 * d)
        qkv = x @ Wqkv + bqkv
        q, k, v = jnp.reshape(qkv, (3, b, n, d, h))
        score = jnp.einsum('bnqh,btqh->bnth', q, k) * d ** (-0.5)
        attn = jax.nn.softmax(score, axis=1)
        av = jnp.einsum('bnnh,bnqh->bnqh', attn, v)
        out = av.reshape(b, n, d * h) @ W0 + b0
        return out

    def _L1_ffn_ref(x, Wr, br, W1, b1, W2, b2, gamma, beta):
        import math
        import jax, jax.numpy as jnp
        import numpy as np
        CAPACITY_FACTOR = 1.25
        TOP_K = 2
        LN_EPS = 1e-05

        def _layer_norm(x, gamma, beta):
            mu = jnp.mean(x, axis=-1, keepdims=True)
            var = jnp.var(x, axis=-1, keepdims=True)
            return (x - mu) * jax.lax.rsqrt(var + LN_EPS) * gamma + beta
        B, S, D = x.shape
        E = Wr.shape[1]
        N = B * S
        K = TOP_K
        logits = jnp.mean(x, axis=1) @ Wr + br
        routing_weights = jax.nn.softmax(logits, axis=-1)
        capacity = float(math.ceil(N * CAPACITY_FACTOR / E))
        expected_loads = routing_weights.sum(axis=0) * (N / B)
        scale = jnp.where(expected_loads > capacity, capacity / expected_loads, 1.0)
        routing_weights = jax.nn.softmax(routing_weights * scale, axis=-1)
        rw_tok = jnp.broadcast_to(routing_weights[:, None, :], (B, S, E)).reshape(N, E)
        top_w, top_i = jax.lax.top_k(rw_tok, K)
        top_w = jax.nn.softmax(top_w, axis=-1)
        xf = x.reshape(N, D)
        h = jax.nn.gelu(jnp.einsum('nd,edf->enf', xf, W1) + b1[:, None, :], approximate=False)
        y = jnp.einsum('enf,efd->end', h, W2) + b2[:, None, :]
        w_dense = jnp.zeros((N, E), x.dtype).at[jnp.arange(N)[:, None], top_i].add(top_w)
        out = jnp.einsum('ne,end->nd', w_dense, y).reshape(B, S, D)
        out = _layer_norm(out + x, gamma, beta)
        return out

    def _gn(v, G=32, eps=1e-05):
        B_, C_, H_, W_ = v.shape
        g = v.reshape(B_, G, C_ // G, H_, W_)
        m = jnp.mean(g, axis=(2, 3, 4), keepdims=True)
        s = jnp.var(g, axis=(2, 3, 4), keepdims=True)
        return ((g - m) / jnp.sqrt(s + eps)).reshape(v.shape)

    def _ln_c(v, eps=1e-06):
        m = jnp.mean(v, axis=1, keepdims=True)
        s = jnp.var(v, axis=1, keepdims=True)
        return (v - m) / jnp.sqrt(s + eps)

    def _ln_t(v, eps=1e-05):
        m = jnp.mean(v, axis=-1, keepdims=True)
        s = jnp.var(v, axis=-1, keepdims=True)
        return (v - m) / jnp.sqrt(s + eps)

    def _to_tokens(v):
        B_, C_, H_, W_ = v.shape
        return v.reshape(B_, C_, H_ * W_).transpose(0, 2, 1)

    def _from_tokens(t, like):
        B_, C_, H_, W_ = like.shape
        return t.transpose(0, 2, 1).reshape(B_, C_, H_, W_)
    x = x + _L0_conv_ref(_gn(x), L0_conv_wq, L0_conv_bq, L0_conv_wk, L0_conv_bk, L0_conv_wv, L0_conv_bv, L0_conv_gamma, L0_conv_beta)
    t = _to_tokens(x)
    t = t + _L1_attn_ref(_ln_t(t), L1_attn_Wqkv, L1_attn_bqkv, L1_attn_W0, L1_attn_b0)
    t = t + _L1_ffn_ref(_ln_t(t), L1_ffn_Wr, L1_ffn_br, L1_ffn_W1, L1_ffn_b1, L1_ffn_W2, L1_ffn_b2, L1_ffn_gamma, L1_ffn_beta)
    x = _from_tokens(t, x)
    return x

_drawn_inputs = setup_inputs


def setup_inputs(seed=0):
    import zlib

    import numpy as np

    out = dict(_drawn_inputs(seed))
    spreads = {'L0_conv_gamma': (1.0, 0.2),
     'L0_conv_beta': (0.0, 0.1),
     'L1_attn_bqkv': (0.0, 2.0),
     'L1_attn_b0': (0.0, 0.269),
     'L1_ffn_br': (0.0, 0.8),
     'L1_ffn_b1': (0.0, 0.397),
     'L1_ffn_b2': (0.0, 0.27),
     'L1_ffn_gamma': (1.0, 0.2),
     'L1_ffn_beta': (0.0, 0.447)}
    factors = {'L0_conv_bq': 3.374,
     'L0_conv_bk': 200.0,
     'L0_conv_bv': 200.0,
     'L1_attn_Wqkv': 64.0,
     'L1_attn_W0': 64.0}
    for name, (base, spread) in spreads.items():
        noise = np.random.default_rng([zlib.crc32(name.encode()), seed]).standard_normal(out[name].shape)
        drawn = base * np.exp(spread * noise) if base else spread * noise
        out[name] = jnp.asarray(drawn.astype(out[name].dtype))
    for name, factor in factors.items():
        out[name] = (out[name] * factor).astype(out[name].dtype)
    return out
```

```python
from contextlib import ExitStack

import concourse.bass as bass
from concourse import mybir

F32 = mybir.dt.float32
BF16 = mybir.dt.bfloat16
U32 = mybir.dt.uint32
ALU = mybir.AluOpType
ACT = mybir.ActivationFunctionType
AX_X = mybir.AxisListType.X

P = 128
NEG = -1.0e30
BIG = 3.0e38


def build(nc, t):
    x_in, out = t["x"], t["out"]
    B, C, H, W = x_in.shape
    HW = H * W
    N = B * HW
    assert C == P and W == 32 and B == 2

    GN_SIZE = C // 32
    UNROLL = 4
    CONV_ITERS = N // P // UNROLL
    CHUNKS = HW // P

    D = C
    HEADS = t["L1_attn_Wqkv"].shape[1] // (3 * D)
    GROUP_AT = [0]
    for r in range(3):
        GROUP_AT.append(GROUP_AT[-1] + (HW - r + 2) // 3)
    SCORE_SCALE = float(D) ** -0.5
    TILES = HW // P

    E = t["L1_ffn_Wr"].shape[1]
    FF = t["L1_ffn_W1"].shape[2]
    FC = FF // P
    TOPK = 2
    CAPACITY = float(-(-N * 1.25 // E))

    def segments(section, image):
        first_row = (2 * section + image) * HW
        pieces = []
        for r in range(3):
            lo, hi = GROUP_AT[r], GROUP_AT[r + 1]
            cuts = [lo] + [c for c in (512,) if lo < c < hi] + [hi]
            for a, b in zip(cuts, cuts[1:]):
                pieces.append((a, b - a, (first_row + r) % 3, (first_row + r) // 3 + a - lo))
        return pieces

    def groups(section, image):
        first_row = (2 * section + image) * HW
        return [(GROUP_AT[r], GROUP_AT[r + 1], (first_row + r) % 3, (first_row + r) // 3) for r in range(3)]

    ctx = ExitStack()
    with ctx:
        def sb(name, shape, dt=F32):
            return ctx.enter_context(nc.sbuf_tensor(name, shape, dt))

        def sem(name):
            return ctx.enter_context(nc.semaphore(name))

        ps = ctx.enter_context(nc.psum_tensor("ps", [P, 8 * 512], F32))

        def bank(n, lo=0, hi=512, rows=P):
            return ps[0:rows, n * 512 + lo:n * 512 + hi]

        def slot(n, lo=0, hi=1024):
            return ps[:, n * 1024 + lo:n * 1024 + hi]

        ident = sb("ident", [P, P])
        ident_b = sb("ident_b", [P, P], BF16)
        ones = sb("ones", [P, P])
        mean_w = sb("mean_w", [P, P])
        group_w = sb("group_w", [P, P])
        head_sel = sb("head_sel", [3 * HEADS, HEADS, P], BF16)

        x = sb("x", [P, N])
        conv_w = sb("conv_w", [P, 3, C])
        conv_wT = sb("conv_wT", [P, 3, C])
        NVEC = 8
        NROWS = NVEC + E * FC + E
        rows = sb("rows", [NROWS, P])
        cols = sb("cols", [P, NROWS])
        VEC = {n: cols[:, i:i + 1] for i, n in enumerate(
            ["L0_conv_bq", "L0_conv_bk", "L0_conv_bv", "L0_conv_gamma", "L0_conv_beta",
             "L1_attn_b0", "L1_ffn_gamma", "L1_ffn_beta"])}
        b1_all = cols[:, NVEC:NVEC + E * FC].rearrange("p (e f) -> p e f", f=FC)
        b2_all = cols[:, NVEC + E * FC:NROWS]
        wqkv = sb("wqkv", [P, 3, D, HEADS])
        bqkv = sb("bqkv", [P, 3, HEADS])
        bqkv_q = sb("bqkv_q", [P, 3, HEADS])
        w0 = sb("w0", [P, HEADS, D])
        w1 = sb("w1", [P, E, FF])
        w2 = sb("w2", [P, E, FC, D])
        wr = sb("wr", [P, E])
        br = sb("br", [1, E])

        xg = sb("xg", [P, N])
        keys = sb("keys", [P, N])
        centred, squares = xg, keys
        vtok = sb("vtok", [P, 2, CHUNKS, C])
        conv_o = sb("conv_o", [P, N])
        x1 = sb("x1", [P, N])
        xn = sb("xn", [P, N])
        diagonals = sb("diagonals", [P, N])
        sd = sb("sd", [P, N // P])
        st = sb("st", [P, 64])
        bn6 = sb("bn6", [P, 4, 6])

        conv_q = sb("conv_q", [P, UNROLL, P])
        scratch = sb("scratch", [P, 2, UNROLL * HW])
        probs, probsT = (scratch[:, i, :].rearrange("p (u k) -> p u k", u=UNROLL) for i in range(2))
        late = scratch[:, :, :].rearrange("p a k -> p (a k)")
        negmax = sb("negmax", [P, UNROLL])
        maxima = sb("maxima", [P, UNROLL])
        psums = sb("psums", [P, UNROLL])
        precip = sb("precip", [P, UNROLL])
        otok = sb("otok", [P, UNROLL, C])

        w_head = sb("w_head", [P, 3, D])
        w_headT = sb("w_headT", [P, 3, D])
        fold = sb("fold", [P, HEADS, 3, D])
        kq = sb("kq", [P, 2, 2, HW])
        kT, qT = kq[:, 0, :, :], kq[:, 1, :, :]
        neighbours = kq[:, :, :, :].rearrange("p a b n -> p (a b n)").bitcast(BF16)\
            .rearrange("p (i k) -> p i k", k=HW)
        exps = sb("exps", [P, 2, HW], BF16)
        diag_junk = sb("diag_junk", [P, P])
        diag8 = sb("diag8", [P, 2, TILES])
        diag_all = sb("diag_all", [P, HEADS * 2 * TILES])
        nmax_all = sb("nmax_all", [P, HEADS * 2 * TILES])
        sum_all = sb("sum_all", [P, HEADS * 2 * TILES])
        a_all = sb("a_all", [P, HEADS * 2 * TILES])
        a_rest = sb("a_rest", [P, HEADS * 2 * TILES])
        a3 = sb("a3", [P, 2 * TILES, 3, HEADS], BF16)
        aT = sb("aT", [3 * HEADS, 2, HW], BF16)
        vb = sb("vb", [P, 3, HEADS])
        vb_rest = sb("vb_rest", [P, 3, HEADS])
        vb3 = sb("vb3", [P, 3, 3, 3, HEADS], BF16)
        vbT = sb("vbT", [3 * HEADS, 3, 3, P], BF16)
        xv = sb("xv", [P, 2, HW])
        xs = late[:, 3 * N:4 * N].rearrange("p (b n) -> p b n", b=2)
        fold_h = sb("fold_h", [P, 2, 3, D])
        sel_h = sb("sel_h", [3 * HEADS, 2, P], BF16)
        xs_flat = xs[:, :, :].rearrange("p b n -> p (b n)")
        t1 = late[:, 0:N]

        mb = sb("mb", [P, 2])
        mbb = sb("mbb", [P, 2, P])
        rt = sb("rt", [P, 12, 2, E])
        rs_ = sb("rs_", [P, 16, 2])
        top_i = sb("top_i", [P, 2, E], U32)
        w1s = late[:, N:N + 2 * TOPK * FF].rearrange("p (b k f) -> p b k f", b=2, k=TOPK)
        w2s = late[:, N + 2 * TOPK * FF:2 * N].rearrange("p (b k f c) -> p b k f c", b=2, k=TOPK, f=FC)
        b1s = sb("b1s", [P, 2, TOPK, FC])
        b2s = sb("b2s", [P, 2, TOPK])
        hid = late[:, 2 * N:3 * N].rearrange("p (n f c) -> p n f c", n=2, f=FC)

        x_in_sem = [sem(f"x_landed{b}") for b in range(2)]
        mask_in = sem("mask_landed")
        conv_w_in, rows_in, wqkv_in, w0_in, ffn_in = (sem(n) for n in (
            "conv_w_landed", "rows_landed", "wqkv_landed", "w0_landed", "ffn_landed"))
        out_sem = sem("out_stored")
        consts, ident_made = sem("consts"), sem("ident_made")
        pool_step, dve_step, act_step = sem("pool_step"), sem("dve_step"), sem("act_step")
        gn_stats, gn_mean, gn_q, gn_var, gn_aff = (sem(n) for n in (
            "gn_stats", "gn_mean", "gn_q", "gn_var", "gn_aff"))
        xg_ready = [sem(f"xg_ready{b}") for b in range(2)]
        wT_ps, wT_sb, cols_ps, cols_sb = (sem(n) for n in ("wT_ps", "wT_sb", "cols_ps", "cols_sb"))
        k_ps, k_sb, v_ps, v_sb = (sem(n) for n in ("k_ps", "k_sb", "v_ps", "v_sb"))

        def per_tile(name):
            return [sem(f"{name}{u}") for u in range(UNROLL)]

        cq_ps, cq_sb, cs_ps, cg_sb, cm_sb, ce_sb, ct_ps, ct_sb, co_ps, co_sb, cx_ps, cr_sb = (
            sem(n) for n in ("cq_ps", "cq_sb", "cs_ps", "cg_sb", "cm_sb", "ce_sb",
                             "ct_ps", "ct_sb", "co_ps", "co_sb", "cx_ps", "cr_sb"))
        cx_sb = per_tile("cx_sb")
        cmax_sb = sem("cmax_sb")
        gn_eps, gn_root, bn_eps, bn_root = (sem(n) for n in ("gn_eps", "gn_root", "bn_eps", "bn_root"))
        bn_aff, bn_relu, x1_ready = sem("bn_aff"), sem("bn_relu"), sem("x1_ready")
        f_stage, f_T_ps, f_T_sb, f_m_ps, f_m_sb = (sem(n) for n in (
            "fold_staged", "fold_T_ps", "fold_T_sb", "fold_m_ps", "fold_m_sb"))
        vb_ps, vb_sb, vbT_ps, vbT_sb = (sem(n) for n in ("vb_ps", "vb_sb", "vbT_ps", "vbT_sb"))

        def ln_sems(k):
            return {n: sem(f"ln{k}_{n}") for n in (
                "mean", "centred", "square", "var", "eps", "sqrt", "diag", "spread", "out")}

        LN = [ln_sems(k) for k in range(3)]
        staged, job_ps, job_done, tile_maxed, diag_full, diag_saved = (sem(n) for n in (
            "w_head_staged", "job_ps", "job_done", "tile_maxed", "diag_full", "diag_saved"))
        bq_ready = sem("bq_ready")
        a_exp, a_sum, a3_ready, aT_ps, aT_sb = (sem(n) for n in ("a_exp", "a_sum", "a3_ready", "aT_ps", "aT_sb"))
        xv_ready = sem("xv_ready")
        v_staged = [sem(f"v_staged{p}") for p in range(2)]
        v_used = [sem(f"v_used{p}") for p in range(2)]
        ab_ps = [sem(f"ab_ps{b}") for b in range(2)]
        xs_sb = [sem(f"xs_sb{b}") for b in range(2)]
        xs_used = [sem(f"xs_used{b}") for b in range(2)]
        t1_ready, t1_beta = sem("t1_ready"), sem("t1_beta")
        mb_ready, lg_ps, r_in, r_exp = (sem(n) for n in ("mb_ready", "logits_ps", "r_in", "r_exp"))
        idx_ready, w1_ready, w2_ready = sem("idx_ready"), sem("w1_ready"), sem("w2_ready")
        h_ps, h_sb, y_ps, u_ready = (sem(n) for n in ("h_ps", "h_sb", "y_ps", "u_ready"))
        out_ready = sem("out_ready")

        def head_jobs(last):
            jobs = [("score", 0, n) for n in range(TILES)]
            jobs[3:3] = [("keys", 1, 0), ("queries", 1, 0)]
            second = [("score", 1, n) for n in range(TILES)]
            if not last:
                second[3:3] = [("next keys", 0, 0), ("next queries", 0, 0)]
            return jobs + second

        PRE = 2
        PER_HEAD = 2 * TILES + 4
        SLOTS = 4

        block = ctx.enter_context(nc.Block())

        @block.sync
        def _(sp):
            xf = x_in.rearrange("b c h w -> c b (h w)")
            for b in range(2):
                sp.dma_start(x[:, b * HW:(b + 1) * HW], xf[:, b, :]).then_inc(x_in_sem[b], 16)
            sp.dma_start(neighbours, t["neighbours"].rearrange("(i p) k -> p i k", p=P)).then_inc(mask_in, 16)
            sp.dma_start(wqkv[:, :, :, :],
                         t["L1_attn_Wqkv"].rearrange("c (j d h) -> c j d h", j=3, h=HEADS)).then_inc(wqkv_in, 16)
            sp.dma_start(bqkv[:, :, :],
                         t["L1_attn_bqkv"].rearrange("(j d h) -> d j h", j=3, h=HEADS)).then_inc(wqkv_in, 16)
            sp.dma_start(w1[:, :, :], t["L1_ffn_W1"].rearrange("e c f -> c e f")).then_inc(ffn_in, 16)
            sp.dma_start(w2[:, :, :, :],
                         t["L1_ffn_W2"].rearrange("e (g f) c -> f e g c", f=P)).then_inc(ffn_in, 16)
            sp.dma_start(wr[:, :], t["L1_ffn_Wr"]).then_inc(ffn_in, 16)
            sp.dma_start(br[:, :], t["L1_ffn_br"].rearrange("(a e) -> a e", a=1)).then_inc(ffn_in, 16)
            of = out.rearrange("b c h w -> c b (h w)")
            for n in range(4):
                sp.wait_ge(out_ready, n + 1)
                b, half = n // 2, n % 2
                sp.dma_start(of[:, b, half * 512:(half + 1) * 512],
                             conv_o[:, n * 512:(n + 1) * 512]).then_inc(out_sem, 16)
            sp.wait_ge(out_sem, 64)

        @block.gpsimd
        def _(pool):
            g = nc.gpsimd
            count = [0]

            def step(inst):
                inst.then_inc(pool_step, 1)
                count[0] += 1
                pool.wait_ge(pool_step, count[0])

            step(g.memset(ident[:, :], 0.0))
            g.affine_select(out=ident[:, :], in_=ident[:, :], compare_op=ALU.not_equal, fill=1.0, base=0,
                            pattern=[[-1, P]], channel_multiplier=1).then_inc(ident_made, 1)
            pool.wait_ge(ident_made, 1)
            g.tensor_copy(ident_b[:, :], ident[:, :]).then_inc(consts, 1)
            g.memset(ones[:, :], 1.0).then_inc(consts, 1)
            g.memset(mean_w[:, :], 1.0 / C).then_inc(consts, 1)
            gv = group_w[:, :].rearrange("p (g k) -> p g k", k=GN_SIZE)
            step(g.memset(group_w[:, :], 1.0 / GN_SIZE))
            step(g.affine_select(out=gv, in_=gv, compare_op=ALU.is_ge, fill=0.0, base=0,
                                 pattern=[[-GN_SIZE, C // GN_SIZE], [0, GN_SIZE]], channel_multiplier=1))
            g.affine_select(out=gv, in_=gv, compare_op=ALU.is_ge, fill=0.0, base=GN_SIZE - 1,
                            pattern=[[GN_SIZE, C // GN_SIZE], [0, GN_SIZE]], channel_multiplier=-1)\
                .then_inc(consts, 1)
            step(g.memset(head_sel[:, :, :], 0.0))
            for part in range(3):
                inst = g.affine_select(out=head_sel[:, :, :], in_=head_sel[:, :, :], compare_op=ALU.not_equal,
                                       fill=1.0, base=-part * HEADS, pattern=[[-1, HEADS], [0, P]],
                                       channel_multiplier=1)
                if part < 2:
                    step(inst)
                else:
                    inst.then_inc(consts, 1)

            pool.wait_ge(wqkv_in, 32)
            with pool.Fori(0, HEADS) as h:
                pool.wait_ge(f_T_ps, h)
                g.tensor_copy(w_head[:, :, :], wqkv[:, :, :, bass.ds(h, 1)].rearrange("p j d o -> p j (d o)"))\
                    .then_inc(f_stage, 1)

            g.tensor_scalar(bqkv_q[:, :, :], bqkv[:, :, :], SCORE_SCALE, None, ALU.mult).then_inc(bq_ready, 1)
            pool.wait_ge(f_T_ps, HEADS)
            g.tensor_copy(w_head[:, :, :], wqkv[:, :, :, 0]).then_inc(staged, 1)

            pool.wait_ge(LN[0]["out"], 4)
            for b in range(2):
                for lo, hi, _, tok in groups(2, b):
                    g.tensor_copy(xv[:, b, lo:hi], xn[:, tok:tok + hi - lo]).then_inc(xv_ready, 1)

            def head(h, last):
                for b in range(2):
                    if b == 0 and not last:
                        pool.wait_ge(job_ps, PRE + h * PER_HEAD + 5)
                        g.tensor_copy(w_head[:, :, :], wqkv[:, :, :, bass.ds(h + 1, 1)]
                                      .rearrange("p j d o -> p j (d o)")).then_inc(staged, 1)
                    pool.wait_ge(diag_full, h * 2 + b + 1)
                    if last:
                        dst = diag_all[:, (2 * h + b) * TILES:(2 * h + b + 1) * TILES]
                    else:
                        dst = diag_all[:, bass.ds(h * (2 * TILES) + b * TILES, TILES)]
                    g.tensor_copy(dst, diag8[:, b, :]).then_inc(diag_saved, 1)

            with pool.Fori(0, HEADS - 1) as h:
                head(h, False)
            head(HEADS - 1, True)

            with pool.Fori(0, HEADS // 2) as h2:
                for p in range(2):
                    pool.wait_ge(v_used[p], h2)
                    g.tensor_copy(fold_h[:, p, :, :], fold[:, bass.ds(h2 * 2 + p, 1), :, :]
                                  .rearrange("p o j d -> p (o j) d")).then_inc(v_staged[p], 1)
                    g.tensor_copy(sel_h[:, p, :], head_sel[:, bass.ds(h2 * 2 + p, 1), :]
                                  .rearrange("p o m -> p (o m)")).then_inc(v_staged[p], 1)

            pool.wait_ge(idx_ready, 2)
            for b in range(2):
                for k in range(TOPK):
                    e = pool.value_load(top_i[0:1, b, k:k + 1], min_val=0, max_val=E - 1)
                    g.tensor_copy(w1s[:, b, k, :], w1[:, bass.ds(e, 1), :].rearrange("p o f -> p (o f)"))\
                        .then_inc(w1_ready, 1)

        @block.scalar
        def _(act):
            a = nc.scalar
            for j, n in enumerate(["wq", "wk", "wv"]):
                act.dma_start(conv_w[:, j, :], t[f"L0_conv_{n}"]).then_inc(conv_w_in, 16)
            for i, n in enumerate(VEC):
                act.dma_start(rows[i:i + 1, :], t[n].rearrange("(a c) -> a c", a=1)).then_inc(rows_in, 16)
            act.dma_start(rows[NVEC:NVEC + E * FC, :],
                          t["L1_ffn_b1"].rearrange("e (g f) -> (e g) f", f=P)).then_inc(rows_in, 16)
            act.dma_start(rows[NVEC + E * FC:NROWS, :], t["L1_ffn_b2"]).then_inc(rows_in, 16)
            act.dma_start(w0[:, :, :], t["L1_attn_W0"].rearrange("(d h) c -> d h c", h=HEADS)).then_inc(w0_in, 16)

            act.wait_ge(wT_ps, 1)
            a.copy(conv_wT[:, :, :], bank(0, 0, 3 * C).rearrange("p (j c) -> p j c", j=3)).then_inc(wT_sb, 1)
            act.wait_ge(cols_ps, 1)
            a.copy(cols[:, :], bank(1, 0, NROWS)).then_inc(cols_sb, 1)
            act.wait_ge(gn_eps, 1)
            a.activation(st[:, 22:24], st[:, 22:24], ACT.Sqrt).then_inc(gn_root, 1)
            act.wait_ge(gn_aff, 1)
            a.activation(xg[:, HW:N], x[:, HW:N], ACT.Identity,
                         scale=st[:, 18:19], bias=st[:, 20:21]).then_inc(xg_ready[1], 1)
            act.wait_ge(cols_sb, 1)
            for n in range(4):
                act.wait_ge(k_ps, n + 1)
                a.activation(keys[:, n * 512:(n + 1) * 512], bank(4 + n), ACT.Identity,
                             bias=VEC["L0_conv_bk"]).then_inc(k_sb, 1)

            with act.Fori(0, CONV_ITERS) as it:
                for u in range(UNROLL):
                    act.wait_ge(cq_ps, it * UNROLL + (u + 1))
                    a.activation(conv_q[:, u, :], slot(u, 0, P), ACT.Identity,
                                 bias=VEC["L0_conv_bq"]).then_inc(cq_sb, 1)
                for u in range(UNROLL):
                    act.wait_ge(cm_sb, it * UNROLL + (u + 1))
                    act.wait_ge(cr_sb, it * UNROLL)
                    a.activation(probs[:, u, :], probs[:, u, :], ACT.Exp, bias=negmax[:, u:u + 1],
                                 accum_out=psums[:, u:u + 1]).then_inc(ce_sb, 1)
                for u in range(UNROLL):
                    act.wait_ge(ct_ps, it * UNROLL + (u + 1))
                    act.wait_ge(co_ps, it * UNROLL)
                    a.copy(probsT[:, u, :], slot(u)).then_inc(ct_sb, 1)
                for u in range(UNROLL):
                    act.wait_ge(cx_ps, it * UNROLL + (u + 1))
                    at = (u // 2) * HW + (u % 2) * P
                    a.activation(conv_o[:, bass.ds(it * (2 * P) + at, P)], slot(u, 0, P), ACT.Identity,
                                 bias=VEC["L0_conv_bv"]).then_inc(cx_sb[u], 1)

            with act.Fori(0, HEADS) as h:
                act.wait_ge(f_T_ps, h + 1)
                act.wait_ge(f_m_ps, h)
                a.copy(w_headT[:, :, :], bank(4, 0, 3 * D).rearrange("p (j d) -> p j d", j=3)).then_inc(f_T_sb, 1)
                act.wait_ge(f_m_ps, h + 1)
                a.copy(fold[:, bass.ds(h, 1), :, :].rearrange("p o j d -> p (o j) d"),
                       bank(5, 0, 3 * D).rearrange("p (j d) -> p j d", j=3)).then_inc(f_m_sb, 1)

            act.wait_ge(bn_eps, 1)
            a.activation(st[:, 26:27], st[:, 26:27], ACT.Sqrt).then_inc(bn_root, 1)
            act.wait_ge(bn_aff, 1)
            for n in range(4):
                a.activation(conv_o[:, n * 512:(n + 1) * 512], conv_o[:, n * 512:(n + 1) * 512], ACT.Relu,
                             scale=st[:, 30:31], bias=st[:, 31:32]).then_inc(bn_relu, 1)

            def squares_of(k):
                for c in range(4):
                    act.wait_ge(LN[k]["centred"], c + 1)
                    a.activation(squares[:, c * 512:(c + 1) * 512], centred[:, c * 512:(c + 1) * 512],
                                 ACT.Square).then_inc(LN[k]["square"], 1)

            def root(k):
                act.wait_ge(LN[k]["eps"], 1)
                a.activation(sd[:, :], sd[:, :], ACT.Sqrt).then_inc(LN[k]["sqrt"], 1)

            squares_of(0)
            root(0)

            act.wait_ge(bq_ready, 1)

            def project(kind, b, h, static):
                section = 1 if "keys" in kind else 0
                dst, bias, scale = (kT, bqkv, 1.0) if section else (qT, bqkv_q, SCORE_SCALE)
                return section, dst, bias, scale

            def evacuate(kind, b, h, s):
                section, dst, bias, scale = project(kind, b, h, isinstance(h, int))
                for i, (lo, hi, j, _) in enumerate(groups(section, b)):
                    bb = bias[:, j, h:h + 1] if isinstance(h, int) else bias[:, j, bass.ds(h, 1)]
                    inst = a.activation(dst[:, b, lo:hi], slot(s, lo, hi), ACT.Identity, scale=scale, bias=bb)
                inst.then_inc(job_done, 1)

            for g, kind in enumerate(("keys", "queries")):
                act.wait_ge(job_ps, g + 1)
                evacuate(kind, 0, 0, g)

            def head(h, last):
                scores = 0
                for n, (kind, b, tile) in enumerate(head_jobs(last)):
                    s = (PRE + n) % SLOTS
                    if kind == "score":
                        col = h * (2 * TILES) + scores
                        at = slice(col, col + 1) if isinstance(h, int) else bass.ds(col, 1)
                        scores += 1
                        act.wait_ge(tile_maxed, h * (4 * TILES) + 2 * scores)
                        act.wait_ge(job_done, h * PER_HEAD + PRE + n - 1)
                        a.activation(exps[:, n % 2, :], slot(s), ACT.Exp, bias=nmax_all[:, at],
                                     accum_out=sum_all[:, at]).then_inc(job_done, 1)
                    else:
                        act.wait_ge(job_ps, PRE + h * PER_HEAD + n + 1)
                        evacuate(kind, b, h + 1 if "next" in kind else h, s)

            with act.Fori(0, HEADS - 1) as h:
                head(h, False)
            head(HEADS - 1, True)

            act.wait_ge(a_sum, 1)
            a.activation(a_all[:, :], a_rest[:, :], ACT.Exp).then_inc(a_exp, 1)
            for b in range(2):
                act.wait_ge(aT_ps, b + 1)
                a.copy(aT[:, b, :], bank(6 + b, rows=3 * HEADS).bitcast(BF16)[:, 0:HW]).then_inc(aT_sb, 1)

            squares_of(1)
            root(1)
            act.wait_ge(t1_ready, 6)
            a.activation(x1[:, :], t1[:, :], ACT.Identity, bias=VEC["L1_ffn_beta"]).then_inc(t1_beta, 1)
            act.wait_ge(r_in, 1)
            a.activation(rt[:, 2, :, :], rt[:, 1, :, :], ACT.Exp).then_inc(r_exp, 1)
            act.wait_ge(r_in, 2)
            a.activation(rt[:, 6, :, :], rt[:, 5, :, :], ACT.Exp).then_inc(r_exp, 1)
            act.wait_ge(r_in, 3)
            a.activation(rs_[:, 8, :], rs_[:, 7, :], ACT.Exp).then_inc(r_exp, 1)

            act.wait_ge(w2_ready, 12)
            for n in range(8):
                b, half, k = n // 4, n // 2 % 2, n % 2
                for f in range(FC):
                    act.wait_ge(h_ps, 2 * n + f + 1)
                    if n >= 2:
                        act.wait_ge(y_ps, n - 1)
                    a.activation(hid[:, n % 2, f, :], bank(2 * (n % 2) + f), ACT.Gelu,
                                 bias=b1s[:, b, k, f:f + 1]).then_inc(h_sb, 1)
                if k == 1:
                    c = n // 2
                    act.wait_ge(LN[2]["centred"], c + 1)
                    a.activation(squares[:, c * 512:(c + 1) * 512], centred[:, c * 512:(c + 1) * 512],
                                 ACT.Square).then_inc(LN[2]["square"], 1)
            root(2)

        @block.tensor
        def _(pe):
            mm = nc.tensor.matmul
            pe.wait_ge(ident_made, 1)
            pe.wait_ge(conv_w_in, 48)
            for j in range(3):
                last = nc.tensor.transpose(bank(0, j * C, (j + 1) * C), conv_w[:, j, :], ident[:, :])
            last.then_inc(wT_ps, 1)
            pe.wait_ge(rows_in, 16 * (NVEC + 2))
            nc.tensor.transpose(bank(1, 0, NROWS), rows[:, :], ident[0:NROWS, 0:NROWS]).then_inc(cols_ps, 1)
            pe.wait_ge(consts, 4)
            pe.wait_ge(gn_stats, 1)
            mm(bank(2, 0, 2), group_w[:, :], st[:, 0:2], start=True, stop=True).then_inc(gn_mean, 1)
            pe.wait_ge(gn_q, 1)
            mm(bank(3, 0, 2), group_w[:, :], st[:, 8:10], start=True, stop=True).then_inc(gn_var, 1)
            pe.wait_ge(wT_sb, 1)
            for n in range(4):
                if n % 2 == 0:
                    pe.wait_ge(xg_ready[n // 2], 1)
                mm(bank(4 + n), conv_wT[:, 1, :], xg[:, n * 512:(n + 1) * 512], start=True, stop=True)\
                    .then_inc(k_ps, 1)
            pe.wait_ge(cols_sb, 1)
            for n in range(2 * CHUNKS):
                last = mm(bank(n // 4, (n % 4) * P, (n % 4 + 1) * P), xg[:, n * P:(n + 1) * P],
                          conv_wT[:, 2, :], start=True, stop=True)
                if n % 4 == 3:
                    last.then_inc(v_ps, 1)

            pe.wait_ge(k_sb, 4)
            pe.wait_ge(v_sb, 4)
            pe.wait_ge(mask_in, 16)
            with pe.Fori(0, CONV_ITERS) as it:
                for u in range(UNROLL):
                    pe.wait_ge(cx_sb[u], it)
                    at = (u // 2) * HW + (u % 2) * P
                    mm(slot(u, 0, P), conv_wT[:, 0, :], xg[:, bass.ds(it * (2 * P) + at, P)],
                       start=True, stop=True).then_inc(cq_ps, 1)
                for u in range(UNROLL):
                    pe.wait_ge(cq_sb, it * UNROLL + (u + 1))
                    for half in range(2):
                        lo, hi = half * 512, (half + 1) * 512
                        mm(slot(u, lo, hi), conv_q[:, u, :], keys[:, (u // 2) * HW + lo:(u // 2) * HW + hi],
                           start=True, stop=False)
                        last = mm(slot(u, lo, hi), ident_b[:, :],
                                  neighbours[:, bass.ds(it * 2 + u % 2, 1), lo:hi].rearrange("p o k -> p (o k)"),
                                  start=False, stop=True)
                    last.then_inc(cs_ps, 1)
                for u in range(UNROLL):
                    pe.wait_ge(ce_sb, it * UNROLL + (u + 1))
                    for k in range(CHUNKS):
                        last = nc.tensor.transpose(slot(u, k * P, (k + 1) * P), probs[:, u, k * P:(k + 1) * P],
                                                   ident[:, :])
                    last.then_inc(ct_ps, 1)
                for u in range(UNROLL):
                    pe.wait_ge(ct_sb, it * UNROLL + (u + 1))
                    for k in range(CHUNKS):
                        last = mm(slot(u, 0, P), probsT[:, u, k * P:(k + 1) * P], vtok[:, u // 2, k, :],
                                  start=(k == 0), stop=(k == CHUNKS - 1))
                    last.then_inc(co_ps, 1)
                for u in range(UNROLL):
                    pe.wait_ge(co_sb, it * UNROLL + (u + 1))
                    nc.tensor.transpose(slot(u, 0, P), otok[:, u, :], ident[:, :]).then_inc(cx_ps, 1)

            for u in range(UNROLL):
                pe.wait_ge(cx_sb[u], CONV_ITERS)
            pe.wait_ge(w0_in, 16)
            with pe.Fori(0, HEADS) as h:
                pe.wait_ge(f_stage, h + 1)
                pe.wait_ge(f_T_sb, h)
                for j in range(3):
                    last = nc.tensor.transpose(bank(4, j * D, (j + 1) * D), w_head[:, j, :], ident[:, :])
                last.then_inc(f_T_ps, 1)
                pe.wait_ge(f_T_sb, h + 1)
                pe.wait_ge(f_m_sb, h)
                for j in range(3):
                    last = mm(bank(5, j * D, (j + 1) * D), w_headT[:, j, :],
                              w0[:, bass.ds(h, 1), :].rearrange("p o c -> p (o c)"), start=True, stop=True)
                last.then_inc(f_m_ps, 1)
            for h in range(HEADS):
                last = mm(bank(6, 3 * h, 3 * h + 3), w0[:, h, :], bqkv[:, :, h], start=True, stop=True)
            last.then_inc(vb_ps, 1)
            pe.wait_ge(vb_sb, 1)
            vbank = bank(7, rows=3 * HEADS).bitcast(BF16)
            for q in range(3):
                for half, js in ((0, (0, 1, 2)),):
                    for j in js:
                        n = 3 * q + j
                        tgt = (vbank if n < 8 else bank(6, rows=3 * HEADS).bitcast(BF16))
                        last = nc.tensor.transpose(tgt[:, (n % 8) * P:(n % 8 + 1) * P],
                                                   vb3[:, j, q, :, :].rearrange("p a h -> p (a h)"), ident_b[:, :])
            last.then_inc(vbT_ps, 1)

            def channel_means(k, c, source, name, n):
                mm(bank(n), mean_w[:, :], source[:, c * 512:(c + 1) * 512], start=True, stop=True)\
                    .then_inc(LN[k][name], 1)

            def variances(k, n):
                for i in range(N // P):
                    if i % 4 == 0:
                        pe.wait_ge(LN[k]["square"], i // 4 + 1)
                    last = mm(bank(n, i, i + 1), squares[:, i * P:(i + 1) * P], mean_w[:, 0:1], start=True, stop=True)
                last.then_inc(LN[k]["var"], 1)

            def spread(k, n):
                for c in range(4):
                    pe.wait_ge(LN[k]["diag"], c + 1)
                    mm(bank(n + c), ones[:, :], diagonals[:, c * 512:(c + 1) * 512], start=True, stop=True)\
                        .then_inc(LN[k]["spread"], 1)

            for c in range(4):
                pe.wait_ge(x1_ready, c + 1)
                channel_means(0, c, x1, "mean", c)
            variances(0, 4)
            spread(0, 0)
            pe.wait_ge(vbT_sb, 2)

            pe.wait_ge(LN[0]["out"], 4)
            pe.wait_ge(staged, 1)

            def project(kind, b, s):
                section = 1 if "keys" in kind else 0
                for at, n, j, tok in segments(section, b):
                    last = mm(slot(s, at, at + n), w_head[:, j, :], xn[:, tok:tok + n], start=True, stop=True)
                last.then_inc(job_ps, 1)

            project("keys", 0, 0)
            project("queries", 0, 1)

            def head(h, last_head):
                for n, (kind, b, tile) in enumerate(head_jobs(last_head)):
                    g = PRE + n
                    if isinstance(h, int) or g >= SLOTS:
                        pe.wait_ge(job_done, h * PER_HEAD + g - SLOTS + 1)
                    else:
                        pe.wait_ge(job_done, h * PER_HEAD)
                    if kind == "score":
                        if tile == 0:
                            pe.wait_ge(job_done, h * PER_HEAD + (PRE if b == 0 else PRE + 5))
                        for half in range(2):
                            last = mm(slot(g % SLOTS, half * 512, (half + 1) * 512),
                                      kT[:, b, tile * P:(tile + 1) * P], qT[:, b, half * 512:(half + 1) * 512],
                                      start=True, stop=True)
                        last.then_inc(job_ps, 1)
                    else:
                        if kind == "next keys":
                            pe.wait_ge(staged, h + 2)
                        project(kind, b, g % SLOTS)

            with pe.Fori(0, HEADS - 1) as h:
                head(h, False)
            head(HEADS - 1, True)

            pe.wait_ge(a3_ready, 3)
            pe.wait_ge(job_done, PRE + HEADS * PER_HEAD - 2)
            for b in range(2):
                tgt = bank(6 + b, rows=3 * HEADS).bitcast(BF16)
                for n in range(TILES):
                    last = nc.tensor.transpose(tgt[:, n * P:(n + 1) * P],
                                               a3[:, b * TILES + n, :, :].rearrange("p a h -> p (a h)"), ident_b[:, :])
                last.then_inc(aT_ps, 1)
            pe.wait_ge(aT_sb, 2)
            for b in range(2):
                opened = set()
                for at, n, j, _ in segments(2, b):
                    for q in range(3):
                        first = at // 512 not in opened
                        opened.add(at // 512)
                        mm(slot(b, at, at + n), vbT[:, j, q, :], aT[:, b, at:at + n], start=first, stop=False,
                           skip_group_check=True)
            pe.wait_ge(xv_ready, 6)
            with pe.Fori(0, HEADS // 2) as h2:
                for p in range(2):
                    pe.wait_ge(v_staged[p], 2 * h2 + 2)
                    for b in range(2):
                        pe.wait_ge(xs_sb[b], 2 * h2 + p)
                        for half in range(2):
                            last = mm(slot(2 + b, half * 512, (half + 1) * 512), sel_h[:, p, :],
                                      aT[:, b, half * 512:(half + 1) * 512], start=True, stop=True)
                        last.then_inc(ab_ps[b], 1)
                    for b in range(2):
                        pe.wait_ge(xs_sb[b], 2 * h2 + p + 1)
                        for at, n, j, _ in segments(2, b):
                            last = mm(slot(b, at, at + n), fold_h[:, p, j, :], xs[:, b, at:at + n],
                                      start=False, stop=False, skip_group_check=True)
                        last.then_inc(xs_used[b], 1)
                    last = mm(bank(4, 0, 2), ident[:, :], ident[:, 0:2], start=True, stop=True)
                    last.then_inc(v_used[p], 1)

            for c in range(4):
                pe.wait_ge(t1_ready, 3 if c < 2 else 6)
                channel_means(1, c, t1, "mean", 4 + c)
            variances(1, 0)
            spread(1, 4)

            pe.wait_ge(mb_ready, 2)
            pe.wait_ge(ffn_in, 64)
            for b in range(2):
                mm(bank(7, b * E, (b + 1) * E), mbb[:, b, :], wr[:, :], start=True, stop=False)
                last = mm(bank(7, b * E, (b + 1) * E), ones[0:1, :], br[:, :], start=False, stop=True)
            last.then_inc(lg_ps, 1)

            pe.wait_ge(w1_ready, 4)
            pe.wait_ge(w2_ready, 12)

            def hidden(n):
                b, half, k = n // 4, n // 2 % 2, n % 2
                if n >= 2:
                    pe.wait_ge(h_sb, 2 * n - 2)
                for f in range(FC):
                    mm(bank(2 * (n % 2) + f), w1s[:, b, k, f * P:(f + 1) * P],
                       xn[:, (n // 2) * 512:(n // 2 + 1) * 512], start=True, stop=True).then_inc(h_ps, 1)

            def outputs(n):
                b, half, k = n // 4, n // 2 % 2, n % 2
                c = n // 2
                pe.wait_ge(h_sb, 2 * n + 2)
                if k == 0 and c >= 2:
                    pe.wait_ge(u_ready, c - 1)
                for f in range(FC):
                    last = mm(bank(4 + c % 2), w2s[:, b, k, f, :], hid[:, n % 2, f, :],
                              start=(k == 0 and f == 0), stop=(k == 1 and f == FC - 1))
                last.then_inc(y_ps, 1)

            hidden(0)
            for n in range(8):
                if n + 1 < 8:
                    hidden(n + 1)
                outputs(n)
                if n % 2 == 1:
                    c = n // 2
                    pe.wait_ge(u_ready, c + 1)
                    if c >= 2:
                        pe.wait_ge(LN[2]["centred"], c - 1)
                    channel_means(2, c, xs_flat, "mean", 6 + c % 2)
            variances(2, 4)
            spread(2, 0)

        @block.vector
        def _(dve):
            v = nc.vector
            count = [0]

            def step(inst):
                inst.then_inc(dve_step, 1)
                count[0] += 1
                dve.wait_ge(dve_step, count[0])

            for b in range(2):
                dve.wait_ge(x_in_sem[b], 16)
                v.bn_stats(bn6[:, 2 * b, :], x[:, b * HW:b * HW + 512]).then_inc(dve_step, 1)
                v.bn_stats(bn6[:, 2 * b + 1, :], x[:, b * HW + 512:(b + 1) * HW]).then_inc(dve_step, 1)
                count[0] += 2
            dve.wait_ge(dve_step, count[0])
            mv = st[:, 4:8].rearrange("p (b k) -> p b k", k=2)
            for b in range(2):
                v.bn_aggr(mv[:, b, :], bn6[:, 2 * b:2 * b + 2, :]).then_inc(dve_step, 1)
            count[0] += 2
            dve.wait_ge(dve_step, count[0])
            v.tensor_copy(st[:, 0:2], mv[:, :, 0]).then_inc(gn_stats, 1)
            v.tensor_copy(st[:, 2:4], mv[:, :, 1]).then_inc(gn_stats, 1)
            dve.wait_ge(gn_mean, 1)
            dve.wait_ge(gn_stats, 2)
            step(v.tensor_copy(st[:, 16:18], bank(2, 0, 2)))
            step(v.tensor_tensor(st[:, 10:12], st[:, 0:2], st[:, 16:18], ALU.subtract))
            step(v.tensor_tensor(st[:, 12:14], st[:, 10:12], st[:, 10:12], ALU.mult))
            v.tensor_tensor(st[:, 8:10], st[:, 12:14], st[:, 2:4], ALU.add).then_inc(gn_q, 1)
            dve.wait_ge(gn_var, 1)
            v.tensor_scalar(st[:, 22:24], bank(3, 0, 2), 1e-5, None, ALU.add).then_inc(gn_eps, 1)
            dve.wait_ge(gn_root, 1)
            step(v.reciprocal(st[:, 22:24], st[:, 22:24]))
            step(v.scalar_tensor_tensor(st[:, 19:21], st[:, 16:18], -1.0, st[:, 22:24], ALU.mult, ALU.mult))
            v.tensor_copy(st[:, 17:19], st[:, 22:24]).then_inc(gn_aff, 1)
            dve.wait_ge(gn_aff, 1)
            v.tensor_scalar(xg[:, 0:HW], x[:, 0:HW], st[:, 17:18], st[:, 19:20],
                            ALU.mult, ALU.add).then_inc(xg_ready[0], 1)
            vflat = vtok[:, :, :, :].rearrange("p b n c -> p (b n c)")
            for n in range(4):
                dve.wait_ge(v_ps, n + 1)
                v.tensor_copy(vflat[:, n * 512:(n + 1) * 512], bank(n)).then_inc(v_sb, 1)

            with dve.Fori(0, CONV_ITERS) as it:
                for u in range(UNROLL):
                    dve.wait_ge(cs_ps, it * UNROLL + (u + 1))
                    dve.wait_ge(ct_ps, it * UNROLL)
                    v.tensor_scalar(probs[:, u, :], slot(u), 0.0, NEG, ALU.is_equal, ALU.mult)\
                        .then_inc(cg_sb, 1)
                    dve.wait_ge(v_sb, 4)
                    dve.wait_ge(ce_sb, it * UNROLL)
                    dve.wait_ge(cg_sb, it * UNROLL + (u + 1))
                    v.tensor_tensor_reduce(out=probs[:, u, :], in0=slot(u), in1=probs[:, u, :],
                                           scale=1.0, scalar=-BIG, op0=ALU.add, op1=ALU.max,
                                           accum_out=maxima[:, u:u + 1]).then_inc(cmax_sb, 1)
                    dve.wait_ge(cmax_sb, it * UNROLL + (u + 1))
                    v.tensor_scalar(negmax[:, u:u + 1], maxima[:, u:u + 1], -1.0, None, ALU.mult)\
                        .then_inc(cm_sb, 1)
                for u in range(UNROLL):
                    dve.wait_ge(ce_sb, it * UNROLL + (u + 1))
                    v.reciprocal(precip[:, u:u + 1], psums[:, u:u + 1]).then_inc(cr_sb, 1)
                for u in range(UNROLL):
                    dve.wait_ge(co_ps, it * UNROLL + (u + 1))
                    dve.wait_ge(cr_sb, it * UNROLL + (u + 1))
                    v.tensor_scalar(otok[:, u, :], slot(u, 0, P), precip[:, u:u + 1], None, ALU.mult)\
                        .then_inc(co_sb, 1)

            for u in range(UNROLL):
                dve.wait_ge(cx_sb[u], CONV_ITERS)
            for n in range(4):
                v.bn_stats(bn6[:, n, :], conv_o[:, n * 512:(n + 1) * 512]).then_inc(dve_step, 1)
            count[0] += 4
            dve.wait_ge(dve_step, count[0])
            step(v.bn_aggr(st[:, 24:26], bn6[:, :, :]))
            v.tensor_scalar(st[:, 26:27], st[:, 25:26], 1e-5, None, ALU.add).then_inc(bn_eps, 1)
            dve.wait_ge(bn_root, 1)
            step(v.reciprocal(st[:, 26:27], st[:, 26:27]))
            step(v.tensor_tensor(st[:, 30:31], st[:, 26:27], VEC["L0_conv_gamma"], ALU.mult))
            step(v.tensor_tensor(st[:, 27:28], st[:, 24:25], st[:, 30:31], ALU.mult))
            v.tensor_tensor(st[:, 31:32], VEC["L0_conv_beta"], st[:, 27:28], ALU.subtract).then_inc(bn_aff, 1)
            dve.wait_ge(vb_ps, 1)
            step(v.tensor_copy(vb[:, :, :], bank(6, 0, 3 * HEADS).rearrange("p (h j) -> p j h", j=3)))

            def repeated(part):
                return vb3[:, :, part, :, :]

            def once(tile):
                return tile[:, :, :]

            for part in range(3):
                src = vb if part != 1 else vb_rest
                if part == 2:
                    src = vb
                for a_ in range(3):
                    v.tensor_copy(vb3[:, :, part, a_, :], src[:, :, :]).then_inc(dve_step, 1)
                count[0] += 3
                dve.wait_ge(dve_step, count[0])
                if part < 2:
                    dst = vb_rest if part == 0 else vb
                    step(v.tensor_tensor(dst[:, :, :], src[:, :, :], vb3[:, :, part, 0, :], ALU.subtract))
            v.tensor_copy(st[:, 40:41], st[:, 30:31]).then_inc(vb_sb, 1)
            for n in range(4):
                dve.wait_ge(bn_relu, n + 1)
                v.tensor_tensor(x1[:, n * 512:(n + 1) * 512], x[:, n * 512:(n + 1) * 512],
                                conv_o[:, n * 512:(n + 1) * 512], ALU.add).then_inc(x1_ready, 1)
            dve.wait_ge(vbT_ps, 1)
            vT = vbT[:, :, :, :]
            vp = bank(7, rows=3 * HEADS).bitcast(BF16)
            for n in range(9):
                src = (vp if n < 8 else bank(6, rows=3 * HEADS).bitcast(BF16))[:, (n % 8) * P:(n % 8 + 1) * P]
                inst = v.tensor_copy(vT[:, n % 3, n // 3, :], src)
                if n >= 7:
                    inst.then_inc(vbT_sb, 1)

            def centre(k, c, source, n):
                dve.wait_ge(LN[k]["mean"], c + 1)
                v.tensor_tensor(centred[:, c * 512:(c + 1) * 512], source[:, c * 512:(c + 1) * 512], bank(n),
                                ALU.subtract).then_inc(LN[k]["centred"], 1)

            def scale(k, var_bank, spread_bank, out_to):
                dve.wait_ge(LN[k]["var"], 1)
                v.tensor_scalar(sd[:, :], bank(var_bank, 0, N // P), 1e-5, None, ALU.add).then_inc(LN[k]["eps"], 1)
                dve.wait_ge(LN[k]["sqrt"], 1)
                step(v.reciprocal(sd[:, :], sd[:, :]))
                for i in range(N // P):
                    inst = v.tensor_scalar(diagonals[:, i * P:(i + 1) * P], ident[:, :], sd[:, i:i + 1], None,
                                           ALU.mult)
                    if i % 4 == 3:
                        inst.then_inc(LN[k]["diag"], 1)
                for c in range(4):
                    dve.wait_ge(LN[k]["spread"], c + 1)
                    v.tensor_tensor(out_to[:, c * 512:(c + 1) * 512], centred[:, c * 512:(c + 1) * 512],
                                    bank(spread_bank + c), ALU.mult).then_inc(LN[k]["out"], 1)

            for c in range(4):
                centre(0, c, x1, c)
            scale(0, 4, 0, xn)

            def head(h, last):
                scores = 0
                for n, (kind, b, tile) in enumerate(head_jobs(last)):
                    if kind != "score":
                        continue
                    s = (PRE + n) % SLOTS
                    col = h * (2 * TILES) + scores
                    at = slice(col, col + 1) if isinstance(h, int) else bass.ds(col, 1)
                    scores += 1
                    dve.wait_ge(job_ps, PRE + h * PER_HEAD + n + 1)
                    v.tensor_reduce(nmax_all[:, at], slot(s), AX_X, ALU.max, negate=True).then_inc(tile_maxed, 1)
                    if tile == 0:
                        dve.wait_ge(diag_saved, h * 2)
                    dve.wait_ge(tile_maxed, h * (4 * TILES) + 2 * scores - 2)
                    v.tensor_tensor_reduce(out=diag_junk[:, :], in0=slot(s, tile * P, (tile + 1) * P),
                                           in1=ident[:, :], scale=1.0, scalar=0.0, op0=ALU.mult, op1=ALU.add,
                                           accum_out=diag8[:, b, tile:tile + 1]).then_inc(tile_maxed, 1)
                    if tile == TILES - 1:
                        dve.wait_ge(tile_maxed, h * (4 * TILES) + 2 * scores)
                        v.tensor_copy(st[:, 42:43], st[:, 30:31]).then_inc(diag_full, 1)

            with dve.Fori(0, HEADS - 1) as h:
                head(h, False)
            head(HEADS - 1, True)

            dve.wait_ge(diag_saved, 2 * HEADS)
            v.tensor_tensor(a_rest[:, :], diag_all[:, :], nmax_all[:, :], ALU.add).then_inc(a_sum, 1)
            dve.wait_ge(job_done, PRE + HEADS * PER_HEAD - 2)
            step(v.reciprocal(sum_all[:, :], sum_all[:, :]))
            dve.wait_ge(a_exp, 1)
            step(v.tensor_tensor(a_all[:, :], a_all[:, :], sum_all[:, :], ALU.mult))

            def by_tile(tile):
                return tile[:, :].rearrange("p (h n) -> p n h", h=HEADS)

            v.tensor_copy(a3[:, :, 0, :], by_tile(a_all)).then_inc(a3_ready, 1)
            dve.wait_ge(a3_ready, 1)
            step(v.tensor_tensor(by_tile(a_rest), by_tile(a_all), a3[:, :, 0, :], ALU.subtract))
            v.tensor_copy(a3[:, :, 1, :], by_tile(a_rest)).then_inc(a3_ready, 1)
            dve.wait_ge(a3_ready, 2)
            step(v.tensor_tensor(by_tile(a_all), by_tile(a_rest), a3[:, :, 1, :], ALU.subtract))
            v.tensor_copy(a3[:, :, 2, :], by_tile(a_all)).then_inc(a3_ready, 1)

            dve.wait_ge(xv_ready, 6)
            with dve.Fori(0, HEADS // 2) as h2:
                for p in range(2):
                    for b in range(2):
                        dve.wait_ge(ab_ps[b], 2 * h2 + p + 1)
                        dve.wait_ge(xs_used[b], 2 * h2 + p)
                        v.tensor_tensor(xs[:, b, :], xv[:, b, :], slot(2 + b), ALU.mult).then_inc(xs_sb[b], 1)

            for b in range(2):
                dve.wait_ge(xs_used[b], HEADS)
                for r in range(3):
                    lo, hi = GROUP_AT[r], GROUP_AT[r + 1]
                    v.scalar_tensor_tensor(t1[:, b * HW + r:(b + 1) * HW:3], slot(b, lo, hi), VEC["L1_attn_b0"],
                                           x1[:, b * HW + r:(b + 1) * HW:3], ALU.add, ALU.add)\
                        .then_inc(t1_ready, 1)
            dve.wait_ge(t1_ready, 6)
            for c in range(4):
                centre(1, c, t1, 4 + c)
            scale(1, 0, 4, xn)
            for b in range(2):
                dve.wait_ge(LN[1]["out"], 2 * b + 2)
                step(v.reduce_sum(mb[:, b:b + 1], xn[:, b * HW:(b + 1) * HW], AX_X))
                v.tensor_scalar(mbb[:, b, :], ones[:, :], mb[:, b:b + 1], 1.0 / HW, ALU.mult, ALU.mult)\
                    .then_inc(mb_ready, 1)

            def spread(col):
                return col.rearrange("p (b o) -> p b o", o=1).broadcast_to([P, 2, E])

            def softmax_head(src, centred_at, col):
                step(v.tensor_reduce(rs_[:, col, :], src, AX_X, ALU.max))
                for b in range(2):
                    inst = v.tensor_scalar(rt[:, centred_at, b, :], src[:, b, :], rs_[:, col, b:b + 1], None,
                                           ALU.subtract)
                    inst.then_inc(dve_step, 1)
                count[0] += 2
                dve.wait_ge(dve_step, count[0])
                v.tensor_copy(st[:, 44:45], st[:, 30:31]).then_inc(r_in, 1)

            def softmax_tail(e_at, out_at, col):
                step(v.reduce_sum(rs_[:, col, :], rt[:, e_at, :, :], AX_X))
                step(v.reciprocal(rs_[:, col + 1, :], rs_[:, col, :]))
                for b in range(2):
                    v.tensor_scalar(rt[:, out_at, b, :], rt[:, e_at, b, :], rs_[:, col + 1, b:b + 1], None,
                                    ALU.mult).then_inc(dve_step, 1)
                count[0] += 2
                dve.wait_ge(dve_step, count[0])

            dve.wait_ge(lg_ps, 1)
            step(v.tensor_copy(rt[:, 0, :, :], bank(7, 0, 2 * E).rearrange("p (b e) -> p b e", b=2)))
            softmax_head(rt[:, 0, :, :], 1, 0)
            dve.wait_ge(r_exp, 1)
            softmax_tail(2, 3, 1)
            step(v.tensor_tensor(rt[:, 4, 0, :], rt[:, 3, 0, :], rt[:, 3, 1, :], ALU.add))
            step(v.tensor_scalar(rt[:, 4, 1, :], rt[:, 4, 0, :], float(N // 2), None, ALU.mult))
            step(v.reciprocal(rt[:, 4, 0, :], rt[:, 4, 1, :]))
            step(v.tensor_scalar(rt[:, 4, 1, :], rt[:, 4, 0, :], CAPACITY, 1.0, ALU.mult, ALU.min))
            for b in range(2):
                step(v.tensor_tensor(rt[:, 3, b, :], rt[:, 3, b, :], rt[:, 4, 1, :], ALU.mult))
            softmax_head(rt[:, 3, :, :], 5, 3)
            dve.wait_ge(r_exp, 2)
            softmax_tail(6, 7, 4)
            for b in range(2):
                step(v.max(rt[:, 8, b, :], rt[:, 7, b, :]))
                v.max_index(top_i[:, b, :], rt[:, 8, b, :], rt[:, 7, b, :]).then_inc(idx_ready, 1)
            v.tensor_tensor(rs_[:, 7, :], rt[:, 8, :, 1], rt[:, 8, :, 0], ALU.subtract).then_inc(r_in, 1)
            dve.wait_ge(r_exp, 3)
            step(v.tensor_scalar(rs_[:, 9, :], rs_[:, 8, :], 1.0, None, ALU.add))
            step(v.reciprocal(rs_[:, 10, :], rs_[:, 9, :]))
            step(v.tensor_tensor(rs_[:, 11, :], rs_[:, 8, :], rs_[:, 10, :], ALU.mult))
            dve.wait_ge(idx_ready, 2)
            for b in range(2):
                for k in range(TOPK):
                    e = dve.value_load(top_i[0:1, b, k:k + 1], min_val=0, max_val=E - 1)
                    v.tensor_copy(b1s[:, b, k, :], b1_all[:, bass.ds(e, 1), :].rearrange("p o f -> p (o f)"))\
                        .then_inc(w2_ready, 1)
                    v.tensor_scalar(w2s[:, b, k, :, :].rearrange("p f c -> p (f c)"),
                                    w2[:, bass.ds(e, 1), :, :].rearrange("p o f c -> p (o f c)"),
                                    rs_[:, 10 + k, b:b + 1], None, ALU.mult).then_inc(w2_ready, 1)
                    v.tensor_scalar(b2s[:, b, k:k + 1], b2_all[:, bass.ds(e, 1)], rs_[:, 10 + k, b:b + 1], None,
                                    ALU.mult).then_inc(w2_ready, 1)
            dve.wait_ge(w2_ready, 12)
            for b in range(2):
                step(v.tensor_tensor(mb[:, b:b + 1], b2s[:, b, 0:1], b2s[:, b, 1:2], ALU.add))
            dve.wait_ge(t1_beta, 1)

            def finish(c):
                dve.wait_ge(LN[2]["out"], c + 1)
                v.scalar_tensor_tensor(conv_o[:, c * 512:(c + 1) * 512], centred[:, c * 512:(c + 1) * 512],
                                       VEC["L1_ffn_gamma"], x1[:, c * 512:(c + 1) * 512], ALU.mult, ALU.add)\
                    .then_inc(out_ready, 1)

            for c in range(4):
                b = c // 2
                dve.wait_ge(y_ps, 2 * c + 2)
                v.scalar_tensor_tensor(xs_flat[:, c * 512:(c + 1) * 512], bank(4 + c % 2), mb[:, b:b + 1],
                                       xn[:, c * 512:(c + 1) * 512], ALU.add, ALU.add).then_inc(u_ready, 1)
                dve.wait_ge(u_ready, c + 1)
                centre(2, c, xs_flat, 6 + c % 2)
            scale(2, 4, 0, centred)
            for c in range(4):
                finish(c)


_INS = ["x", "L0_conv_wq", "L0_conv_bq", "L0_conv_wk", "L0_conv_bk", "L0_conv_wv", "L0_conv_bv",
        "L0_conv_gamma", "L0_conv_beta", "L1_attn_Wqkv", "L1_attn_bqkv", "L1_attn_W0", "L1_attn_b0",
        "L1_ffn_Wr", "L1_ffn_br", "L1_ffn_W1", "L1_ffn_b1", "L1_ffn_W2", "L1_ffn_b2",
        "L1_ffn_gamma", "L1_ffn_beta"]


def kernel(**inputs):
    import ml_dtypes
    import numpy as np
    import concourse.bacc as bacc
    from concourse.bass_utils import run_bass_kernel_spmd

    nc = bacc.Bacc("TRN2", target_bir_lowering=False, num_devices=1)
    arrays, tensors = {}, {}
    for name in _INS:
        a = np.ascontiguousarray(inputs[name])
        arrays[f"in_{name}"] = a
        tensors[name] = nc.dram_tensor(f"in_{name}", a.shape, mybir.dt.from_np(a.dtype), kind="ExternalInput").ap()
    tensors["out"] = nc.dram_tensor("out_0", inputs["x"].shape, F32, kind="ExternalOutput").ap()
    _, _, h, w = inputs["x"].shape
    pair = np.arange(h * w * 49)
    row = pair // 49 // w + pair % 49 // 7 - 3
    col = pair // 49 % w + pair % 49 % 7 - 3
    inside = (row >= 0) & (row < h) & (col >= 0) & (col < w)
    mask = np.full((h * w, h * w), NEG, dtype=ml_dtypes.bfloat16)
    mask[pair[inside] % (h * w), (row * w + col)[inside]] = 0
    arrays["neighbours"] = mask
    tensors["neighbours"] = nc.dram_tensor("neighbours", mask.shape, BF16, kind="ExternalInput").ap()
    build(nc, tensors)
    r = run_bass_kernel_spmd(nc, [arrays], core_ids=[0])
    return r.results[0]["out_0"]
```

```python
from contextlib import ExitStack

import concourse.bass as bass
from concourse import mybir

F32 = mybir.dt.float32
BF16 = mybir.dt.bfloat16
F32R = mybir.dt.float32r
U32 = mybir.dt.uint32
ALU = mybir.AluOpType
ACT = mybir.ActivationFunctionType
AX_X = mybir.AxisListType.X

P = 128
NEG = -1.0e30
BIG = 3.0e38


def build(nc, t):
    x_in, out = t["x"], t["out"]
    B, C, H, W = x_in.shape
    HW = H * W
    N = B * HW
    assert C == P and W == 32 and B == 2

    GN_SIZE = C // 32
    UNROLL = 4
    CONV_ITERS = N // P // UNROLL
    CHUNKS = HW // P

    D = C
    HEADS = t["L1_attn_Wqkv"].shape[1] // (3 * D)
    GROUP_AT = [0]
    for r in range(3):
        GROUP_AT.append(GROUP_AT[-1] + (HW - r + 2) // 3)
    SCORE_SCALE = float(D) ** -0.5
    TILES = HW // P

    E = t["L1_ffn_Wr"].shape[1]
    FF = t["L1_ffn_W1"].shape[2]
    FC = FF // P
    TOPK = 2
    CAPACITY = float(-(-N * 1.25 // E))

    def segments(section, image):
        first_row = (2 * section + image) * HW
        pieces = []
        for r in range(3):
            lo, hi = GROUP_AT[r], GROUP_AT[r + 1]
            cuts = [lo] + [c for c in (512,) if lo < c < hi] + [hi]
            for a, b in zip(cuts, cuts[1:]):
                pieces.append((a, b - a, (first_row + r) % 3, (first_row + r) // 3 + a - lo))
        return pieces

    def groups(section, image):
        first_row = (2 * section + image) * HW
        return [(GROUP_AT[r], GROUP_AT[r + 1], (first_row + r) % 3, (first_row + r) // 3) for r in range(3)]

    ctx = ExitStack()
    with ctx:
        def sb(name, shape, dt=F32):
            return ctx.enter_context(nc.sbuf_tensor(name, shape, dt))

        def sem(name):
            return ctx.enter_context(nc.semaphore(name))

        ps = ctx.enter_context(nc.psum_tensor("ps", [P, 8 * 512], F32))

        def bank(n, lo=0, hi=512, rows=P):
            return ps[0:rows, n * 512 + lo:n * 512 + hi]

        def slot(n, lo=0, hi=1024):
            return ps[:, n * 1024 + lo:n * 1024 + hi]

        ident = sb("ident", [P, P])
        ident_b = sb("ident_b", [P, P], BF16)
        ones = sb("ones", [P, P])
        mean_w = sb("mean_w", [P, P])
        group_w = sb("group_w", [P, P])
        head_sel = sb("head_sel", [3 * HEADS, HEADS, P], BF16)

        x = sb("x", [P, N])
        conv_w = sb("conv_w", [P, 3, C])
        conv_wT = sb("conv_wT", [P, 3, C])
        NVEC = 8
        NROWS = NVEC + E * FC + E
        rows = sb("rows", [NROWS, P])
        cols = sb("cols", [P, NROWS])
        VEC = {n: cols[:, i:i + 1] for i, n in enumerate(
            ["L0_conv_bq", "L0_conv_bk", "L0_conv_bv", "L0_conv_gamma", "L0_conv_beta",
             "L1_attn_b0", "L1_ffn_gamma", "L1_ffn_beta"])}
        b1_all = cols[:, NVEC:NVEC + E * FC].rearrange("p (e f) -> p e f", f=FC)
        b2_all = cols[:, NVEC + E * FC:NROWS]
        wqkv = sb("wqkv", [P, 3, D, HEADS])
        bqkv = sb("bqkv", [P, 3, HEADS])
        bqkv_q = sb("bqkv_q", [P, 3, HEADS])
        w0 = sb("w0", [P, HEADS, D])
        w1 = sb("w1", [P, E, FF])
        w2 = sb("w2", [P, E, FC, D])
        wr = sb("wr", [P, E])
        score_scale = sb("score_scale", [P, 1])
        br = sb("br", [1, E])

        xg = sb("xg", [P, N])
        keys = sb("keys", [P, N])
        centred, squares = xg, keys
        vtok = sb("vtok", [P, 2, CHUNKS, C])
        conv_o = sb("conv_o", [P, N])
        x1 = sb("x1", [P, N])
        xn = sb("xn", [P, N])
        diagonals = sb("diagonals", [P, N])
        sd = sb("sd", [P, N // P])
        st = sb("st", [P, 64])
        bn6 = sb("bn6", [P, 4, 6])

        conv_q = sb("conv_q", [P, UNROLL, P])
        with ExitStack() as early:
            probs = early.enter_context(nc.sbuf_tensor("probs", [P, UNROLL, HW], F32))
            probsT = early.enter_context(nc.sbuf_tensor("probsT", [P, UNROLL, HW], F32))
        with ExitStack() as middle:
            kT_hi, kT_lo, qT_hi, qT_lo = (
                middle.enter_context(nc.sbuf_tensor(n, [P, 2, HW], F32R)) for n in ("kT_hi", "kT_lo", "qT_hi", "qT_lo"))
        late_buf = sb("late", [P, 4 * N])
        late = late_buf[:, :]
        negmax = sb("negmax", [P, UNROLL])
        maxima = sb("maxima", [P, UNROLL])
        psums = sb("psums", [P, UNROLL])
        precip = sb("precip", [P, UNROLL])
        otok = sb("otok", [P, UNROLL, C])

        w_head = sb("w_head", [P, 2, 3, D])
        w_headT = sb("w_headT", [P, 3, D])
        fold = sb("fold", [P, HEADS, 3, D])
        neighbours = sb("neighbours_sb", [P, TILES, HW], BF16)
        exps = sb("exps", [P, 2, HW], BF16)
        diag_junk = sb("diag_junk", [P, P])
        diag8 = sb("diag8", [P, 2, TILES])
        diag_all = sb("diag_all", [P, HEADS * 2 * TILES])
        nmax_all = sb("nmax_all", [P, HEADS * 2 * TILES])
        sum_all = sb("sum_all", [P, HEADS * 2 * TILES])
        a_all = sb("a_all", [P, HEADS * 2 * TILES])
        a_rest = sb("a_rest", [P, HEADS * 2 * TILES])
        a3 = sb("a3", [P, 2 * TILES, 3, HEADS], BF16)
        aT = sb("aT", [3 * HEADS, 2, HW], BF16)
        vb = sb("vb", [P, 3, HEADS])
        vb_rest = sb("vb_rest", [P, 3, HEADS])
        vb3 = sb("vb3", [P, 3, 3, 3, HEADS], BF16)
        vbT = sb("vbT", [3 * HEADS, 3, 3, P], BF16)
        xv = sb("xv", [P, 2, HW])
        xs = late[:, 3 * N:4 * N].rearrange("p (b n) -> p b n", b=2)
        fold_h = w_head
        sel_h = sb("sel_h", [3 * HEADS, 2, P], BF16)
        xs_flat = xs[:, :, :].rearrange("p b n -> p (b n)")
        t1 = late[:, 0:N]

        mb = sb("mb", [P, 2])
        mbb = sb("mbb", [P, 2, P])
        rt = sb("rt", [P, 12, 2, E])
        rs_ = sb("rs_", [P, 16, 2])
        top_i = sb("top_i", [P, 2, E], U32)
        w1s = late[:, N:N + 2 * TOPK * FF].rearrange("p (b k f) -> p b k f", b=2, k=TOPK)
        w2s = late[:, N + 2 * TOPK * FF:2 * N].rearrange("p (b k f c) -> p b k f c", b=2, k=TOPK, f=FC)
        b1s = sb("b1s", [P, 2, TOPK, FC])
        b2s = sb("b2s", [P, 2, TOPK])
        hid = late[:, 2 * N:3 * N].rearrange("p (n f c) -> p n f c", n=2, f=FC)

        x_in_sem = [sem(f"x_landed{b}") for b in range(2)]
        mask_in = sem("mask_landed")
        conv_w_in, rows_in, wqkv_in, w0_in, ffn_in = (sem(n) for n in (
            "conv_w_landed", "rows_landed", "wqkv_landed", "w0_landed", "ffn_landed"))
        out_sem = sem("out_stored")
        consts, ident_made = sem("consts"), sem("ident_made")
        pool_step, dve_step, act_step = sem("pool_step"), sem("dve_step"), sem("act_step")
        gn_stats, gn_mean, gn_q, gn_var, gn_aff = (sem(n) for n in (
            "gn_stats", "gn_mean", "gn_q", "gn_var", "gn_aff"))
        xg_ready = [sem(f"xg_ready{b}") for b in range(2)]
        wT_ps, wT_sb, cols_ps, cols_sb = (sem(n) for n in ("wT_ps", "wT_sb", "cols_ps", "cols_sb"))
        k_ps, k_sb, v_ps, v_sb = (sem(n) for n in ("k_ps", "k_sb", "v_ps", "v_sb"))

        cq_ps, cq_sb, cs_ps, cg_sb, cm_sb, ce_sb, ct_ps, ct_sb, co_ps, co_sb, cx_ps, cr_sb = (
            sem(n) for n in ("cq_ps", "cq_sb", "cs_ps", "cg_sb", "cm_sb", "ce_sb",
                             "ct_ps", "ct_sb", "co_ps", "co_sb", "cx_ps", "cr_sb"))
        cx_sb, cmax_sb = sem("cx_sb"), sem("cmax_sb")
        gn_eps, gn_root, bn_eps, bn_root = (sem(n) for n in ("gn_eps", "gn_root", "bn_eps", "bn_root"))
        bn_aff, bn_relu, x1_ready = sem("bn_aff"), sem("bn_relu"), sem("x1_ready")
        f_stage, f_T_ps, f_T_sb, f_m_ps, f_m_sb = (sem(n) for n in (
            "fold_staged", "fold_T_ps", "fold_T_sb", "fold_m_ps", "fold_m_sb"))
        vb_ps, vb_sb, vbT_ps, vbT_sb = (sem(n) for n in ("vb_ps", "vb_sb", "vbT_ps", "vbT_sb"))

        def ln_sems(k):
            return {n: sem(f"ln{k}_{n}") for n in (
                "mean", "centred", "square", "var", "eps", "sqrt", "diag", "spread", "out")}

        LN = [ln_sems(k) for k in range(3)]
        hi_ready, split_done = sem("hi_ready"), sem("split_done")
        staged, job_ps, exp_done, tile_maxed, diag_full, diag_saved = (sem(n) for n in (
            "w_head_staged", "job_ps", "exp_done", "tile_maxed", "diag_full", "diag_saved"))
        bq_ready = sem("bq_ready")
        a_exp, a_sum, a3_ready, aT_ps, aT_sb = (sem(n) for n in ("a_exp", "a_sum", "a3_ready", "aT_ps", "aT_sb"))
        xv_ready = sem("xv_ready")
        v_staged = [sem(f"v_staged{p}") for p in range(2)]
        ab_ps = [sem(f"ab_ps{b}") for b in range(2)]
        xs_sb = [sem(f"xs_sb{b}") for b in range(2)]
        xs_used = [sem(f"xs_used{b}") for b in range(2)]
        t1_ready, t1_beta = sem("t1_ready"), sem("t1_beta")
        mb_ready, lg_ps, r_in, r_exp = (sem(n) for n in ("mb_ready", "logits_ps", "r_in", "r_exp"))
        idx_ready, w1_ready, w2_ready = sem("idx_ready"), sem("w1_ready"), sem("w2_ready")
        h_ps, h_sb, y_ps, u_ready = (sem(n) for n in ("h_ps", "h_sb", "y_ps", "u_ready"))
        out_ready = sem("out_ready")

        def conv_tile(it, u, lag):
            v = (u - lag) % UNROLL
            start = (u - lag) // UNROLL * UNROLL
            if isinstance(it, int):
                n = it * UNROLL + start + v
                return (n, v) if 0 <= n < N // P else None
            return it * UNROLL + (start + v), v

        def conv_row(it, u, lag):
            return it * (UNROLL // 2) + ((u - lag) // UNROLL * (UNROLL // 2) + (u - lag) % UNROLL // 2)

        def at_row(it, u, lag, size):
            row = conv_row(it, u, lag)
            return slice(row * size, (row + 1) * size) if isinstance(it, int) else bass.ds(row * size, size)

        def in_loop(eng, first, end, body, *tail):
            for i in range(first):
                body(i)
            with eng.Fori(first, end) as i:
                body(i)
            for i in tail:
                body(i)

        def at_head(h):
            return slice(h, h + 1) if isinstance(h, int) else bass.ds(h, 1)

        def head_jobs(last):
            jobs = [("score", 0, n) for n in range(TILES)]
            jobs[3:3] = [("keys", 1, 0), ("queries", 1, 0)]
            second = [("score", 1, n) for n in range(TILES)]
            if not last:
                second[3:3] = [("next keys", 0, 0), ("next queries", 0, 0)]
            return jobs + second

        PRE = 2
        PER_HEAD = 2 * TILES + 4
        SLOTS = 4

        block = ctx.enter_context(nc.Block())

        @block.sync
        def _(sp):
            xf = x_in.rearrange("b c h w -> c b (h w)")
            for b in range(2):
                sp.dma_start(x[:, b * HW:(b + 1) * HW], xf[:, b, :]).then_inc(x_in_sem[b], 16)
            sp.dma_start(neighbours[:, :, :], t["neighbours"].rearrange("(i p) k -> p i k", p=P)).then_inc(mask_in, 16)
            sp.dma_start(wqkv[:, :, :, :],
                         t["L1_attn_Wqkv"].rearrange("c (j d h) -> c j d h", j=3, h=HEADS)).then_inc(wqkv_in, 16)
            sp.dma_start(bqkv[:, :, :],
                         t["L1_attn_bqkv"].rearrange("(j d h) -> d j h", j=3, h=HEADS)).then_inc(wqkv_in, 16)
            sp.dma_start(w1[:, :, :], t["L1_ffn_W1"].rearrange("e c f -> c e f")).then_inc(ffn_in, 16)
            sp.dma_start(w2[:, :, :, :],
                         t["L1_ffn_W2"].rearrange("e (g f) c -> f e g c", f=P)).then_inc(ffn_in, 16)
            sp.dma_start(wr[:, :], t["L1_ffn_Wr"]).then_inc(ffn_in, 16)
            sp.dma_start(br[:, :], t["L1_ffn_br"].rearrange("(a e) -> a e", a=1)).then_inc(ffn_in, 16)
            of = out.rearrange("b c h w -> c b (h w)")
            for n in range(4):
                sp.wait_ge(out_ready, n + 1)
                b, half = n // 2, n % 2
                sp.dma_start(of[:, b, half * 512:(half + 1) * 512],
                             conv_o[:, n * 512:(n + 1) * 512]).then_inc(out_sem, 16)
            sp.wait_ge(out_sem, 64)

        @block.gpsimd
        def _(pool):
            g = nc.gpsimd
            count = [0]

            def step(inst):
                inst.then_inc(pool_step, 1)
                count[0] += 1
                pool.wait_ge(pool_step, count[0])

            step(g.memset(ident[:, :], 0.0))
            g.affine_select(out=ident[:, :], in_=ident[:, :], compare_op=ALU.not_equal, fill=1.0, base=0,
                            pattern=[[-1, P]], channel_multiplier=1).then_inc(ident_made, 1)
            pool.wait_ge(ident_made, 1)
            g.tensor_copy(ident_b[:, :], ident[:, :]).then_inc(consts, 1)
            g.memset(ones[:, :], 1.0).then_inc(consts, 1)
            g.memset(mean_w[:, :], 1.0 / C).then_inc(consts, 1)
            gv = group_w[:, :].rearrange("p (g k) -> p g k", k=GN_SIZE)
            step(g.memset(group_w[:, :], 1.0 / GN_SIZE))
            step(g.affine_select(out=gv, in_=gv, compare_op=ALU.is_ge, fill=0.0, base=0,
                                 pattern=[[-GN_SIZE, C // GN_SIZE], [0, GN_SIZE]], channel_multiplier=1))
            g.affine_select(out=gv, in_=gv, compare_op=ALU.is_ge, fill=0.0, base=GN_SIZE - 1,
                            pattern=[[GN_SIZE, C // GN_SIZE], [0, GN_SIZE]], channel_multiplier=-1)\
                .then_inc(consts, 1)
            step(g.memset(head_sel[:, :, :], 0.0))
            for part in range(3):
                inst = g.affine_select(out=head_sel[:, :, :], in_=head_sel[:, :, :], compare_op=ALU.not_equal,
                                       fill=1.0, base=-part * HEADS, pattern=[[-1, HEADS], [0, P]],
                                       channel_multiplier=1)
                if part < 2:
                    step(inst)
                else:
                    inst.then_inc(consts, 1)

            pool.wait_ge(wqkv_in, 32)
            def stage_fold(h):
                if not (isinstance(h, int) and h == 0):
                    pool.wait_ge(f_T_ps, h)
                g.tensor_copy(w_head[:, 0, :, :], wqkv[:, :, :, at_head(h)].rearrange("p j d o -> p j (d o)"))\
                    .then_inc(f_stage, 1)

            in_loop(pool, 1, HEADS, stage_fold)

            step(g.memset(score_scale[:, :], SCORE_SCALE))
            g.tensor_scalar(bqkv_q[:, :, :], bqkv[:, :, :], SCORE_SCALE, None, ALU.mult).then_inc(bq_ready, 1)
            pool.wait_ge(f_T_ps, HEADS)
            def stage(h):
                src = wqkv[:, :, :, at_head(h)].rearrange("p j d o -> p j (d o)")
                g.tensor_copy(w_head[:, 0, :, :], src).then_inc(staged, 1)
                g.tensor_tensor(w_head[:, 1, :, :], src, score_scale[:, 0:1].broadcast_to([P, 3 * D])
                                .rearrange("p (j d) -> p j d", j=3), ALU.mult).then_inc(staged, 1)

            stage(0)

            pool.wait_ge(LN[0]["out"], 4)
            for b in range(2):
                for lo, hi, _, tok in groups(2, b):
                    g.tensor_copy(xv[:, b, lo:hi], xn[:, tok:tok + hi - lo]).then_inc(xv_ready, 1)

            def head(h, last):
                for b in range(2):
                    if b == 0 and not last:
                        pool.wait_ge(job_ps, PRE + h * PER_HEAD + 5)
                        stage(h + 1)
                    pool.wait_ge(diag_full, h * 2 + b + 1)
                    if last:
                        dst = diag_all[:, (2 * h + b) * TILES:(2 * h + b + 1) * TILES]
                    else:
                        dst = diag_all[:, bass.ds(h * (2 * TILES) + b * TILES, TILES)]
                    g.tensor_copy(dst, diag8[:, b, :]).then_inc(diag_saved, 1)

            in_loop(pool, 1, HEADS - 1, lambda h: head(h, isinstance(h, int) and h == HEADS - 1), HEADS - 1)

            def stage_values(h2):
                for p in range(2):
                    if not (isinstance(h2, int) and h2 == 0):
                        pool.wait_ge(xs_used[1], h2 * 2 + p - 1)
                    pair = h2 * 2 + p
                    g.tensor_copy(sel_h[:, p, :], head_sel[:, at_head(pair), :].rearrange("p o m -> p (o m)"))\
                        .then_inc(v_staged[p], 1)
                    g.tensor_copy(fold_h[:, p, :, :], fold[:, at_head(pair), :, :]
                                  .rearrange("p o j d -> p (o j) d")).then_inc(v_staged[p], 1)

            in_loop(pool, 1, HEADS // 2, stage_values)

            pool.wait_ge(idx_ready, 2)
            for b in range(2):
                for k in range(TOPK):
                    e = pool.value_load(top_i[0:1, b, k:k + 1], min_val=0, max_val=E - 1)
                    g.tensor_copy(w1s[:, b, k, :], w1[:, bass.ds(e, 1), :].rearrange("p o f -> p (o f)"))\
                        .then_inc(w1_ready, 1)

        @block.scalar
        def _(act):
            a = nc.scalar
            for j, n in enumerate(["wq", "wk", "wv"]):
                act.dma_start(conv_w[:, j, :], t[f"L0_conv_{n}"]).then_inc(conv_w_in, 16)
            for i, n in enumerate(VEC):
                act.dma_start(rows[i:i + 1, :], t[n].rearrange("(a c) -> a c", a=1)).then_inc(rows_in, 16)
            act.dma_start(rows[NVEC:NVEC + E * FC, :],
                          t["L1_ffn_b1"].rearrange("e (g f) -> (e g) f", f=P)).then_inc(rows_in, 16)
            act.dma_start(rows[NVEC + E * FC:NROWS, :], t["L1_ffn_b2"]).then_inc(rows_in, 16)
            act.dma_start(w0[:, :, :], t["L1_attn_W0"].rearrange("(d h) c -> d h c", h=HEADS)).then_inc(w0_in, 16)

            act.wait_ge(wT_ps, 1)
            a.copy(conv_wT[:, :, :], bank(0, 0, 3 * C).rearrange("p (j c) -> p j c", j=3)).then_inc(wT_sb, 1)
            act.wait_ge(cols_ps, 1)
            a.copy(cols[:, :], bank(1, 0, NROWS)).then_inc(cols_sb, 1)
            act.wait_ge(gn_eps, 1)
            a.activation(st[:, 22:24], st[:, 22:24], ACT.Sqrt).then_inc(gn_root, 1)
            act.wait_ge(gn_aff, 1)
            a.activation(xg[:, HW:N], x[:, HW:N], ACT.Identity,
                         scale=st[:, 18:19], bias=st[:, 20:21]).then_inc(xg_ready[1], 1)
            act.wait_ge(cols_sb, 1)
            for n in range(4):
                act.wait_ge(k_ps, n + 1)
                a.activation(keys[:, n * 512:(n + 1) * 512], bank(4 + n), ACT.Identity,
                             bias=VEC["L0_conv_bk"]).then_inc(k_sb, 1)

            def conv_step(it):
                for u in range(UNROLL):
                    exponentiate(it, u)
                    if conv_tile(it, u, 4):
                        n, v = conv_tile(it, u, 4)
                        act.wait_ge(cx_ps, n + 1)
                        a.activation(conv_o2[:, v % 2, at_row(it, u, 4, P)], slot(v, 0, P), ACT.Identity,
                                     bias=VEC["L0_conv_bv"]).then_inc(cx_sb, 1)
                    if conv_tile(it, u, 2):
                        n, v = conv_tile(it, u, 2)
                        act.wait_ge(ct_ps, n + 1)
                        a.copy(probsT[:, v, :], slot(v)).then_inc(ct_sb, 1)
                    if conv_tile(it, u, 0):
                        n, v = conv_tile(it, u, 0)
                        act.wait_ge(cq_ps, n + 1)
                        a.activation(conv_q[:, v, :], slot(v, 0, P), ACT.Identity,
                                     bias=VEC["L0_conv_bq"]).then_inc(cq_sb, 1)

            def exponentiate(it, u):
                if conv_tile(it, u, 2):
                    n, v = conv_tile(it, u, 2)
                    act.wait_ge(cm_sb, n + 1)
                    a.activation(probs[:, v, :], probs[:, v, :], ACT.Exp, bias=negmax[:, v:v + 1],
                                 accum_out=psums[:, v:v + 1]).then_inc(ce_sb, 1)

            conv_o2 = conv_o[:, :].rearrange("p (b n) -> p b n", b=2)
            in_loop(act, 1, CONV_ITERS, conv_step, CONV_ITERS)

            def fold_head(h):
                act.wait_ge(f_T_ps, h + 1)
                a.copy(w_headT[:, :, :], bank(4, 0, 3 * D).rearrange("p (j d) -> p j d", j=3)).then_inc(f_T_sb, 1)
                act.wait_ge(f_m_ps, h + 1)
                a.copy(fold[:, at_head(h), :, :].rearrange("p o j d -> p (o j) d"),
                       bank(5, 0, 3 * D).rearrange("p (j d) -> p j d", j=3)).then_inc(f_m_sb, 1)

            in_loop(act, 1, HEADS, fold_head)

            act.wait_ge(bn_eps, 1)
            a.activation(st[:, 26:27], st[:, 26:27], ACT.Sqrt).then_inc(bn_root, 1)
            act.wait_ge(bn_aff, 1)
            for n in range(4):
                a.activation(conv_o[:, n * 512:(n + 1) * 512], conv_o[:, n * 512:(n + 1) * 512], ACT.Relu,
                             scale=st[:, 30:31], bias=st[:, 31:32]).then_inc(bn_relu, 1)

            def squares_of(k):
                for c in range(4):
                    act.wait_ge(LN[k]["centred"], c + 1)
                    a.activation(squares[:, c * 512:(c + 1) * 512], centred[:, c * 512:(c + 1) * 512],
                                 ACT.Square).then_inc(LN[k]["square"], 1)

            def root(k):
                act.wait_ge(LN[k]["eps"], 1)
                a.activation(sd[:, :], sd[:, :], ACT.Sqrt).then_inc(LN[k]["sqrt"], 1)

            squares_of(0)
            root(0)

            act.wait_ge(bq_ready, 1)

            def evacuate(kind, b, h, s):
                section = 1 if "keys" in kind else 0
                dst, bias = (kT_hi, bqkv) if section else (qT_hi, bqkv_q)
                for lo, hi, j, _ in groups(section, b):
                    a.activation(dst[:, b, lo:hi], slot(s, lo, hi), ACT.Identity, bias=bias[:, j, at_head(h)])\
                        .then_inc(hi_ready, 1)

            for g, kind in enumerate(("keys", "queries")):
                act.wait_ge(job_ps, g + 1)
                evacuate(kind, 0, 0, g)

            def head(h):
                last = isinstance(h, int) and h == HEADS - 1
                scores = 0
                for n, (kind, b, tile) in enumerate(head_jobs(last)):
                    s = (PRE + n) % SLOTS
                    if kind == "score":
                        col = h * (2 * TILES) + scores
                        at = at_head(col)
                        scores += 1
                        act.wait_ge(tile_maxed, h * (4 * TILES) + 2 * scores)
                        if not (isinstance(h, int) and h == 0 and scores <= 2):
                            act.wait_ge(exp_done, h * (2 * TILES) + scores - 2)
                        a.activation(exps[:, scores % 2, :], slot(s), ACT.Exp, bias=nmax_all[:, at],
                                     accum_out=sum_all[:, at]).then_inc(exp_done, 1)
                    else:
                        act.wait_ge(job_ps, PRE + h * PER_HEAD + n + 1)
                        evacuate(kind, b, h + 1 if "next" in kind else h, s)

            in_loop(act, 1, HEADS - 1, head, HEADS - 1)

            act.wait_ge(a_sum, 1)
            a.activation(a_all[:, :], a_rest[:, :], ACT.Exp).then_inc(a_exp, 1)
            for b in range(2):
                act.wait_ge(aT_ps, b + 1)
                a.copy(aT[:, b, :], bank(6 + b, rows=3 * HEADS).bitcast(BF16)[:, 0:HW]).then_inc(aT_sb, 1)

            squares_of(1)
            root(1)
            act.wait_ge(t1_ready, 6)
            a.activation(x1[:, :], t1[:, :], ACT.Identity, bias=VEC["L1_ffn_beta"]).then_inc(t1_beta, 1)
            act.wait_ge(r_in, 1)
            a.activation(rt[:, 2, :, :], rt[:, 1, :, :], ACT.Exp).then_inc(r_exp, 1)
            act.wait_ge(r_in, 2)
            a.activation(rt[:, 6, :, :], rt[:, 5, :, :], ACT.Exp).then_inc(r_exp, 1)
            act.wait_ge(r_in, 3)
            a.activation(rs_[:, 8, :], rs_[:, 7, :], ACT.Exp).then_inc(r_exp, 1)

            act.wait_ge(w2_ready, 12)
            for n in range(8):
                b, half, k = n // 4, n // 2 % 2, n % 2
                for f in range(FC):
                    act.wait_ge(h_ps, 2 * n + f + 1)
                    if n >= 2:
                        act.wait_ge(y_ps, n - 1)
                    a.activation(hid[:, n % 2, f, :], bank(2 * (n % 2) + f), ACT.Gelu,
                                 bias=b1s[:, b, k, f:f + 1]).then_inc(h_sb, 1)
                if k == 1:
                    c = n // 2
                    act.wait_ge(LN[2]["centred"], c + 1)
                    a.activation(squares[:, c * 512:(c + 1) * 512], centred[:, c * 512:(c + 1) * 512],
                                 ACT.Square).then_inc(LN[2]["square"], 1)
            root(2)

        @block.tensor
        def _(pe):
            mm = nc.tensor.matmul
            pe.wait_ge(ident_made, 1)
            pe.wait_ge(conv_w_in, 48)
            for j in range(3):
                last = nc.tensor.transpose(bank(0, j * C, (j + 1) * C), conv_w[:, j, :], ident[:, :])
            last.then_inc(wT_ps, 1)
            pe.wait_ge(rows_in, 16 * (NVEC + 2))
            nc.tensor.transpose(bank(1, 0, NROWS), rows[:, :], ident[0:NROWS, 0:NROWS]).then_inc(cols_ps, 1)
            pe.wait_ge(consts, 4)
            pe.wait_ge(gn_stats, 1)
            mm(bank(2, 0, 2), group_w[:, :], st[:, 0:2], start=True, stop=True).then_inc(gn_mean, 1)
            pe.wait_ge(gn_q, 1)
            mm(bank(3, 0, 2), group_w[:, :], st[:, 8:10], start=True, stop=True).then_inc(gn_var, 1)
            pe.wait_ge(wT_sb, 1)
            for n in range(4):
                if n % 2 == 0:
                    pe.wait_ge(xg_ready[n // 2], 1)
                mm(bank(4 + n), conv_wT[:, 1, :], xg[:, n * 512:(n + 1) * 512], start=True, stop=True)\
                    .then_inc(k_ps, 1)
            pe.wait_ge(cols_sb, 1)
            for n in range(2 * CHUNKS):
                last = mm(bank(n // 4, (n % 4) * P, (n % 4 + 1) * P), xg[:, n * P:(n + 1) * P],
                          conv_wT[:, 2, :], start=True, stop=True)
                if n % 4 == 3:
                    last.then_inc(v_ps, 1)

            pe.wait_ge(k_sb, 4)
            pe.wait_ge(v_sb, 4)
            pe.wait_ge(mask_in, 16)
            def conv_step(it):
                for u in range(UNROLL):
                    if conv_tile(it, u, 1):
                        n, v = conv_tile(it, u, 1)
                        pe.wait_ge(cq_sb, n + 1)
                        row = at_head(conv_row(it, u, 1))
                        for half in range(2):
                            lo, hi = half * 512, (half + 1) * 512
                            mm(slot(v, lo, hi), conv_q[:, v, :], keys[:, (v % 2) * HW + lo:(v % 2) * HW + hi],
                               start=True, stop=False)
                            last = mm(slot(v, lo, hi), ident_b[:, :],
                                      neighbours[:, row, lo:hi].rearrange("p o k -> p (o k)"),
                                      start=False, stop=True)
                        last.then_inc(cs_ps, 1)
                    if conv_tile(it, u, 4):
                        n, v = conv_tile(it, u, 4)
                        pe.wait_ge(co_sb, n + 1)
                        nc.tensor.transpose(slot(v, 0, P), otok[:, v, :], ident[:, :]).then_inc(cx_ps, 1)
                    if conv_tile(it, u, 2):
                        n, v = conv_tile(it, u, 2)
                        pe.wait_ge(ce_sb, n + 1)
                        for k in range(CHUNKS):
                            last = nc.tensor.transpose(slot(v, k * P, (k + 1) * P), probs[:, v, k * P:(k + 1) * P],
                                                       ident[:, :])
                        last.then_inc(ct_ps, 1)
                    if conv_tile(it, u, 0):
                        n, v = conv_tile(it, u, 0)
                        if conv_tile(it, u, 4):
                            pe.wait_ge(cx_sb, conv_tile(it, u, 4)[0] + 1)
                        mm(slot(v, 0, P), conv_wT[:, 0, :], xg2[:, v % 2, at_row(it, u, 0, P)],
                           start=True, stop=True).then_inc(cq_ps, 1)
                    if conv_tile(it, u, 3):
                        n, v = conv_tile(it, u, 3)
                        pe.wait_ge(ct_sb, n + 1)
                        for k in range(CHUNKS):
                            last = mm(slot(v, 0, P), probsT[:, v, k * P:(k + 1) * P], vtok[:, v % 2, k, :],
                                      start=(k == 0), stop=(k == CHUNKS - 1))
                        last.then_inc(co_ps, 1)

            xg2 = xg[:, :].rearrange("p (b n) -> p b n", b=2)
            in_loop(pe, 1, CONV_ITERS, conv_step, CONV_ITERS)

            pe.wait_ge(cx_sb, N // P)
            pe.wait_ge(w0_in, 16)

            def fold_head(h):
                pe.wait_ge(f_stage, h + 1)
                for j in range(3):
                    last = nc.tensor.transpose(bank(4, j * D, (j + 1) * D), w_head[:, 0, j, :], ident[:, :])
                last.then_inc(f_T_ps, 1)
                pe.wait_ge(f_T_sb, h + 1)
                if not (isinstance(h, int) and h == 0):
                    pe.wait_ge(f_m_sb, h)
                for j in range(3):
                    last = mm(bank(5, j * D, (j + 1) * D), w_headT[:, j, :],
                              w0[:, at_head(h), :].rearrange("p o c -> p (o c)"), start=True, stop=True)
                last.then_inc(f_m_ps, 1)

            in_loop(pe, 1, HEADS, fold_head)
            for h in range(HEADS):
                last = mm(bank(6, 3 * h, 3 * h + 3), w0[:, h, :], bqkv[:, :, h], start=True, stop=True)
            last.then_inc(vb_ps, 1)
            pe.wait_ge(vb_sb, 1)
            vbank = bank(7, rows=3 * HEADS).bitcast(BF16)
            for q in range(3):
                for half, js in ((0, (0, 1, 2)),):
                    for j in js:
                        n = 3 * q + j
                        tgt = (vbank if n < 8 else bank(6, rows=3 * HEADS).bitcast(BF16))
                        last = nc.tensor.transpose(tgt[:, (n % 8) * P:(n % 8 + 1) * P],
                                                   vb3[:, j, q, :, :].rearrange("p a h -> p (a h)"), ident_b[:, :])
            last.then_inc(vbT_ps, 1)

            def channel_means(k, c, source, name, n):
                mm(bank(n), mean_w[:, :], source[:, c * 512:(c + 1) * 512], start=True, stop=True)\
                    .then_inc(LN[k][name], 1)

            def variances(k, n):
                for i in range(N // P):
                    if i % 4 == 0:
                        pe.wait_ge(LN[k]["square"], i // 4 + 1)
                    last = mm(bank(n, i, i + 1), squares[:, i * P:(i + 1) * P], mean_w[:, 0:1], start=True, stop=True)
                last.then_inc(LN[k]["var"], 1)

            def spread(k, n):
                for c in range(4):
                    pe.wait_ge(LN[k]["diag"], c + 1)
                    mm(bank(n + c), ones[:, :], diagonals[:, c * 512:(c + 1) * 512], start=True, stop=True)\
                        .then_inc(LN[k]["spread"], 1)

            for c in range(4):
                pe.wait_ge(x1_ready, c + 1)
                channel_means(0, c, x1, "mean", c)
            variances(0, 4)
            spread(0, 0)
            pe.wait_ge(vbT_sb, 2)

            pe.wait_ge(LN[0]["out"], 4)
            pe.wait_ge(staged, 2)

            def project(kind, b, s):
                section = 1 if "keys" in kind else 0
                for at, n, j, tok in segments(section, b):
                    last = mm(slot(s, at, at + n), w_head[:, 1 - section, j, :], xn[:, tok:tok + n], start=True, stop=True)
                last.then_inc(job_ps, 1)

            project("keys", 0, 0)
            project("queries", 0, 1)

            def head(h):
                zeroth, last_head = (isinstance(h, int) and h == k for k in (0, HEADS - 1))
                scores = 0
                jobs = head_jobs(last_head)
                for n, (kind, b, tile) in enumerate(jobs):
                    g = PRE + n
                    before = n - SLOTS
                    order = jobs if before >= 0 else head_jobs(False)
                    if order[before][0] == "score" and not (zeroth and before < 0):
                        pe.wait_ge(exp_done, h * (2 * TILES) + sum(o[0] == "score" for o in order[:before + 1])
                                   if before >= 0 else
                                   h * (2 * TILES) - sum(o[0] == "score" for o in order[before:]) + 1)
                    elif before >= 0:
                        pe.wait_ge(split_done, h * 4 + PRE + sum(o[0] != "score" for o in order[:before + 1]))
                    if kind == "score":
                        if tile == 0:
                            pe.wait_ge(split_done, h * 4 + PRE + 2 * b)
                        rows_ = slice(tile * P, (tile + 1) * P)
                        for half in range(2):
                            cols_ = slice(half * 512, (half + 1) * 512)
                            tgt = slot(g % SLOTS, half * 512, (half + 1) * 512)
                            mm(tgt, kT_hi[:, b, rows_], qT_hi[:, b, cols_], start=True, stop=False)
                            mm(tgt, kT_hi[:, b, rows_], qT_lo[:, b, cols_], start=False, stop=False)
                            last = mm(tgt, kT_lo[:, b, rows_], qT_hi[:, b, cols_], start=False, stop=True)
                        last.then_inc(job_ps, 1)
                    else:
                        if kind == "next keys":
                            pe.wait_ge(staged, h * 2 + 4)
                        project(kind, b, g % SLOTS)

            in_loop(pe, 1, HEADS - 1, head, HEADS - 1)

            pe.wait_ge(a3_ready, 3)
            pe.wait_ge(exp_done, HEADS * 2 * TILES)
            for b in range(2):
                tgt = bank(6 + b, rows=3 * HEADS).bitcast(BF16)
                for n in range(TILES):
                    last = nc.tensor.transpose(tgt[:, n * P:(n + 1) * P],
                                               a3[:, b * TILES + n, :, :].rearrange("p a h -> p (a h)"), ident_b[:, :])
                last.then_inc(aT_ps, 1)
            pe.wait_ge(aT_sb, 2)
            for b in range(2):
                opened = set()
                for at, n, j, _ in segments(2, b):
                    for q in range(3):
                        first = at // 512 not in opened
                        opened.add(at // 512)
                        mm(slot(b, at, at + n), vbT[:, j, q, :], aT[:, b, at:at + n], start=first, stop=False,
                           skip_group_check=True)
            pe.wait_ge(xv_ready, 6)

            def broadcast(h, p, b):
                if not (isinstance(h, int) and h == 0):
                    pe.wait_ge(xs_sb[b], h)
                for half in range(2):
                    last = mm(slot(2 + b, half * 512, (half + 1) * 512), sel_h[:, p, :],
                              aT[:, b, half * 512:(half + 1) * 512], start=True, stop=True)
                last.then_inc(ab_ps[b], 1)

            def value_products(h, p, b):
                pe.wait_ge(xs_sb[b], h + 1)
                for at, n, j, _ in segments(2, b):
                    last = mm(slot(b, at, at + n), fold_h[:, p, j, :], xs[:, b, at:at + n],
                              start=False, stop=False, skip_group_check=True)
                last.then_inc(xs_used[b], 1)

            def values(h2):
                for p in range(2):
                    h = h2 * 2 + p
                    pe.wait_ge(v_staged[p], h2 * 2 + 2)
                    broadcast(h, p, 0)
                    if not (isinstance(h, int) and h == 0):
                        value_products(h - 1, 1 - p, 1)
                    broadcast(h, p, 1)
                    value_products(h, p, 0)

            in_loop(pe, 1, HEADS // 2, values)
            value_products(HEADS - 1, 1, 1)

            for c in range(4):
                pe.wait_ge(t1_ready, 3 if c < 2 else 6)
                channel_means(1, c, t1, "mean", 4 + c)
            variances(1, 0)
            spread(1, 4)

            pe.wait_ge(mb_ready, 2)
            pe.wait_ge(ffn_in, 64)
            for b in range(2):
                mm(bank(7, b * E, (b + 1) * E), mbb[:, b, :], wr[:, :], start=True, stop=False)
                last = mm(bank(7, b * E, (b + 1) * E), ones[0:1, :], br[:, :], start=False, stop=True)
            last.then_inc(lg_ps, 1)

            pe.wait_ge(w1_ready, 4)
            pe.wait_ge(w2_ready, 12)

            def hidden(n):
                b, half, k = n // 4, n // 2 % 2, n % 2
                if n >= 2:
                    pe.wait_ge(h_sb, 2 * n - 2)
                for f in range(FC):
                    mm(bank(2 * (n % 2) + f), w1s[:, b, k, f * P:(f + 1) * P],
                       xn[:, (n // 2) * 512:(n // 2 + 1) * 512], start=True, stop=True).then_inc(h_ps, 1)

            def outputs(n):
                b, half, k = n // 4, n // 2 % 2, n % 2
                c = n // 2
                pe.wait_ge(h_sb, 2 * n + 2)
                if k == 0 and c >= 2:
                    pe.wait_ge(u_ready, c - 1)
                for f in range(FC):
                    last = mm(bank(4 + c % 2), w2s[:, b, k, f, :], hid[:, n % 2, f, :],
                              start=(k == 0 and f == 0), stop=(k == 1 and f == FC - 1))
                last.then_inc(y_ps, 1)

            hidden(0)
            for n in range(8):
                if n + 1 < 8:
                    hidden(n + 1)
                outputs(n)
                if n % 2 == 1:
                    c = n // 2
                    pe.wait_ge(u_ready, c + 1)
                    if c >= 2:
                        pe.wait_ge(LN[2]["centred"], c - 1)
                    channel_means(2, c, xs_flat, "mean", 6 + c % 2)
            variances(2, 4)
            spread(2, 0)

        @block.vector
        def _(dve):
            v = nc.vector
            count = [0]

            def step(inst):
                inst.then_inc(dve_step, 1)
                count[0] += 1
                dve.wait_ge(dve_step, count[0])

            for b in range(2):
                dve.wait_ge(x_in_sem[b], 16)
                v.bn_stats(bn6[:, 2 * b, :], x[:, b * HW:b * HW + 512]).then_inc(dve_step, 1)
                v.bn_stats(bn6[:, 2 * b + 1, :], x[:, b * HW + 512:(b + 1) * HW]).then_inc(dve_step, 1)
                count[0] += 2
            dve.wait_ge(dve_step, count[0])
            mv = st[:, 4:8].rearrange("p (b k) -> p b k", k=2)
            for b in range(2):
                v.bn_aggr(mv[:, b, :], bn6[:, 2 * b:2 * b + 2, :]).then_inc(dve_step, 1)
            count[0] += 2
            dve.wait_ge(dve_step, count[0])
            v.tensor_copy(st[:, 0:2], mv[:, :, 0]).then_inc(gn_stats, 1)
            v.tensor_copy(st[:, 2:4], mv[:, :, 1]).then_inc(gn_stats, 1)
            dve.wait_ge(gn_mean, 1)
            dve.wait_ge(gn_stats, 2)
            step(v.tensor_copy(st[:, 16:18], bank(2, 0, 2)))
            step(v.tensor_tensor(st[:, 10:12], st[:, 0:2], st[:, 16:18], ALU.subtract))
            step(v.tensor_tensor(st[:, 12:14], st[:, 10:12], st[:, 10:12], ALU.mult))
            v.tensor_tensor(st[:, 8:10], st[:, 12:14], st[:, 2:4], ALU.add).then_inc(gn_q, 1)
            dve.wait_ge(gn_var, 1)
            v.tensor_scalar(st[:, 22:24], bank(3, 0, 2), 1e-5, None, ALU.add).then_inc(gn_eps, 1)
            dve.wait_ge(gn_root, 1)
            step(v.reciprocal(st[:, 22:24], st[:, 22:24]))
            step(v.scalar_tensor_tensor(st[:, 19:21], st[:, 16:18], -1.0, st[:, 22:24], ALU.mult, ALU.mult))
            v.tensor_copy(st[:, 17:19], st[:, 22:24]).then_inc(gn_aff, 1)
            dve.wait_ge(gn_aff, 1)
            v.tensor_scalar(xg[:, 0:HW], x[:, 0:HW], st[:, 17:18], st[:, 19:20],
                            ALU.mult, ALU.add).then_inc(xg_ready[0], 1)
            vflat = vtok[:, :, :, :].rearrange("p b n c -> p (b n c)")
            for n in range(4):
                dve.wait_ge(v_ps, n + 1)
                v.tensor_copy(vflat[:, n * 512:(n + 1) * 512], bank(n)).then_inc(v_sb, 1)

            def conv_step(it):
                for u in range(UNROLL):
                    if conv_tile(it, u, 1):
                        n, w = conv_tile(it, u, 1)
                        dve.wait_ge(cs_ps, n + 1)
                        v.tensor_scalar(probs[:, w, :], slot(w), 0.0, NEG, ALU.is_equal, ALU.mult)\
                            .then_inc(cg_sb, 1)
                        dve.wait_ge(v_sb, 4)
                        dve.wait_ge(cg_sb, n + 1)
                        v.tensor_tensor_reduce(out=probs[:, w, :], in0=slot(w), in1=probs[:, w, :],
                                               scale=1.0, scalar=-BIG, op0=ALU.add, op1=ALU.max,
                                               accum_out=maxima[:, w:w + 1]).then_inc(cmax_sb, 1)
                        dve.wait_ge(cmax_sb, n + 1)
                        v.tensor_scalar(negmax[:, w:w + 1], maxima[:, w:w + 1], -1.0, None, ALU.mult)\
                            .then_inc(cm_sb, 1)
                    if conv_tile(it, u, 3):
                        n, w = conv_tile(it, u, 3)
                        dve.wait_ge(ce_sb, n + 1)
                        v.reciprocal(precip[:, w:w + 1], psums[:, w:w + 1]).then_inc(cr_sb, 1)
                        dve.wait_ge(co_ps, n + 1)
                        dve.wait_ge(cr_sb, n + 1)
                        v.tensor_scalar(otok[:, w, :], slot(w, 0, P), precip[:, w:w + 1], None, ALU.mult)\
                            .then_inc(co_sb, 1)

            in_loop(dve, 1, CONV_ITERS, conv_step, CONV_ITERS)

            dve.wait_ge(cx_sb, N // P)
            for n in range(4):
                v.bn_stats(bn6[:, n, :], conv_o[:, n * 512:(n + 1) * 512]).then_inc(dve_step, 1)
            count[0] += 4
            dve.wait_ge(dve_step, count[0])
            step(v.bn_aggr(st[:, 24:26], bn6[:, :, :]))
            v.tensor_scalar(st[:, 26:27], st[:, 25:26], 1e-5, None, ALU.add).then_inc(bn_eps, 1)
            dve.wait_ge(bn_root, 1)
            step(v.reciprocal(st[:, 26:27], st[:, 26:27]))
            step(v.tensor_tensor(st[:, 30:31], st[:, 26:27], VEC["L0_conv_gamma"], ALU.mult))
            step(v.tensor_tensor(st[:, 27:28], st[:, 24:25], st[:, 30:31], ALU.mult))
            v.tensor_tensor(st[:, 31:32], VEC["L0_conv_beta"], st[:, 27:28], ALU.subtract).then_inc(bn_aff, 1)
            dve.wait_ge(vb_ps, 1)
            step(v.tensor_copy(vb[:, :, :], bank(6, 0, 3 * HEADS).rearrange("p (h j) -> p j h", j=3)))

            def repeated(part):
                return vb3[:, :, part, :, :]

            def once(tile):
                return tile[:, :, :]

            for part in range(3):
                src = vb if part != 1 else vb_rest
                if part == 2:
                    src = vb
                for a_ in range(3):
                    v.tensor_copy(vb3[:, :, part, a_, :], src[:, :, :]).then_inc(dve_step, 1)
                count[0] += 3
                dve.wait_ge(dve_step, count[0])
                if part < 2:
                    dst = vb_rest if part == 0 else vb
                    step(v.tensor_tensor(dst[:, :, :], src[:, :, :], vb3[:, :, part, 0, :], ALU.subtract))
            v.tensor_copy(st[:, 40:41], st[:, 30:31]).then_inc(vb_sb, 1)
            for n in range(4):
                dve.wait_ge(bn_relu, n + 1)
                v.tensor_tensor(x1[:, n * 512:(n + 1) * 512], x[:, n * 512:(n + 1) * 512],
                                conv_o[:, n * 512:(n + 1) * 512], ALU.add).then_inc(x1_ready, 1)
            dve.wait_ge(vbT_ps, 1)
            vT = vbT[:, :, :, :]
            vp = bank(7, rows=3 * HEADS).bitcast(BF16)
            for n in range(9):
                src = (vp if n < 8 else bank(6, rows=3 * HEADS).bitcast(BF16))[:, (n % 8) * P:(n % 8 + 1) * P]
                inst = v.tensor_copy(vT[:, n % 3, n // 3, :], src)
                if n >= 7:
                    inst.then_inc(vbT_sb, 1)

            def centre(k, c, source, n):
                dve.wait_ge(LN[k]["mean"], c + 1)
                v.tensor_tensor(centred[:, c * 512:(c + 1) * 512], source[:, c * 512:(c + 1) * 512], bank(n),
                                ALU.subtract).then_inc(LN[k]["centred"], 1)

            def scale(k, var_bank, spread_bank, out_to):
                dve.wait_ge(LN[k]["var"], 1)
                v.tensor_scalar(sd[:, :], bank(var_bank, 0, N // P), 1e-5, None, ALU.add).then_inc(LN[k]["eps"], 1)
                dve.wait_ge(LN[k]["sqrt"], 1)
                step(v.reciprocal(sd[:, :], sd[:, :]))
                for i in range(N // P):
                    inst = v.tensor_scalar(diagonals[:, i * P:(i + 1) * P], ident[:, :], sd[:, i:i + 1], None,
                                           ALU.mult)
                    if i % 4 == 3:
                        inst.then_inc(LN[k]["diag"], 1)
                for c in range(4):
                    dve.wait_ge(LN[k]["spread"], c + 1)
                    v.tensor_tensor(out_to[:, c * 512:(c + 1) * 512], centred[:, c * 512:(c + 1) * 512],
                                    bank(spread_bank + c), ALU.mult).then_inc(LN[k]["out"], 1)

            for c in range(4):
                centre(0, c, x1, c)
            scale(0, 4, 0, xn)

            def remainder(kind, b, h, s, count_):
                section = 1 if "keys" in kind else 0
                hi_, lo_, bias = (kT_hi, kT_lo, bqkv) if section else (qT_hi, qT_lo, bqkv_q)
                dve.wait_ge(hi_ready, count_ * 3 + 3)
                for lo, hi, j, _ in groups(section, b):
                    inst = v.scalar_tensor_tensor(lo_[:, b, lo:hi], slot(s, lo, hi), bias[:, j, at_head(h)],
                                                  hi_[:, b, lo:hi].bitcast(F32), ALU.add, ALU.subtract)
                inst.then_inc(split_done, 1)

            for g, kind in enumerate(("keys", "queries")):
                remainder(kind, 0, 0, g, g)

            def head(h):
                zeroth, last = (isinstance(h, int) and h == k for k in (0, HEADS - 1))
                jobs = head_jobs(last)
                order = [n for n in range(len(jobs)) if jobs[n][0] == "score"]
                done_after = {2: 3, 5: 4, 12: 13, 15: 14}
                scores = projected = 0
                for n in order:
                    kind, b, tile = jobs[n]
                    s = (PRE + n) % SLOTS
                    col = h * (2 * TILES) + scores
                    scores += 1
                    dve.wait_ge(job_ps, PRE + h * PER_HEAD + n + 1)
                    v.tensor_reduce(nmax_all[:, at_head(col)], slot(s), AX_X, ALU.max, negate=True)\
                        .then_inc(tile_maxed, 1)
                    if tile == 0 and not zeroth:
                        dve.wait_ge(diag_saved, h * 2)
                    if not (zeroth and n == 0):
                        dve.wait_ge(tile_maxed, h * (4 * TILES) + 2 * scores - 2)
                    v.tensor_tensor_reduce(out=diag_junk[:, :], in0=slot(s, tile * P, (tile + 1) * P),
                                           in1=ident[:, :], scale=1.0, scalar=0.0, op0=ALU.mult, op1=ALU.add,
                                           accum_out=diag8[:, b, tile:tile + 1]).then_inc(tile_maxed, 1)
                    if tile == TILES - 1:
                        dve.wait_ge(tile_maxed, h * (4 * TILES) + 2 * scores)
                        v.tensor_copy(st[:, 42:43], st[:, 30:31]).then_inc(diag_full, 1)
                    if n in done_after and done_after[n] < len(jobs) and jobs[done_after[n]][0] != "score":
                        m = done_after[n]
                        remainder(jobs[m][0], jobs[m][1], h + 1 if "next" in jobs[m][0] else h,
                                  (PRE + m) % SLOTS, h * 4 + PRE + projected)
                        projected += 1

            in_loop(dve, 1, HEADS - 1, head, HEADS - 1)

            dve.wait_ge(diag_saved, 2 * HEADS)
            v.tensor_tensor(a_rest[:, :], diag_all[:, :], nmax_all[:, :], ALU.add).then_inc(a_sum, 1)
            dve.wait_ge(exp_done, HEADS * 2 * TILES)
            step(v.reciprocal(sum_all[:, :], sum_all[:, :]))
            dve.wait_ge(a_exp, 1)
            step(v.tensor_tensor(a_all[:, :], a_all[:, :], sum_all[:, :], ALU.mult))

            def by_tile(tile):
                return tile[:, :].rearrange("p (h n) -> p n h", h=HEADS)

            v.tensor_copy(a3[:, :, 0, :], by_tile(a_all)).then_inc(a3_ready, 1)
            dve.wait_ge(a3_ready, 1)
            step(v.tensor_tensor(by_tile(a_rest), by_tile(a_all), a3[:, :, 0, :], ALU.subtract))
            v.tensor_copy(a3[:, :, 1, :], by_tile(a_rest)).then_inc(a3_ready, 1)
            dve.wait_ge(a3_ready, 2)
            step(v.tensor_tensor(by_tile(a_all), by_tile(a_rest), a3[:, :, 1, :], ALU.subtract))
            v.tensor_copy(a3[:, :, 2, :], by_tile(a_all)).then_inc(a3_ready, 1)

            dve.wait_ge(xv_ready, 6)

            def scale_tokens(h):
                for b in range(2):
                    dve.wait_ge(ab_ps[b], h + 1)
                    if not (isinstance(h, int) and h == 0):
                        dve.wait_ge(xs_used[b], h)
                    v.tensor_tensor(xs[:, b, :], xv[:, b, :], slot(2 + b), ALU.mult).then_inc(xs_sb[b], 1)

            in_loop(dve, 1, HEADS, scale_tokens)

            for b in range(2):
                dve.wait_ge(xs_used[b], HEADS)
                for r in range(3):
                    lo, hi = GROUP_AT[r], GROUP_AT[r + 1]
                    v.scalar_tensor_tensor(t1[:, b * HW + r:(b + 1) * HW:3], slot(b, lo, hi), VEC["L1_attn_b0"],
                                           x1[:, b * HW + r:(b + 1) * HW:3], ALU.add, ALU.add)\
                        .then_inc(t1_ready, 1)
            dve.wait_ge(t1_ready, 6)
            for c in range(4):
                centre(1, c, t1, 4 + c)
            scale(1, 0, 4, xn)
            for b in range(2):
                dve.wait_ge(LN[1]["out"], 2 * b + 2)
                step(v.reduce_sum(mb[:, b:b + 1], xn[:, b * HW:(b + 1) * HW], AX_X))
                v.tensor_scalar(mbb[:, b, :], ones[:, :], mb[:, b:b + 1], 1.0 / HW, ALU.mult, ALU.mult)\
                    .then_inc(mb_ready, 1)

            def spread(col):
                return col.rearrange("p (b o) -> p b o", o=1).broadcast_to([P, 2, E])

            def softmax_head(src, centred_at, col):
                step(v.tensor_reduce(rs_[:, col, :], src, AX_X, ALU.max))
                for b in range(2):
                    inst = v.tensor_scalar(rt[:, centred_at, b, :], src[:, b, :], rs_[:, col, b:b + 1], None,
                                           ALU.subtract)
                    inst.then_inc(dve_step, 1)
                count[0] += 2
                dve.wait_ge(dve_step, count[0])
                v.tensor_copy(st[:, 44:45], st[:, 30:31]).then_inc(r_in, 1)

            def softmax_tail(e_at, out_at, col):
                step(v.reduce_sum(rs_[:, col, :], rt[:, e_at, :, :], AX_X))
                step(v.reciprocal(rs_[:, col + 1, :], rs_[:, col, :]))
                for b in range(2):
                    v.tensor_scalar(rt[:, out_at, b, :], rt[:, e_at, b, :], rs_[:, col + 1, b:b + 1], None,
                                    ALU.mult).then_inc(dve_step, 1)
                count[0] += 2
                dve.wait_ge(dve_step, count[0])

            dve.wait_ge(lg_ps, 1)
            step(v.tensor_copy(rt[:, 0, :, :], bank(7, 0, 2 * E).rearrange("p (b e) -> p b e", b=2)))
            softmax_head(rt[:, 0, :, :], 1, 0)
            dve.wait_ge(r_exp, 1)
            softmax_tail(2, 3, 1)
            step(v.tensor_tensor(rt[:, 4, 0, :], rt[:, 3, 0, :], rt[:, 3, 1, :], ALU.add))
            step(v.tensor_scalar(rt[:, 4, 1, :], rt[:, 4, 0, :], float(N // 2), None, ALU.mult))
            step(v.reciprocal(rt[:, 4, 0, :], rt[:, 4, 1, :]))
            step(v.tensor_scalar(rt[:, 4, 1, :], rt[:, 4, 0, :], CAPACITY, 1.0, ALU.mult, ALU.min))
            for b in range(2):
                step(v.tensor_tensor(rt[:, 3, b, :], rt[:, 3, b, :], rt[:, 4, 1, :], ALU.mult))
            softmax_head(rt[:, 3, :, :], 5, 3)
            dve.wait_ge(r_exp, 2)
            softmax_tail(6, 7, 4)
            for b in range(2):
                step(v.max(rt[:, 8, b, :], rt[:, 7, b, :]))
                v.max_index(top_i[:, b, :], rt[:, 8, b, :], rt[:, 7, b, :]).then_inc(idx_ready, 1)
            v.tensor_tensor(rs_[:, 7, :], rt[:, 8, :, 1], rt[:, 8, :, 0], ALU.subtract).then_inc(r_in, 1)
            dve.wait_ge(r_exp, 3)
            step(v.tensor_scalar(rs_[:, 9, :], rs_[:, 8, :], 1.0, None, ALU.add))
            step(v.reciprocal(rs_[:, 10, :], rs_[:, 9, :]))
            step(v.tensor_tensor(rs_[:, 11, :], rs_[:, 8, :], rs_[:, 10, :], ALU.mult))
            dve.wait_ge(idx_ready, 2)
            for b in range(2):
                for k in range(TOPK):
                    e = dve.value_load(top_i[0:1, b, k:k + 1], min_val=0, max_val=E - 1)
                    v.tensor_copy(b1s[:, b, k, :], b1_all[:, bass.ds(e, 1), :].rearrange("p o f -> p (o f)"))\
                        .then_inc(w2_ready, 1)
                    v.tensor_scalar(w2s[:, b, k, :, :].rearrange("p f c -> p (f c)"),
                                    w2[:, bass.ds(e, 1), :, :].rearrange("p o f c -> p (o f c)"),
                                    rs_[:, 10 + k, b:b + 1], None, ALU.mult).then_inc(w2_ready, 1)
                    v.tensor_scalar(b2s[:, b, k:k + 1], b2_all[:, bass.ds(e, 1)], rs_[:, 10 + k, b:b + 1], None,
                                    ALU.mult).then_inc(w2_ready, 1)
            dve.wait_ge(w2_ready, 12)
            for b in range(2):
                step(v.tensor_tensor(mb[:, b:b + 1], b2s[:, b, 0:1], b2s[:, b, 1:2], ALU.add))
            dve.wait_ge(t1_beta, 1)

            def finish(c):
                dve.wait_ge(LN[2]["out"], c + 1)
                v.scalar_tensor_tensor(conv_o[:, c * 512:(c + 1) * 512], centred[:, c * 512:(c + 1) * 512],
                                       VEC["L1_ffn_gamma"], x1[:, c * 512:(c + 1) * 512], ALU.mult, ALU.add)\
                    .then_inc(out_ready, 1)

            for c in range(4):
                b = c // 2
                dve.wait_ge(y_ps, 2 * c + 2)
                v.scalar_tensor_tensor(xs_flat[:, c * 512:(c + 1) * 512], bank(4 + c % 2), mb[:, b:b + 1],
                                       xn[:, c * 512:(c + 1) * 512], ALU.add, ALU.add).then_inc(u_ready, 1)
                dve.wait_ge(u_ready, c + 1)
                centre(2, c, xs_flat, 6 + c % 2)
            scale(2, 4, 0, centred)
            for c in range(4):
                finish(c)


_INS = ["x", "L0_conv_wq", "L0_conv_bq", "L0_conv_wk", "L0_conv_bk", "L0_conv_wv", "L0_conv_bv",
        "L0_conv_gamma", "L0_conv_beta", "L1_attn_Wqkv", "L1_attn_bqkv", "L1_attn_W0", "L1_attn_b0",
        "L1_ffn_Wr", "L1_ffn_br", "L1_ffn_W1", "L1_ffn_b1", "L1_ffn_W2", "L1_ffn_b2",
        "L1_ffn_gamma", "L1_ffn_beta"]


def kernel(**inputs):
    import ml_dtypes
    import numpy as np
    import concourse.bacc as bacc
    from concourse.bass_utils import run_bass_kernel_spmd

    nc = bacc.Bacc("TRN2", target_bir_lowering=False, num_devices=1)
    arrays, tensors = {}, {}
    for name in _INS:
        a = np.ascontiguousarray(inputs[name])
        arrays[f"in_{name}"] = a
        tensors[name] = nc.dram_tensor(f"in_{name}", a.shape, mybir.dt.from_np(a.dtype), kind="ExternalInput").ap()
    tensors["out"] = nc.dram_tensor("out_0", inputs["x"].shape, F32, kind="ExternalOutput").ap()
    _, _, h, w = inputs["x"].shape
    pair = np.arange(h * w * 49)
    row = pair // 49 // w + pair % 49 // 7 - 3
    col = pair // 49 % w + pair % 49 % 7 - 3
    inside = (row >= 0) & (row < h) & (col >= 0) & (col < w)
    mask = np.full((h * w, h * w), NEG, dtype=ml_dtypes.bfloat16)
    mask[pair[inside] % (h * w), (row * w + col)[inside]] = 0
    arrays["neighbours"] = mask
    tensors["neighbours"] = nc.dram_tensor("neighbours", mask.shape, BF16, kind="ExternalInput").ap()
    build(nc, tensors)
    r = run_bass_kernel_spmd(nc, [arrays], core_ids=[0])
    return r.results[0]["out_0"]
```

```python
from contextlib import ExitStack

import concourse.bass as bass
from concourse import mybir

F32 = mybir.dt.float32
BF16 = mybir.dt.bfloat16
F32R = mybir.dt.float32r
U32 = mybir.dt.uint32
ALU = mybir.AluOpType
ACT = mybir.ActivationFunctionType
AX_X = mybir.AxisListType.X

P = 128
NEG = -1.0e30
BIG = 3.0e38


def build(nc, t):
    x_in, out = t["x"], t["out"]
    B, C, H, W = x_in.shape
    HW = H * W
    N = B * HW
    assert C == P and W == 32 and B == 2

    GN_SIZE = C // 32
    UNROLL = 4
    CONV_ITERS = N // P // UNROLL
    CHUNKS = HW // P

    D = C
    HEADS = t["L1_attn_Wqkv"].shape[1] // (3 * D)
    GROUP_AT = [0]
    for r in range(3):
        GROUP_AT.append(GROUP_AT[-1] + (HW - r + 2) // 3)
    SCORE_SCALE = float(D) ** -0.5
    TILES = HW // P

    E = t["L1_ffn_Wr"].shape[1]
    FF = t["L1_ffn_W1"].shape[2]
    FC = FF // P
    TOPK = 2
    CAPACITY = float(-(-N * 1.25 // E))

    def segments(section, image):
        first_row = (2 * section + image) * HW
        pieces = []
        for r in range(3):
            lo, hi = GROUP_AT[r], GROUP_AT[r + 1]
            cuts = [lo] + [c for c in (512,) if lo < c < hi] + [hi]
            for a, b in zip(cuts, cuts[1:]):
                pieces.append((a, b - a, (first_row + r) % 3, (first_row + r) // 3 + a - lo))
        return pieces

    def groups(section, image):
        first_row = (2 * section + image) * HW
        return [(GROUP_AT[r], GROUP_AT[r + 1], (first_row + r) % 3, (first_row + r) // 3) for r in range(3)]

    ctx = ExitStack()
    with ctx:
        def sb(name, shape, dt=F32):
            return ctx.enter_context(nc.sbuf_tensor(name, shape, dt))

        def sem(name):
            return ctx.enter_context(nc.semaphore(name))

        ps = ctx.enter_context(nc.psum_tensor("ps", [P, 8 * 512], F32))

        def bank(n, lo=0, hi=512, rows=P):
            return ps[0:rows, n * 512 + lo:n * 512 + hi]

        def slot(n, lo=0, hi=1024):
            return ps[:, n * 1024 + lo:n * 1024 + hi]

        ident = sb("ident", [P, P])
        ident_b = sb("ident_b", [P, P], BF16)
        ones = sb("ones", [P, P])
        mean_w = sb("mean_w", [P, P])
        group_w = sb("group_w", [P, P])
        head_sel = sb("head_sel", [9 * HEADS, HEADS, P], BF16)

        x = sb("x", [P, N])
        conv_w = sb("conv_w", [P, 3, C])
        conv_wT = sb("conv_wT", [P, 3, C])
        NVEC = 8
        NROWS = NVEC + E * FC + E
        rows = sb("rows", [NROWS, P])
        cols = sb("cols", [P, NROWS])
        VEC = {n: cols[:, i:i + 1] for i, n in enumerate(
            ["L0_conv_bq", "L0_conv_bk", "L0_conv_bv", "L0_conv_gamma", "L0_conv_beta",
             "L1_attn_b0", "L1_ffn_gamma", "L1_ffn_beta"])}
        b1_all = cols[:, NVEC:NVEC + E * FC].rearrange("p (e f) -> p e f", f=FC)
        b2_all = cols[:, NVEC + E * FC:NROWS]
        wqkv = sb("wqkv", [P, 3, D, HEADS])
        bqkv = sb("bqkv", [P, 3, HEADS])
        bqkv_q = sb("bqkv_q", [P, 3, HEADS])
        w0 = sb("w0", [P, HEADS, D])
        w1 = sb("w1", [P, E, FF])
        w2 = sb("w2", [P, E, FC, D])
        wr = sb("wr", [P, E])
        score_scale = sb("score_scale", [P, 1])
        br = sb("br", [1, E])

        xg = sb("xg", [P, N])
        centred = xg
        with ExitStack() as conv_only:
            conv_k_hi, conv_k_lo = (
                conv_only.enter_context(nc.sbuf_tensor(n, [P, N], F32R)) for n in ("conv_k_hi", "conv_k_lo"))
        squares = sb("squares", [P, N])
        xn = sb("xn", [P, N])
        queries_full = xg[:, 0:HW]
        vtok = sb("vtok", [P, 2, CHUNKS, C])
        conv_o = sb("conv_o", [P, N])
        x1 = sb("x1", [P, N])
        ROWS = N // P
        mean_window = sb("mean_window", [P, 2 * ROWS - 1])
        row_sel = sb("row_sel", [ROWS, ROWS, P])
        rstd = sb("rstd", [ROWS, 2, P])
        norm_eps = sb("norm_eps", [P, 1])
        st = sb("st", [P, 64])
        bn6 = sb("bn6", [P, 4, 6])
        table_probe = sb("table_probe", [P, 8])

        conv_q_hi = sb("conv_q_hi", [P, UNROLL, P], F32R)
        conv_q_lo = sb("conv_q_lo", [P, UNROLL, P], F32R)
        with ExitStack() as early:
            probs = early.enter_context(nc.sbuf_tensor("probs", [P, UNROLL, HW], F32))
            probsT = early.enter_context(nc.sbuf_tensor("probsT", [P, UNROLL, HW], F32))
        with ExitStack() as middle:
            kT_hi, kT_lo, qT_hi, qT_lo = (
                middle.enter_context(nc.sbuf_tensor(n, [P, 2, HW], F32R)) for n in ("kT_hi", "kT_lo", "qT_hi", "qT_lo"))
        with ExitStack() as values_phase:
            t1, _, xs = (values_phase.enter_context(nc.sbuf_tensor(n, shape, F32)) for n, shape in (
                ("t1", [P, N]), ("between", [P, 2 * N]), ("xs", [P, 2, HW])))
        w2_hi = sb("w2_hi", [P, 2, TOPK, FC, D], F32R)
        w2_lo = sb("w2_lo", [P, 2, TOPK, FC, D], F32R)
        hid_hi = sb("hid_hi", [P, 2, FC, 512], F32R)
        hid_lo = sb("hid_lo", [P, 2, FC, 512], F32R)
        w1_hi = sb("w1_hi", [P, 2, TOPK, FF], F32R)
        w1_lo = sb("w1_lo", [P, 2, TOPK, FF], F32R)
        negmax = sb("negmax", [P, UNROLL])
        maxima = sb("maxima", [P, UNROLL])
        psums = sb("psums", [P, UNROLL])
        precip = sb("precip", [P, UNROLL])
        otok = sb("otok", [P, UNROLL, C])

        w_head = sb("w_head", [P, 2, 3, D])
        fold = sb("fold", [P, HEADS, 3, D])
        with ExitStack() as conv_mask:
            neighbours = conv_mask.enter_context(nc.sbuf_tensor("neighbours_sb", [P, TILES, HW], BF16))
        xn_hi = sb("xn_hi", [P, N], F32R)
        xn_lo = sb("xn_lo", [P, N], F32R)
        exps = sb("exps", [P, 2, HW], BF16)
        diag_junk = sb("diag_junk", [P, P])
        diag8 = sb("diag8", [P, 2, TILES])
        diag_all = sb("diag_all", [P, HEADS * 2 * TILES])
        nmax_all = sb("nmax_all", [P, HEADS * 2 * TILES])
        sum_all = sb("sum_all", [P, HEADS * 2 * TILES])
        a_all = sb("a_all", [P, HEADS * 2 * TILES])
        a_rest = sb("a_rest", [P, HEADS * 2 * TILES])
        a3 = sb("a3", [P, 2 * TILES, 3, 3, HEADS], BF16)
        aT = sb("aT", [9 * HEADS, 2, HW], BF16)
        vb = sb("vb", [P, 3, HEADS])
        vb_rest = sb("vb_rest", [P, 3, HEADS])
        vb3 = sb("vb3", [P, 3, 3, 3, HEADS], BF16)
        vbT = sb("vbT", [9 * HEADS, 3, P], BF16)
        xv = sb("xv", [P, 2, HW])
        fold_h = w_head
        sel_h = sb("sel_h", [9 * HEADS, 2, P], BF16)

        FOLD_BANKS = 3 * HEADS // 4
        FOLD_AT = (5, 7, 6, 5, 7, 6)

        def wvT(n):
            place = xv[:, :, :].rearrange("p b n -> p (b n)") if n < 4 else \
                vtok[:, :, :, :].rearrange("p b n c -> p (b n c)")
            return place[:, n % 4 * 512:(n % 4 + 1) * 512]

        def wvT_block(n):
            return wvT(n // 4)[:, n % 4 * D:(n % 4 + 1) * D]

        fold_flat = fold[:, :, :, :].rearrange("p h j d -> p (h j d)")

        mb = sb("mb", [P, 4])
        mbb = sb("mbb", [P, 4, P])
        b2sum = sb("b2sum", [P, 2])
        rt = sb("rt", [P, 12, 2, E])
        rs_ = sb("rs_", [P, 16, 2])
        top_i = sb("top_i", [P, 2, E], U32)
        b1s = sb("b1s", [P, 2, TOPK, FC])
        b2s = sb("b2s", [P, 2, TOPK])
        hid = conv_o[:, :].rearrange("p (n f c) -> p n f c", n=2, f=FC)
        tokens_out = xv[:, :, :].rearrange("p b n -> p (b n)")

        x_in_sem = [sem(f"x_landed{b}") for b in range(2)]
        mask_in = sem("mask_landed")
        conv_w_in, rows_in, wqkv_in, w0_in, ffn_in = (sem(n) for n in (
            "conv_w_landed", "rows_landed", "wqkv_landed", "w0_landed", "ffn_landed"))
        out_sem = sem("out_stored")
        consts, ident_made = sem("consts"), sem("ident_made")
        pool_step, dve_step = sem("pool_step"), sem("dve_step")
        gn_stats, gn_mean, gn_q, gn_var, gn_aff = (sem(n) for n in (
            "gn_stats", "gn_mean", "gn_q", "gn_var", "gn_aff"))
        xg_ready = [sem(f"xg_ready{b}") for b in range(2)]
        wT_ps, wT_sb, cols_ps, cols_sb = (sem(n) for n in ("wT_ps", "wT_sb", "cols_ps", "cols_sb"))
        k_ps, k_sb, v_ps, v_sb = (sem(n) for n in ("k_ps", "k_sb", "v_ps", "v_sb"))

        cq_ps, cq_sb, cs_ps, cg_sb, cm_sb, ce_sb, ct_ps, ct_sb, co_ps, co_sb, cx_ps, cr_sb = (
            sem(n) for n in ("cq_ps", "cq_sb", "cs_ps", "cg_sb", "cm_sb", "ce_sb",
                             "ct_ps", "ct_sb", "co_ps", "co_sb", "cx_ps", "cr_sb"))
        cx_sb, cmax_sb = sem("cx_sb"), sem("cmax_sb")
        k_lo_sb, cq_lo = sem("k_lo_sb"), sem("cq_lo")
        gn_eps, gn_root, bn_eps, bn_root = (sem(n) for n in ("gn_eps", "gn_root", "bn_eps", "bn_root"))
        bn_aff, bn_relu, x1_ready = sem("bn_aff"), sem("bn_relu"), sem("x1_ready")
        f_T_ps, f_T_sb, f_m_ps, f_m_sb = (sem(n) for n in ("fold_T_ps", "fold_T_sb", "fold_m_ps", "fold_m_sb"))
        vb3_ready, norm_consts = sem("vb3_ready"), sem("norm_consts")
        vb_ps, vb_sb, vbT_ps, vbT_sb = (sem(n) for n in ("vb_ps", "vb_sb", "vbT_ps", "vbT_sb"))

        def ln_sems(k):
            return {n: sem(f"ln{k}_{n}") for n in (
                "mean", "centred", "square", "var", "sqrt", "rstd", "spread", "out")}

        LN = [ln_sems(k) for k in range(3)]
        hi_ready, k_split, q_full, q_split = (sem(n) for n in ("hi_ready", "k_split", "q_full", "q_split"))
        staged, job_ps, exp_done, tile_maxed, diag_saved = (sem(n) for n in (
            "w_head_staged", "job_ps", "exp_done", "tile_maxed", "diag_saved"))
        bq_ready = sem("bq_ready")
        a_exp, a_sum, a3_ready, aT_ps, aT_sb = (sem(n) for n in ("a_exp", "a_sum", "a3_ready", "aT_ps", "aT_sb"))
        xv_ready = sem("xv_ready")
        v_staged = [sem(f"v_staged{p}") for p in range(2)]
        ab_ps = [sem(f"ab_ps{b}") for b in range(2)]
        xs_sb = [sem(f"xs_sb{b}") for b in range(2)]
        xs_used = [sem(f"xs_used{b}") for b in range(2)]
        t1_ready, t1_beta = sem("t1_ready"), sem("t1_beta")
        mb_ready, lg_ps, r_in, r_exp = (sem(n) for n in ("mb_ready", "logits_ps", "r_in", "r_exp"))
        idx_ready, w1_ready, w2_ready = sem("idx_ready"), sem("w1_ready"), sem("w2_ready")
        h_ps, h_full, h_sb, h_lo, y_ps, u_ready = (sem(n) for n in (
            "h_ps", "h_full", "h_sb", "h_lo", "y_ps", "u_ready"))
        xn_hi_ready, xn_lo_ready = sem("xn_hi_ready"), sem("xn_lo_ready")
        out_ready = sem("out_ready")

        LN_PARTS = [((0, 1, 2, 3),), ((0, 1, 2, 3),), ((0, 1, 2), (3,))]

        def conv_tile(it, u, lag):
            v = (u - lag) % UNROLL
            start = (u - lag) // UNROLL * UNROLL
            if isinstance(it, int):
                n = it * UNROLL + start + v
                return (n, v) if 0 <= n < N // P else None
            return it * UNROLL + (start + v), v

        def conv_row(it, u, lag):
            return it * (UNROLL // 2) + ((u - lag) // UNROLL * (UNROLL // 2) + (u - lag) % UNROLL // 2)

        def at_row(it, u, lag, size):
            row = conv_row(it, u, lag)
            return slice(row * size, (row + 1) * size) if isinstance(it, int) else bass.ds(row * size, size)

        def in_loop(eng, first, end, body, *tail):
            for i in range(first):
                body(i)
            with eng.Fori(first, end) as i:
                body(i)
            for i in tail:
                body(i)

        def at_head(h):
            return slice(h, h + 1) if isinstance(h, int) else bass.ds(h, 1)

        def head_jobs(last, keys_at, queries_at):
            jobs = []
            for b in range(2):
                name, image = (("", 1), ("next ", 0))[b]
                for n in range(TILES):
                    for kind, at in (("keys", keys_at), ("queries", queries_at)):
                        if n == at and not (b and last):
                            jobs.append((name + kind, image, 0))
                    jobs.append(("score", b, n))
            return jobs

        def tensor_jobs(last):
            return head_jobs(last, 1, 1)

        def scalar_jobs(last):
            return head_jobs(last, 0, 1)

        def vector_jobs(last):
            return head_jobs(last, 1, 1)

        PRE = 2
        PER_HEAD = 2 * TILES + 4
        SLOTS = 4

        block = ctx.enter_context(nc.Block())

        @block.sync
        def _(sp):
            xf = x_in.rearrange("b c h w -> c b (h w)")
            for b in range(2):
                sp.dma_start(x[:, b * HW:(b + 1) * HW], xf[:, b, :]).then_inc(x_in_sem[b], 16)
            for i in range(0, NVEC, 2):
                n = list(VEC)[i]
                sp.dma_start(rows[i:i + 1, :], t[n].rearrange("(a c) -> a c", a=1)).then_inc(rows_in, 16)
            sp.dma_start(bqkv[:, :, :],
                         t["L1_attn_bqkv"].rearrange("(j d h) -> d j h", j=3, h=HEADS)).then_inc(wqkv_in, 16)
            sp.wait_ge(conv_w_in, 48)
            sp.wait_ge(rows_in, 16 * (NVEC + 2))
            sp.dma_start(neighbours[:, :, :], t["neighbours"].rearrange("(i p) k -> p i k", p=P)).then_inc(mask_in, 16)
            sp.dma_start(wqkv[:, :, :, :],
                         t["L1_attn_Wqkv"].rearrange("c (j d h) -> c j d h", j=3, h=HEADS)).then_inc(wqkv_in, 16)
            sp.dma_start(w1[:, :, :], t["L1_ffn_W1"].rearrange("e c f -> c e f")).then_inc(ffn_in, 16)
            sp.dma_start(w2[:, :, :, :],
                         t["L1_ffn_W2"].rearrange("e (g f) c -> f e g c", f=P)).then_inc(ffn_in, 16)
            sp.dma_start(wr[:, :], t["L1_ffn_Wr"]).then_inc(ffn_in, 16)
            sp.dma_start(br[:, :], t["L1_ffn_br"].rearrange("(a e) -> a e", a=1)).then_inc(ffn_in, 16)
            of = out.rearrange("b c h w -> c b (h w)")
            for n in range(4):
                sp.wait_ge(out_ready, n + 1)
                b, half = n // 2, n % 2
                sp.dma_start(of[:, b, half * 512:(half + 1) * 512],
                             conv_o[:, n * 512:(n + 1) * 512]).then_inc(out_sem, 16)
            sp.wait_ge(out_sem, 64)

        @block.gpsimd
        def _(pool):
            g = nc.gpsimd
            count = [0]

            def step(inst):
                inst.then_inc(pool_step, 1)
                count[0] += 1
                pool.wait_ge(pool_step, count[0])

            step(g.memset(ident[:, :], 0.0))
            g.affine_select(out=ident[:, :], in_=ident[:, :], compare_op=ALU.not_equal, fill=1.0, base=0,
                            pattern=[[-1, P]], channel_multiplier=1).then_inc(ident_made, 1)
            pool.wait_ge(ident_made, 1)
            g.tensor_copy(ident_b[:, :], ident[:, :]).then_inc(consts, 1)
            g.memset(ones[:, :], 1.0).then_inc(consts, 1)
            g.memset(mean_w[:, :], 1.0 / C).then_inc(consts, 1)
            gv = group_w[:, :].rearrange("p (g k) -> p g k", k=GN_SIZE)
            step(g.memset(group_w[:, :], 1.0 / GN_SIZE))
            step(g.affine_select(out=gv, in_=gv, compare_op=ALU.is_ge, fill=0.0, base=0,
                                 pattern=[[-GN_SIZE, C // GN_SIZE], [0, GN_SIZE]], channel_multiplier=1))
            g.affine_select(out=gv, in_=gv, compare_op=ALU.is_ge, fill=0.0, base=GN_SIZE - 1,
                            pattern=[[GN_SIZE, C // GN_SIZE], [0, GN_SIZE]], channel_multiplier=-1)\
                .then_inc(consts, 1)
            g.memset(norm_eps[:, :], 1e-5).then_inc(norm_consts, 1)
            step(g.memset(mean_window[:, :], 0.0))
            g.memset(mean_window[:, ROWS - 1:ROWS], 1.0 / C).then_inc(norm_consts, 1)
            step(g.memset(row_sel[:, :, :], 0.0))
            g.affine_select(out=row_sel[:, :, :], in_=row_sel[:, :, :], compare_op=ALU.not_equal, fill=1.0,
                            base=0, pattern=[[-1, ROWS], [0, P]], channel_multiplier=1).then_inc(norm_consts, 1)
            step(g.memset(head_sel[:, :, :], 0.0))
            for part in range(3):
                inst = g.affine_select(out=head_sel[:, :, :], in_=head_sel[:, :, :], compare_op=ALU.not_equal,
                                       fill=1.0, base=-part * HEADS, pattern=[[-1, HEADS], [0, P]],
                                       channel_multiplier=1)
                if part < 2:
                    step(inst)
                else:
                    inst.then_inc(consts, 1)

            pool.wait_ge(wqkv_in, 32)
            step(g.memset(score_scale[:, :], SCORE_SCALE))
            g.tensor_scalar(bqkv_q[:, :, :], bqkv[:, :, :], SCORE_SCALE, None, ALU.mult).then_inc(bq_ready, 1)
            def stage(h):
                src = wqkv[:, :, :, at_head(h)].rearrange("p j d o -> p j (d o)")
                g.tensor_copy(w_head[:, 0, :, :], src).then_inc(staged, 1)
                g.tensor_tensor(w_head[:, 1, :, :], src, score_scale[:, 0:1].broadcast_to([P, 3 * D])
                                .rearrange("p (j d) -> p j d", j=3), ALU.mult).then_inc(staged, 1)

            stage(0)

            pool.wait_ge(vb_sb, 1)
            for part, (src, rest) in enumerate(((vb, vb_rest), (vb_rest, vb), (vb, None))):
                for copy in range(3):
                    g.tensor_copy(vb3[:, :, part, copy, :], src[:, :, :]).then_inc(vb3_ready, 1)
                pool.wait_ge(vb3_ready, 3 * part + 3)
                if rest is not None:
                    step(g.tensor_tensor(rest[:, :, :], src[:, :, :], vb3[:, :, part, 0, :], ALU.subtract))

            def queries_remainder(b, count):
                pool.wait_ge(q_full, count * 3 + 3)
                g.tensor_tensor(qT_lo[:, b, :], queries_full, qT_hi[:, b, :].bitcast(F32), ALU.subtract)\
                    .then_inc(q_split, 1)

            queries_remainder(0, 0)

            def head(h):
                last = isinstance(h, int) and h == HEADS - 1
                for b in range(2):
                    if b == 0:
                        queries_remainder(1, h * 2 + 1)
                        if last:
                            for image in range(2):
                                for lo, hi, _, tok in groups(2, image):
                                    g.tensor_copy(xv[:, image, lo:hi], xn[:, tok:tok + hi - lo])\
                                        .then_inc(xv_ready, 1)
                        else:
                            pool.wait_ge(job_ps, PRE + h * PER_HEAD + tensor_jobs(False).index(("queries", 1, 0)) + 1)
                            stage(h + 1)
                    elif not last:
                        queries_remainder(0, h * 2 + 2)
                    pool.wait_ge(tile_maxed, h * (4 * TILES) + (b + 1) * 2 * TILES)
                    g.tensor_copy(diag_all[:, bass.ds(h * (2 * TILES) + b * TILES, TILES)], diag8[:, b, :])\
                        .then_inc(diag_saved, 1)

            in_loop(pool, 1, HEADS - 1, head, HEADS - 1)

            def stage_values(h2):
                for p in range(2):
                    if not (isinstance(h2, int) and h2 == 0):
                        pool.wait_ge(xs_used[1], h2 * 2 + p - 1)
                    pair = h2 * 2 + p
                    g.tensor_copy(sel_h[:, p, :], head_sel[:, at_head(pair), :].rearrange("p o m -> p (o m)"))\
                        .then_inc(v_staged[p], 1)
                    g.tensor_copy(fold_h[:, p, :, :], fold[:, at_head(pair), :, :]
                                  .rearrange("p o j d -> p (o j) d")).then_inc(v_staged[p], 1)

            in_loop(pool, 1, HEADS // 2, stage_values)

            for c in range(4):
                pool.wait_ge(xn_hi_ready, c + 1)
                at = slice(c * 512, (c + 1) * 512)
                g.tensor_tensor(xn_lo[:, at], xn[:, at], xn_hi[:, at].bitcast(F32), ALU.subtract)\
                    .then_inc(xn_lo_ready, 1)

            pool.wait_ge(idx_ready, 2)
            pool.wait_ge(xs_used[1], HEADS)
            for b in range(2):
                for k in range(TOPK):
                    n = b * TOPK + k
                    e = pool.value_load(top_i[0:1, b, k:k + 1], min_val=0, max_val=E - 1)
                    chosen = w1[:, bass.ds(e, 1), :].rearrange("p o f -> p (o f)")
                    g.tensor_copy(w1_hi[:, b, k, :], chosen).then_inc(w1_ready, 1)
                    pool.wait_ge(w1_ready, 2 * n + 1)
                    g.tensor_tensor(w1_lo[:, b, k, :], chosen, w1_hi[:, b, k, :].bitcast(F32), ALU.subtract)\
                        .then_inc(w1_ready, 1)

        @block.scalar
        def _(act):
            a = nc.scalar
            for j, n in enumerate(["wq", "wk", "wv"]):
                act.dma_start(conv_w[:, j, :], t[f"L0_conv_{n}"]).then_inc(conv_w_in, 16)
            act.dma_start(rows[NVEC:NVEC + E * FC, :],
                          t["L1_ffn_b1"].rearrange("e (g f) -> (e g) f", f=P)).then_inc(rows_in, 16)
            act.dma_start(rows[NVEC + E * FC:NROWS, :], t["L1_ffn_b2"]).then_inc(rows_in, 16)
            for i in range(1, NVEC, 2):
                n = list(VEC)[i]
                act.dma_start(rows[i:i + 1, :], t[n].rearrange("(a c) -> a c", a=1)).then_inc(rows_in, 16)
            act.dma_start(w0[:, :, :], t["L1_attn_W0"].rearrange("(d h) c -> d h c", h=HEADS)).then_inc(w0_in, 16)

            probes = [0]

            def load_table(function):
                n = probes[0]
                probes[0] += 1
                a.activation(table_probe[:, n:n + 1], ones[:, 0:1], function)

            act.wait_ge(consts, 4)
            load_table(ACT.Sqrt)
            act.wait_ge(wT_ps, 1)
            a.copy(conv_wT[:, :, :], bank(0, 0, 3 * C).rearrange("p (j c) -> p j c", j=3)).then_inc(wT_sb, 1)
            act.wait_ge(gn_eps, 1)
            a.activation(st[:, 22:24], st[:, 22:24], ACT.Sqrt).then_inc(gn_root, 1)
            act.wait_ge(gn_aff, 1)
            a.activation(xg[:, HW:N], x[:, HW:N], ACT.Identity,
                         scale=st[:, 18:19], bias=st[:, 20:21]).then_inc(xg_ready[1], 1)
            act.wait_ge(cols_ps, 1)
            a.copy(cols[:, :], bank(1, 0, NROWS)).then_inc(cols_sb, 1)
            act.wait_ge(cols_sb, 1)
            for n in range(4):
                act.wait_ge(k_ps, n + 1)
                a.activation(conv_k_hi[:, n * 512:(n + 1) * 512], bank(4 + n), ACT.Identity,
                             bias=VEC["L0_conv_bk"]).then_inc(k_sb, 1)

            load_table(ACT.Exp)

            def conv_step(it):
                for u in range(UNROLL):
                    exponentiate(it, u)
                    if conv_tile(it, u, 4):
                        n, v = conv_tile(it, u, 4)
                        act.wait_ge(cx_ps, n + 1)
                        a.activation(conv_o2[:, v % 2, at_row(it, u, 4, P)], slot(v, 0, P), ACT.Identity,
                                     bias=VEC["L0_conv_bv"]).then_inc(cx_sb, 1)
                    if conv_tile(it, u, 0):
                        n, v = conv_tile(it, u, 0)
                        act.wait_ge(cq_ps, n + 1)
                        a.activation(conv_q_hi[:, v, :], slot(v, 0, P), ACT.Identity,
                                     bias=VEC["L0_conv_bq"]).then_inc(cq_sb, 1)
                    if conv_tile(it, u, 2):
                        n, v = conv_tile(it, u, 2)
                        act.wait_ge(ct_ps, n + 1)
                        a.copy(probsT[:, v, :], slot(v)).then_inc(ct_sb, 1)

            def exponentiate(it, u):
                if conv_tile(it, u, 2):
                    n, v = conv_tile(it, u, 2)
                    act.wait_ge(cm_sb, n + 1)
                    a.activation(probs[:, v, :], probs[:, v, :], ACT.Exp, bias=negmax[:, v:v + 1],
                                 accum_out=psums[:, v:v + 1]).then_inc(ce_sb, 1)

            conv_o2 = conv_o[:, :].rearrange("p (b n) -> p b n", b=2)
            in_loop(act, 1, CONV_ITERS, conv_step, CONV_ITERS)

            load_table(ACT.Sqrt)
            def take_transposed(first, end):
                for n in range(first, end):
                    act.wait_ge(f_T_ps, n + 1)
                    a.copy(wvT(n), bank(n)).then_inc(f_T_sb, 1)

            def take_folded(first, end):
                for n in range(first, end):
                    act.wait_ge(f_m_ps, n + 1)
                    a.copy(fold_flat[:, n * 512:(n + 1) * 512], bank(FOLD_AT[n])).then_inc(f_m_sb, 1)

            take_transposed(0, 2)
            act.wait_ge(bn_eps, 1)
            a.activation(st[:, 26:27], st[:, 26:27], ACT.Sqrt).then_inc(bn_root, 1)
            take_transposed(2, 4)
            act.wait_ge(bn_aff, 1)
            for n in range(4):
                a.activation(conv_o[:, n * 512:(n + 1) * 512], conv_o[:, n * 512:(n + 1) * 512], ACT.Relu,
                             scale=st[:, 30:31], bias=st[:, 31:32]).then_inc(bn_relu, 1)
            take_transposed(4, FOLD_BANKS)

            def squares_of(k):
                for c in range(4):
                    act.wait_ge(LN[k]["centred"], c + 1)
                    a.activation(squares[:, c * 512:(c + 1) * 512], centred[:, c * 512:(c + 1) * 512],
                                 ACT.Square).then_inc(LN[k]["square"], 1)

            def root(k, n, var_bank):
                act.wait_ge(LN[k]["var"], n + 1)
                a.activation(rstd[:, n, :], bank(var_bank, 0, P, rows=ROWS), ACT.Sqrt, bias=norm_eps[0:ROWS, :])\
                    .then_inc(LN[k]["sqrt"], 1)

            squares_of(0)
            take_folded(0, 2)
            act.wait_ge(norm_consts, 3)
            root(0, 0, 4)
            load_table(ACT.Exp)
            take_folded(2, FOLD_BANKS)

            act.wait_ge(bq_ready, 1)

            def evacuate(kind, b, h, s, count):
                section = 1 if "keys" in kind else 0
                dst, bias = (kT_hi, bqkv) if section else (qT_hi, bqkv_q)
                if section == 0 and not (isinstance(count, int) and count == 0):
                    act.wait_ge(q_split, count)
                for lo, hi, j, _ in groups(section, b):
                    a.activation(dst[:, b, lo:hi], slot(s, lo, hi), ACT.Identity, bias=bias[:, j, at_head(h)])\
                        .then_inc(hi_ready, 1)
                if section == 0:
                    for lo, hi, j, _ in groups(section, b):
                        a.activation(queries_full[:, lo:hi], slot(s, lo, hi), ACT.Identity,
                                     bias=bias[:, j, at_head(h)]).then_inc(q_full, 1)

            for g, kind in enumerate(("queries", "keys")):
                act.wait_ge(job_ps, g + 1)
                evacuate(kind, 0, 0, g, 0)

            def head(h):
                last = isinstance(h, int) and h == HEADS - 1
                scores = 0
                for kind, b, tile in scalar_jobs(last):
                    n = tensor_jobs(last).index((kind, b, tile))
                    s = (PRE + n) % SLOTS
                    if kind == "score":
                        col = h * (2 * TILES) + scores
                        at = at_head(col)
                        scores += 1
                        act.wait_ge(tile_maxed, h * (4 * TILES) + 2 * scores)
                        if not (isinstance(h, int) and h == 0 and scores <= 2):
                            act.wait_ge(exp_done, h * (2 * TILES) + scores - 2)
                        a.activation(exps[:, scores % 2, :], slot(s), ACT.Exp, bias=nmax_all[:, at],
                                     accum_out=sum_all[:, at]).then_inc(exp_done, 1)
                    else:
                        act.wait_ge(job_ps, PRE + h * PER_HEAD + n + 1)
                        evacuate(kind, b, h + 1 if "next" in kind else h, s, h * 2 + (2 if "next" in kind else 1))

            in_loop(act, 1, HEADS - 1, head, HEADS - 1)

            act.wait_ge(a_sum, 1)
            a.activation(a_all[:, :], a_rest[:, :], ACT.Exp).then_inc(a_exp, 1)
            for b in range(2):
                act.wait_ge(aT_ps, b + 1)
                a.copy(aT[:, b, :], bank(6 + b, rows=9 * HEADS).bitcast(BF16)[:, 0:HW]).then_inc(aT_sb, 1)

            load_table(ACT.Sqrt)
            squares_of(1)
            root(1, 0, 0)
            load_table(ACT.Exp)
            act.wait_ge(t1_ready, 6)
            a.activation(x1[:, :], t1[:, :], ACT.Identity, bias=VEC["L1_ffn_beta"]).then_inc(t1_beta, 1)
            for c in range(4):
                act.wait_ge(LN[1]["out"], c + 1)
                a.copy(xn_hi[:, c * 512:(c + 1) * 512], xn[:, c * 512:(c + 1) * 512]).then_inc(xn_hi_ready, 1)
            for n, (src, e_at, col) in enumerate((
                    (bank(2, 0, 2 * E).rearrange("p (b e) -> p b e", b=2), 2, 0), (rt[:, 5, :, :], 6, 3))):
                act.wait_ge(r_in, n + 1)
                for b in range(2):
                    a.activation(rt[:, e_at, b, :], src[:, b, :], ACT.Exp, bias=rs_[:, col, b:b + 1],
                                 accum_out=rs_[:, col + 1, b:b + 1]).then_inc(r_exp, 1)
            act.wait_ge(r_in, 3)
            a.activation(rs_[:, 8, :], rs_[:, 7, :], ACT.Exp).then_inc(r_exp, 1)
            load_table(ACT.Gelu)

            def gelu(n):
                b, k = n // 4, n % 2
                act.wait_ge(w2_ready, 4 * (b * TOPK + k) + 1)
                for f in range(FC):
                    act.wait_ge(h_ps, 2 * n + f + 1)
                    if n >= 2:
                        act.wait_ge(h_lo, 2 * n - 3 + f)
                    a.activation(hid[:, n % 2, f, :], bank(2 * (n % 2) + f), ACT.Gelu,
                                 bias=b1s[:, b, k, f:f + 1]).then_inc(h_full, 1)
                for f in range(FC):
                    act.wait_ge(h_full, 2 * n + f + 1)
                    if n >= 2:
                        act.wait_ge(y_ps, n - 1)
                    a.copy(hid_hi[:, n % 2, f, :], hid[:, n % 2, f, :]).then_inc(h_sb, 1)

            def square(c):
                act.wait_ge(LN[2]["centred"], c + 1)
                a.activation(squares[:, c * 512:(c + 1) * 512], centred[:, c * 512:(c + 1) * 512],
                             ACT.Square).then_inc(LN[2]["square"], 1)

            for n in range(8):
                gelu(n)
                if n in (5, 7):
                    square((n - 5) // 2)
            load_table(ACT.Sqrt)
            square(2)
            root(2, 0, 0)
            square(3)
            root(2, 1, 6)

        @block.tensor
        def _(pe):
            mm = nc.tensor.matmul
            pe.wait_ge(ident_made, 1)
            pe.wait_ge(conv_w_in, 48)
            for j in range(3):
                last = nc.tensor.transpose(bank(0, j * C, (j + 1) * C), conv_w[:, j, :], ident[:, :])
            last.then_inc(wT_ps, 1)
            pe.wait_ge(consts, 4)
            pe.wait_ge(gn_stats, 1)
            mm(bank(2, 0, 2), group_w[:, :], st[:, 0:2], start=True, stop=True).then_inc(gn_mean, 1)
            pe.wait_ge(gn_q, 1)
            mm(bank(3, 0, 2), group_w[:, :], st[:, 8:10], start=True, stop=True).then_inc(gn_var, 1)
            pe.wait_ge(rows_in, 16 * (NVEC + 2))
            nc.tensor.transpose(bank(1, 0, NROWS), rows[:, :], ident[0:NROWS, 0:NROWS]).then_inc(cols_ps, 1)
            pe.wait_ge(wT_sb, 1)
            for n in range(4):
                if n % 2 == 0:
                    pe.wait_ge(xg_ready[n // 2], 1)
                mm(bank(4 + n), conv_wT[:, 1, :], xg[:, n * 512:(n + 1) * 512], start=True, stop=True)\
                    .then_inc(k_ps, 1)
            pe.wait_ge(cols_sb, 1)
            for n in range(2 * CHUNKS):
                last = mm(bank(n // 4, (n % 4) * P, (n % 4 + 1) * P), xg[:, n * P:(n + 1) * P],
                          conv_wT[:, 2, :], start=True, stop=True)
                if n % 4 == 3:
                    last.then_inc(v_ps, 1)

            pe.wait_ge(k_sb, 4)
            pe.wait_ge(k_lo_sb, 4)
            pe.wait_ge(v_sb, 4)
            pe.wait_ge(mask_in, 16)
            def conv_step(it):
                for u in range(UNROLL):
                    if conv_tile(it, u, 1):
                        n, v = conv_tile(it, u, 1)
                        pe.wait_ge(cq_lo, n + 1)
                        row = at_head(conv_row(it, u, 1))
                        for half in range(2):
                            lo, hi = half * 512, (half + 1) * 512
                            of_image = slice((v % 2) * HW + lo, (v % 2) * HW + hi)
                            mm(slot(v, lo, hi), conv_q_hi[:, v, :], conv_k_hi[:, of_image], start=True, stop=False)
                            mm(slot(v, lo, hi), conv_q_hi[:, v, :], conv_k_lo[:, of_image], start=False, stop=False)
                            mm(slot(v, lo, hi), conv_q_lo[:, v, :], conv_k_hi[:, of_image], start=False, stop=False)
                            last = mm(slot(v, lo, hi), ident_b[:, :],
                                      neighbours[:, row, lo:hi].rearrange("p o k -> p (o k)"),
                                      start=False, stop=True)
                        last.then_inc(cs_ps, 1)
                    if conv_tile(it, u, 4):
                        n, v = conv_tile(it, u, 4)
                        pe.wait_ge(co_sb, n + 1)
                        nc.tensor.transpose(slot(v, 0, P), otok[:, v, :], ident[:, :]).then_inc(cx_ps, 1)
                    probabilities_transposed(it, u, 0)
                    if conv_tile(it, u, 0):
                        n, v = conv_tile(it, u, 0)
                        if conv_tile(it, u, 4):
                            pe.wait_ge(cx_sb, conv_tile(it, u, 4)[0] + 1)
                        mm(slot(v, 0, P), conv_wT[:, 0, :], xg2[:, v % 2, at_row(it, u, 0, P)],
                           start=True, stop=True).then_inc(cq_ps, 1)
                    probabilities_transposed(it, u, 1)
                    if conv_tile(it, u, 3):
                        n, v = conv_tile(it, u, 3)
                        pe.wait_ge(ct_sb, n + 1)
                        for k in range(CHUNKS):
                            last = mm(slot(v, 0, P), probsT[:, v, k * P:(k + 1) * P], vtok[:, v % 2, k, :],
                                      start=(k == 0), stop=(k == CHUNKS - 1))
                        last.then_inc(co_ps, 1)

            def probabilities_transposed(it, u, half):
                if conv_tile(it, u, 2):
                    n, v = conv_tile(it, u, 2)
                    if half == 0:
                        pe.wait_ge(ce_sb, n + 1)
                    for k in range(half * CHUNKS // 2, (half + 1) * CHUNKS // 2):
                        last = nc.tensor.transpose(slot(v, k * P, (k + 1) * P), probs[:, v, k * P:(k + 1) * P],
                                                   ident[:, :])
                    if half == 1:
                        last.then_inc(ct_ps, 1)

            xg2 = xg[:, :].rearrange("p (b n) -> p b n", b=2)
            in_loop(pe, 1, CONV_ITERS, conv_step, CONV_ITERS)

            pe.wait_ge(wqkv_in, 32)
            pe.wait_ge(cx_sb, N // P)
            for n in range(3 * HEADS):
                last = nc.tensor.transpose(bank(n // 4, n % 4 * D, (n % 4 + 1) * D), wqkv[:, n % 3, :, n // 3],
                                           ident[:, :])
                if n % 4 == 3:
                    last.then_inc(f_T_ps, 1)
            pe.wait_ge(w0_in, 16)
            for h in range(HEADS):
                last = mm(bank(6, 3 * h, 3 * h + 3), w0[:, h, :], bqkv[:, :, h], start=True, stop=True)
            last.then_inc(vb_ps, 1)
            def fold_products(n):
                if n == 2:
                    pe.wait_ge(vb_sb, 1)
                elif n > 2:
                    pe.wait_ge(f_m_sb, n - 2)
                for m in range(4 * n, 4 * n + 4):
                    last = mm(bank(FOLD_AT[n], m % 4 * D, (m % 4 + 1) * D), wvT_block(m), w0[:, m // 3, :],
                              start=True, stop=True)
                last.then_inc(f_m_ps, 1)

            def channel_means(k, c, source, name, n):
                mm(bank(n), mean_w[:, :], source[:, c * 512:(c + 1) * 512], start=True, stop=True)\
                    .then_inc(LN[k][name], 1)

            def variances(k, part, n, c):
                chunks = LN_PARTS[k][part]
                pe.wait_ge(LN[k]["square"], c + 1)
                for i in range(4 * c, 4 * c + 4):
                    last = mm(bank(n, 0, P, rows=ROWS), mean_window[:, ROWS - 1 - i:2 * ROWS - 1 - i],
                              squares[:, i * P:(i + 1) * P], start=i == 4 * chunks[0],
                              stop=i == 4 * chunks[-1] + 3)
                if c == chunks[-1]:
                    last.then_inc(LN[k]["var"], 1)

            def spread(k, c, n):
                part = [c in chunks for chunks in LN_PARTS[k]].index(True)
                pe.wait_ge(LN[k]["rstd"], part + 1)
                for i in range(4 * c, 4 * c + 4):
                    last = mm(bank(n, i % 4 * P, (i % 4 + 1) * P), row_sel[:, i, :], rstd[:, part, :],
                              start=True, stop=True)
                last.then_inc(LN[k]["spread"], 1)

            pe.wait_ge(norm_consts, 3)
            for c in range(4):
                pe.wait_ge(x1_ready, c + 1)
                pe.wait_ge(f_T_sb, c + 1)
                channel_means(0, c, x1, "mean", c)
            pe.wait_ge(f_T_sb, FOLD_BANKS)
            fold_products(0)
            fold_products(1)
            for c in range(4):
                variances(0, 0, 4, c)
            fold_products(2)
            fold_products(3)
            pe.wait_ge(LN[0]["centred"], 4)
            for c in range(4):
                spread(0, c, c)
            fold_products(4)
            fold_products(5)
            pe.wait_ge(vb3_ready, 9)
            for j in range(3):
                last = nc.tensor.transpose(bank(4, rows=9 * HEADS).bitcast(BF16)[:, j * P:(j + 1) * P],
                                           vb3[:, j, :, :, :].rearrange("p q a h -> p (q a h)"), ident_b[:, :])
            last.then_inc(vbT_ps, 1)

            pe.wait_ge(LN[0]["out"], 4)
            pe.wait_ge(staged, 2)

            def project(kind, b, s):
                section = 1 if "keys" in kind else 0
                for at, n, j, tok in segments(section, b):
                    last = mm(slot(s, at, at + n), w_head[:, 1 - section, j, :], xn[:, tok:tok + n], start=True, stop=True)
                last.then_inc(job_ps, 1)

            project("queries", 0, 0)
            project("keys", 0, 1)
            pe.wait_ge(f_m_sb, FOLD_BANKS)
            pe.wait_ge(vbT_sb, 1)

            def head(h):
                zeroth, last_head = (isinstance(h, int) and h == k for k in (0, HEADS - 1))
                scores = 0
                jobs = tensor_jobs(last_head)
                for n, (kind, b, tile) in enumerate(jobs):
                    g = PRE + n
                    before = n - SLOTS
                    order = jobs if before >= 0 else tensor_jobs(False)
                    if order[before][0] == "score" and not (zeroth and before < 0):
                        pe.wait_ge(exp_done, h * (2 * TILES) + sum(o[0] == "score" for o in order[:before + 1])
                                   if before >= 0 else
                                   h * (2 * TILES) - sum(o[0] == "score" for o in order[before:]) + 1)
                    elif before >= 0 and "keys" in order[before][0]:
                        pe.wait_ge(k_split, h * 2 + 1 + sum("keys" in o[0] for o in order[:before + 1]))
                    elif before >= 0:
                        pe.wait_ge(q_full, (h * 2 + 1 + sum("queries" in o[0] for o in order[:before + 1])) * 3)
                    if kind == "score":
                        if tile == 0:
                            pe.wait_ge(k_split, h * 2 + 1 + b)
                            pe.wait_ge(q_split, h * 2 + 1 + b)
                        rows_ = slice(tile * P, (tile + 1) * P)
                        for half in range(2):
                            cols_ = slice(half * 512, (half + 1) * 512)
                            tgt = slot(g % SLOTS, half * 512, (half + 1) * 512)
                            mm(tgt, kT_hi[:, b, rows_], qT_hi[:, b, cols_], start=True, stop=False)
                            mm(tgt, kT_hi[:, b, rows_], qT_lo[:, b, cols_], start=False, stop=False)
                            last = mm(tgt, kT_lo[:, b, rows_], qT_hi[:, b, cols_], start=False, stop=True)
                        last.then_inc(job_ps, 1)
                    else:
                        if kind == "next keys":
                            pe.wait_ge(staged, h * 2 + 4)
                        project(kind, b, g % SLOTS)

            in_loop(pe, 1, HEADS - 1, head, HEADS - 1)

            pe.wait_ge(a3_ready, 3)
            pe.wait_ge(exp_done, HEADS * 2 * TILES)
            for b in range(2):
                tgt = bank(6 + b, rows=9 * HEADS).bitcast(BF16)
                for n in range(TILES):
                    last = nc.tensor.transpose(tgt[:, n * P:(n + 1) * P],
                                               a3[:, b * TILES + n, :, :, :].rearrange("p q a h -> p (q a h)"),
                                               ident_b[:, :])
                last.then_inc(aT_ps, 1)
            pe.wait_ge(aT_sb, 2)
            for b in range(2):
                opened = set()
                for at, n, j, _ in segments(2, b):
                    first = at // 512 not in opened
                    opened.add(at // 512)
                    mm(slot(b, at, at + n), vbT[:, j, :], aT[:, b, at:at + n], start=first, stop=False,
                       skip_group_check=True)
            pe.wait_ge(xv_ready, 6)

            def broadcast(h, p, b):
                if not (isinstance(h, int) and h == 0):
                    pe.wait_ge(xs_sb[b], h)
                for half in range(2):
                    last = mm(slot(2 + b, half * 512, (half + 1) * 512), sel_h[:, p, :],
                              aT[:, b, half * 512:(half + 1) * 512], start=True, stop=True)
                last.then_inc(ab_ps[b], 1)

            def value_products(h, p, b):
                pe.wait_ge(xs_sb[b], h + 1)
                for at, n, j, _ in segments(2, b):
                    last = mm(slot(b, at, at + n), fold_h[:, p, j, :], xs[:, b, at:at + n],
                              start=False, stop=False, skip_group_check=True)
                last.then_inc(xs_used[b], 1)

            def values(h2):
                for p in range(2):
                    h = h2 * 2 + p
                    pe.wait_ge(v_staged[p], h2 * 2 + 2)
                    broadcast(h, p, 0)
                    if not (isinstance(h, int) and h == 0):
                        value_products(h - 1, 1 - p, 1)
                    broadcast(h, p, 1)
                    value_products(h, p, 0)

            in_loop(pe, 1, HEADS // 2, values)
            value_products(HEADS - 1, 1, 1)

            for c in range(4):
                pe.wait_ge(t1_ready, 3 if c < 2 else 6)
                channel_means(1, c, t1, "mean", 4 + c)
            pe.wait_ge(LN[1]["centred"], 4)
            for c in range(4):
                variances(1, 0, 0, c)
            for c in range(4):
                spread(1, c, 4 + c)

            pe.wait_ge(ffn_in, 64)
            for c in range(4):
                pe.wait_ge(mb_ready, c + 1)
                b = c // 2
                mm(bank(2, b * E, (b + 1) * E), mbb[:, c, :], wr[:, :], start=c % 2 == 0, stop=False)
                if c % 2:
                    last = mm(bank(2, b * E, (b + 1) * E), ones[0:1, :], br[:, :], start=False, stop=True)
            last.then_inc(lg_ps, 1)

            def hidden(n):
                b, half, k = n // 4, n // 2 % 2, n % 2
                pe.wait_ge(w1_ready, 2 * (b * TOPK + k) + 2)
                pe.wait_ge(xn_lo_ready, n // 2 + 1)
                if n >= 2:
                    pe.wait_ge(h_full, 2 * n - 2)
                at = slice((n // 2) * 512, (n // 2 + 1) * 512)
                for f in range(FC):
                    of = slice(f * P, (f + 1) * P)
                    tgt = bank(2 * (n % 2) + f)
                    mm(tgt, w1_hi[:, b, k, of], xn_hi[:, at], start=True, stop=False)
                    mm(tgt, w1_hi[:, b, k, of], xn_lo[:, at], start=False, stop=False)
                    mm(tgt, w1_lo[:, b, k, of], xn_hi[:, at], start=False, stop=True).then_inc(h_ps, 1)

            def outputs(n):
                b, half, k = n // 4, n // 2 % 2, n % 2
                c = n // 2
                pe.wait_ge(h_sb, 2 * n + 2)
                pe.wait_ge(h_lo, 2 * n + 2)
                pe.wait_ge(w2_ready, 4 * (b * TOPK + k) + 4)
                if k == 0 and c >= 2:
                    pe.wait_ge(u_ready, c - 1)
                for f in range(FC):
                    tgt = bank(4 + c % 2)
                    mm(tgt, w2_hi[:, b, k, f, :], hid_hi[:, n % 2, f, :], start=(k == 0 and f == 0), stop=False)
                    mm(tgt, w2_hi[:, b, k, f, :], hid_lo[:, n % 2, f, :], start=False, stop=False)
                    last = mm(tgt, w2_lo[:, b, k, f, :], hid_hi[:, n % 2, f, :], start=False,
                              stop=(k == 1 and f == FC - 1))
                last.then_inc(y_ps, 1)

            def last_means(c):
                pe.wait_ge(u_ready, c + 1)
                if c >= 2:
                    pe.wait_ge(LN[2]["centred"], c - 1)
                channel_means(2, c, tokens_out, "mean", 6 + c % 2)

            hidden(0)
            hidden(1)
            for n in range(8):
                outputs(n)
                if n + 2 < 8:
                    hidden(n + 2)
                if n in (2, 4, 6):
                    last_means(n // 2 - 1)
                if n == 6:
                    variances(2, 0, 0, 0)
                    variances(2, 0, 0, 1)
            variances(2, 0, 0, 2)
            last_means(3)
            for c in range(3):
                spread(2, c, 1 + c)
            pe.wait_ge(u_ready, 4)
            variances(2, 1, 6, 3)
            spread(2, 3, 4)

        @block.vector
        def _(dve):
            v = nc.vector
            count = [0]

            def step(inst):
                inst.then_inc(dve_step, 1)
                count[0] += 1
                dve.wait_ge(dve_step, count[0])

            for b in range(2):
                dve.wait_ge(x_in_sem[b], 16)
                v.bn_stats(bn6[:, 2 * b, :], x[:, b * HW:b * HW + 512]).then_inc(dve_step, 1)
                v.bn_stats(bn6[:, 2 * b + 1, :], x[:, b * HW + 512:(b + 1) * HW]).then_inc(dve_step, 1)
                count[0] += 2
            dve.wait_ge(dve_step, count[0])
            mv = st[:, 4:8].rearrange("p (b k) -> p b k", k=2)
            for b in range(2):
                v.bn_aggr(mv[:, b, :], bn6[:, 2 * b:2 * b + 2, :]).then_inc(dve_step, 1)
            count[0] += 2
            dve.wait_ge(dve_step, count[0])
            v.tensor_copy(st[:, 0:2], mv[:, :, 0]).then_inc(gn_stats, 1)
            v.tensor_copy(st[:, 2:4], mv[:, :, 1]).then_inc(gn_stats, 1)
            dve.wait_ge(gn_mean, 1)
            dve.wait_ge(gn_stats, 2)
            step(v.tensor_copy(st[:, 16:18], bank(2, 0, 2)))
            step(v.tensor_tensor(st[:, 10:12], st[:, 0:2], st[:, 16:18], ALU.subtract))
            step(v.tensor_tensor(st[:, 12:14], st[:, 10:12], st[:, 10:12], ALU.mult))
            v.tensor_tensor(st[:, 8:10], st[:, 12:14], st[:, 2:4], ALU.add).then_inc(gn_q, 1)
            dve.wait_ge(gn_var, 1)
            v.tensor_scalar(st[:, 22:24], bank(3, 0, 2), 1e-5, None, ALU.add).then_inc(gn_eps, 1)
            dve.wait_ge(gn_root, 1)
            step(v.reciprocal(st[:, 22:24], st[:, 22:24]))
            step(v.scalar_tensor_tensor(st[:, 19:21], st[:, 16:18], -1.0, st[:, 22:24], ALU.mult, ALU.mult))
            v.tensor_copy(st[:, 17:19], st[:, 22:24]).then_inc(gn_aff, 1)
            dve.wait_ge(gn_aff, 1)
            v.tensor_scalar(xg[:, 0:HW], x[:, 0:HW], st[:, 17:18], st[:, 19:20],
                            ALU.mult, ALU.add).then_inc(xg_ready[0], 1)
            for n in range(4):
                at = slice(n * 512, (n + 1) * 512)
                dve.wait_ge(k_sb, n + 1)
                v.scalar_tensor_tensor(conv_k_lo[:, at], bank(4 + n), VEC["L0_conv_bk"],
                                       conv_k_hi[:, at].bitcast(F32), ALU.add, ALU.subtract).then_inc(k_lo_sb, 1)
            vflat = vtok[:, :, :, :].rearrange("p b n c -> p (b n c)")
            for n in range(4):
                dve.wait_ge(v_ps, n + 1)
                v.tensor_copy(vflat[:, n * 512:(n + 1) * 512], bank(n)).then_inc(v_sb, 1)

            def conv_step(it):
                for u in range(UNROLL):
                    if conv_tile(it, u, 1):
                        n, w = conv_tile(it, u, 1)
                        dve.wait_ge(cs_ps, n + 1)
                        v.tensor_scalar(probs[:, w, :], slot(w), 0.0, NEG, ALU.is_equal, ALU.mult)\
                            .then_inc(cg_sb, 1)
                    if conv_tile(it, u, 0):
                        n, w = conv_tile(it, u, 0)
                        dve.wait_ge(cq_sb, n + 1)
                        v.scalar_tensor_tensor(conv_q_lo[:, w, :], slot(w, 0, P), VEC["L0_conv_bq"],
                                               conv_q_hi[:, w, :].bitcast(F32), ALU.add, ALU.subtract)\
                            .then_inc(cq_lo, 1)
                    if conv_tile(it, u, 1):
                        n, w = conv_tile(it, u, 1)
                        dve.wait_ge(v_sb, 4)
                        dve.wait_ge(cg_sb, n + 1)
                        v.tensor_tensor_reduce(out=probs[:, w, :], in0=slot(w), in1=probs[:, w, :],
                                               scale=1.0, scalar=-BIG, op0=ALU.add, op1=ALU.max,
                                               accum_out=maxima[:, w:w + 1]).then_inc(cmax_sb, 1)
                        dve.wait_ge(cmax_sb, n + 1)
                        v.tensor_scalar(negmax[:, w:w + 1], maxima[:, w:w + 1], -1.0, None, ALU.mult)\
                            .then_inc(cm_sb, 1)
                    if conv_tile(it, u, 3):
                        n, w = conv_tile(it, u, 3)
                        dve.wait_ge(ce_sb, n + 1)
                        v.reciprocal(precip[:, w:w + 1], psums[:, w:w + 1]).then_inc(cr_sb, 1)
                        dve.wait_ge(co_ps, n + 1)
                        dve.wait_ge(cr_sb, n + 1)
                        v.tensor_scalar(otok[:, w, :], slot(w, 0, P), precip[:, w:w + 1], None, ALU.mult)\
                            .then_inc(co_sb, 1)
                    if isinstance(it, int) and it == CONV_ITERS and u == 1:
                        dve.wait_ge(cx_sb, N // P // 2)
                        for c in (0, 2):
                            channel_stats(c)

            def channel_stats(c):
                v.bn_stats(bn6[:, c, :], conv_o[:, c * 512:(c + 1) * 512]).then_inc(dve_step, 1)
                count[0] += 1

            in_loop(dve, 1, CONV_ITERS, conv_step, CONV_ITERS)

            dve.wait_ge(cx_sb, N // P)
            for c in (1, 3):
                channel_stats(c)
            dve.wait_ge(dve_step, count[0])
            step(v.bn_aggr(st[:, 24:26], bn6[:, :, :]))
            v.tensor_scalar(st[:, 26:27], st[:, 25:26], 1e-5, None, ALU.add).then_inc(bn_eps, 1)
            dve.wait_ge(bn_root, 1)
            step(v.reciprocal(st[:, 26:27], st[:, 26:27]))
            step(v.tensor_tensor(st[:, 30:31], st[:, 26:27], VEC["L0_conv_gamma"], ALU.mult))
            step(v.tensor_tensor(st[:, 27:28], st[:, 24:25], st[:, 30:31], ALU.mult))
            v.tensor_tensor(st[:, 31:32], VEC["L0_conv_beta"], st[:, 27:28], ALU.subtract).then_inc(bn_aff, 1)
            dve.wait_ge(vb_ps, 1)
            v.tensor_copy(vb[:, :, :], bank(6, 0, 3 * HEADS).rearrange("p (h j) -> p j h", j=3)).then_inc(vb_sb, 1)
            for n in range(4):
                dve.wait_ge(bn_relu, n + 1)
                v.tensor_tensor(x1[:, n * 512:(n + 1) * 512], x[:, n * 512:(n + 1) * 512],
                                conv_o[:, n * 512:(n + 1) * 512], ALU.add).then_inc(x1_ready, 1)
            def centre(k, c, source, n):
                dve.wait_ge(LN[k]["mean"], c + 1)
                v.tensor_tensor(centred[:, c * 512:(c + 1) * 512], source[:, c * 512:(c + 1) * 512], bank(n),
                                ALU.subtract).then_inc(LN[k]["centred"], 1)

            def reciprocals(k, n):
                dve.wait_ge(LN[k]["sqrt"], n + 1)
                v.reciprocal(rstd[:, n, :], rstd[:, n, :]).then_inc(LN[k]["rstd"], 1)

            def normalise(k, c, spread_bank, out_to, sums=None):
                dve.wait_ge(LN[k]["spread"], c + 1)
                at = slice(c * 512, (c + 1) * 512)
                if sums is None:
                    inst = v.tensor_tensor(out_to[:, at], centred[:, at], bank(spread_bank), ALU.mult)
                else:
                    inst = v.tensor_tensor_reduce(out=out_to[:, at], in0=bank(spread_bank), in1=centred[:, at],
                                                  scale=1.0, scalar=0.0, op0=ALU.mult, op1=ALU.add, accum_out=sums)
                inst.then_inc(LN[k]["out"], 1)

            for c in range(4):
                centre(0, c, x1, c)
            reciprocals(0, 0)
            for c in range(4):
                normalise(0, c, c, xn)
            dve.wait_ge(vbT_ps, 1)
            v.tensor_copy(vbT[:, :, :], bank(4, rows=9 * HEADS).bitcast(BF16)[:, 0:3 * P]
                          .rearrange("k (j p) -> k j p", j=3)).then_inc(vbT_sb, 1)

            def keys_remainder(b, h, s, count):
                dve.wait_ge(hi_ready, 6 if isinstance(count, int) and count == 0 else count * 6 + 3)
                for lo, hi, j, _ in groups(1, b):
                    inst = v.scalar_tensor_tensor(kT_lo[:, b, lo:hi], slot(s, lo, hi), bqkv[:, j, at_head(h)],
                                                  kT_hi[:, b, lo:hi].bitcast(F32), ALU.add, ALU.subtract)
                inst.then_inc(k_split, 1)

            keys_remainder(0, 0, 1, 0)

            def head(h):
                zeroth, last = (isinstance(h, int) and h == k for k in (0, HEADS - 1))
                scores = 0
                for kind, b, tile in vector_jobs(last):
                    n = tensor_jobs(last).index((kind, b, tile))
                    s = (PRE + n) % SLOTS
                    if "queries" in kind:
                        continue
                    if "keys" in kind:
                        following = "next" in kind
                        keys_remainder(b, h + 1 if following else h, s, h * 2 + (2 if following else 1))
                        continue
                    col = h * (2 * TILES) + scores
                    scores += 1
                    dve.wait_ge(job_ps, PRE + h * PER_HEAD + n + 1)
                    v.tensor_reduce(nmax_all[:, at_head(col)], slot(s), AX_X, ALU.max, negate=True)\
                        .then_inc(tile_maxed, 1)
                    if tile == 0 and not zeroth:
                        dve.wait_ge(diag_saved, h * 2)
                    if not (zeroth and n == 0):
                        dve.wait_ge(tile_maxed, h * (4 * TILES) + 2 * scores - 2)
                    v.tensor_tensor_reduce(out=diag_junk[:, :], in0=slot(s, tile * P, (tile + 1) * P),
                                           in1=ident[:, :], scale=1.0, scalar=0.0, op0=ALU.mult, op1=ALU.add,
                                           accum_out=diag8[:, b, tile:tile + 1]).then_inc(tile_maxed, 1)

            in_loop(dve, 1, HEADS - 1, head, HEADS - 1)

            dve.wait_ge(diag_saved, 2 * HEADS)
            v.tensor_tensor(a_rest[:, :], diag_all[:, :], nmax_all[:, :], ALU.add).then_inc(a_sum, 1)
            dve.wait_ge(exp_done, HEADS * 2 * TILES)
            step(v.reciprocal(sum_all[:, :], sum_all[:, :]))
            dve.wait_ge(a_exp, 1)
            step(v.tensor_tensor(a_all[:, :], a_all[:, :], sum_all[:, :], ALU.mult))

            def by_tile(tile):
                return tile[:, :].rearrange("p (h n) -> p n h", h=HEADS)

            def part(n, source):
                v.tensor_copy(a3[:, :, :, n, :],
                              source[:, :].rearrange("p (h n o) -> p n o h", h=HEADS, o=1)
                              .broadcast_to([P, 2 * TILES, 3, HEADS])).then_inc(a3_ready, 1)
                dve.wait_ge(a3_ready, n + 1)

            part(0, a_all)
            step(v.tensor_tensor(by_tile(a_rest), by_tile(a_all), a3[:, :, 0, 0, :], ALU.subtract))
            part(1, a_rest)
            step(v.tensor_tensor(by_tile(a_all), by_tile(a_rest), a3[:, :, 0, 1, :], ALU.subtract))
            part(2, a_all)

            dve.wait_ge(xv_ready, 6)

            def scale_tokens(h):
                for b in range(2):
                    dve.wait_ge(ab_ps[b], h + 1)
                    if not (isinstance(h, int) and h == 0):
                        dve.wait_ge(xs_used[b], h)
                    v.tensor_tensor(xs[:, b, :], xv[:, b, :], slot(2 + b), ALU.mult).then_inc(xs_sb[b], 1)

            in_loop(dve, 1, HEADS, scale_tokens)

            for b in range(2):
                dve.wait_ge(xs_used[b], HEADS)
                for r in range(3):
                    lo, hi = GROUP_AT[r], GROUP_AT[r + 1]
                    v.scalar_tensor_tensor(t1[:, b * HW + r:(b + 1) * HW:3], slot(b, lo, hi), VEC["L1_attn_b0"],
                                           x1[:, b * HW + r:(b + 1) * HW:3], ALU.add, ALU.add)\
                        .then_inc(t1_ready, 1)
            dve.wait_ge(t1_ready, 6)
            for c in range(4):
                centre(1, c, t1, 4 + c)
            def chunk_mean(c):
                dve.wait_ge(LN[1]["out"], c + 1)
                v.tensor_scalar(mbb[:, c, :], ones[:, :], mb[:, c:c + 1], 1.0 / HW, ALU.mult, ALU.mult)\
                    .then_inc(mb_ready, 1)

            reciprocals(1, 0)
            for c in range(4):
                normalise(1, c, 4 + c, xn, mb[:, c:c + 1])
                if c:
                    chunk_mean(c - 1)
            chunk_mean(3)

            def softmax_input(src, col):
                v.tensor_reduce(rs_[:, col, :], src, AX_X, ALU.max, negate=True).then_inc(r_in, 1)

            def softmax_output(n, e_at, out_at, col):
                dve.wait_ge(r_exp, n)
                step(v.reciprocal(rs_[:, col + 1, :], rs_[:, col, :]))
                for b in range(2):
                    v.tensor_scalar(rt[:, out_at, b, :], rt[:, e_at, b, :], rs_[:, col + 1, b:b + 1], None,
                                    ALU.mult).then_inc(dve_step, 1)
                count[0] += 2
                dve.wait_ge(dve_step, count[0])

            dve.wait_ge(lg_ps, 1)
            softmax_input(bank(2, 0, 2 * E).rearrange("p (b e) -> p b e", b=2), 0)
            softmax_output(2, 2, 3, 1)
            step(v.tensor_tensor(rt[:, 4, 0, :], rt[:, 3, 0, :], rt[:, 3, 1, :], ALU.add))
            step(v.tensor_scalar(rt[:, 4, 1, :], rt[:, 4, 0, :], float(N // 2), None, ALU.mult))
            step(v.reciprocal(rt[:, 4, 0, :], rt[:, 4, 1, :]))
            step(v.tensor_scalar(rt[:, 4, 1, :], rt[:, 4, 0, :], CAPACITY, 1.0, ALU.mult, ALU.min))
            for b in range(2):
                v.tensor_tensor(rt[:, 5, b, :], rt[:, 3, b, :], rt[:, 4, 1, :], ALU.mult).then_inc(dve_step, 1)
            count[0] += 2
            dve.wait_ge(dve_step, count[0])
            softmax_input(rt[:, 5, :, :], 3)
            softmax_output(4, 6, 7, 4)
            for b in range(2):
                v.max(rt[:, 8, b, :], rt[:, 7, b, :]).then_inc(dve_step, 1)
            count[0] += 2
            dve.wait_ge(dve_step, count[0])
            for b in range(2):
                v.max_index(top_i[:, b, :], rt[:, 8, b, :], rt[:, 7, b, :]).then_inc(idx_ready, 1)
            v.tensor_tensor(rs_[:, 7, :], rt[:, 8, :, 1], rt[:, 8, :, 0], ALU.subtract).then_inc(r_in, 1)
            dve.wait_ge(r_exp, 5)
            step(v.tensor_scalar(rs_[:, 9, :], rs_[:, 8, :], 1.0, None, ALU.add))
            step(v.reciprocal(rs_[:, 10, :], rs_[:, 9, :]))
            step(v.tensor_tensor(rs_[:, 11, :], rs_[:, 8, :], rs_[:, 10, :], ALU.mult))
            dve.wait_ge(t1_beta, 1)

            def second_layer(b):
                for k in range(TOPK):
                    n = b * TOPK + k
                    e = dve.value_load(top_i[0:1, b, k:k + 1], min_val=0, max_val=E - 1)
                    v.tensor_copy(b1s[:, b, k, :], b1_all[:, bass.ds(e, 1), :].rearrange("p o f -> p (o f)"))\
                        .then_inc(w2_ready, 1)
                    chosen = w2[:, bass.ds(e, 1), :, :].rearrange("p o f c -> p (o f c)")
                    hi_, lo_ = (t_[:, b, k, :, :].rearrange("p f c -> p (f c)") for t_ in (w2_hi, w2_lo))
                    v.tensor_scalar(hi_, chosen, rs_[:, 10 + k, b:b + 1], None, ALU.mult).then_inc(w2_ready, 1)
                    v.tensor_scalar(b2s[:, b, k:k + 1], b2_all[:, bass.ds(e, 1)], rs_[:, 10 + k, b:b + 1], None,
                                    ALU.mult).then_inc(w2_ready, 1)
                    dve.wait_ge(w2_ready, 4 * n + 3)
                    v.scalar_tensor_tensor(lo_, chosen, rs_[:, 10 + k, b:b + 1], hi_.bitcast(F32),
                                           ALU.mult, ALU.subtract).then_inc(w2_ready, 1)
                dve.wait_ge(w2_ready, 4 * (b + 1) * TOPK)
                step(v.tensor_tensor(b2sum[:, b:b + 1], b2s[:, b, 0:1], b2s[:, b, 1:2], ALU.add))

            dve.wait_ge(idx_ready, 2)
            second_layer(0)

            def finish(c):
                dve.wait_ge(LN[2]["out"], c + 1)
                v.scalar_tensor_tensor(conv_o[:, c * 512:(c + 1) * 512], centred[:, c * 512:(c + 1) * 512],
                                       VEC["L1_ffn_gamma"], x1[:, c * 512:(c + 1) * 512], ALU.mult, ALU.add)\
                    .then_inc(out_ready, 1)

            def hidden_remainder(n):
                for f in range(FC):
                    dve.wait_ge(h_sb, 2 * n + f + 1)
                    if n >= 2:
                        dve.wait_ge(y_ps, n - 1)
                    v.tensor_tensor(hid_lo[:, n % 2, f, :], hid[:, n % 2, f, :], hid_hi[:, n % 2, f, :].bitcast(F32),
                                    ALU.subtract).then_inc(h_lo, 1)

            def residual(c):
                dve.wait_ge(y_ps, 2 * c + 2)
                v.scalar_tensor_tensor(tokens_out[:, c * 512:(c + 1) * 512], bank(4 + c % 2),
                                       b2sum[:, c // 2:c // 2 + 1], xn[:, c * 512:(c + 1) * 512], ALU.add, ALU.add)\
                    .then_inc(u_ready, 1)

            hidden_remainder(0)
            hidden_remainder(1)
            second_layer(1)
            for c in range(4):
                if c < 3:
                    hidden_remainder(2 * c + 2)
                residual(c)
                if c < 3:
                    hidden_remainder(2 * c + 3)
                else:
                    reciprocals(2, 0)
                dve.wait_ge(u_ready, c + 1)
                centre(2, c, tokens_out, 6 + c % 2)
            for c in range(3):
                normalise(2, c, 1 + c, centred)
                finish(c)
            reciprocals(2, 1)
            normalise(2, 3, 4, centred)
            finish(3)


_INS = ["x", "L0_conv_wq", "L0_conv_bq", "L0_conv_wk", "L0_conv_bk", "L0_conv_wv", "L0_conv_bv",
        "L0_conv_gamma", "L0_conv_beta", "L1_attn_Wqkv", "L1_attn_bqkv", "L1_attn_W0", "L1_attn_b0",
        "L1_ffn_Wr", "L1_ffn_br", "L1_ffn_W1", "L1_ffn_b1", "L1_ffn_W2", "L1_ffn_b2",
        "L1_ffn_gamma", "L1_ffn_beta"]


def kernel(**inputs):
    import ml_dtypes
    import numpy as np
    import concourse.bacc as bacc
    from concourse.bass_utils import run_bass_kernel_spmd

    nc = bacc.Bacc("TRN2", target_bir_lowering=False, num_devices=1)
    arrays, tensors = {}, {}
    for name in _INS:
        a = np.ascontiguousarray(inputs[name])
        arrays[f"in_{name}"] = a
        tensors[name] = nc.dram_tensor(f"in_{name}", a.shape, mybir.dt.from_np(a.dtype), kind="ExternalInput").ap()
    tensors["out"] = nc.dram_tensor("out_0", inputs["x"].shape, F32, kind="ExternalOutput").ap()
    _, _, h, w = inputs["x"].shape
    pair = np.arange(h * w * 49)
    row = pair // 49 // w + pair % 49 // 7 - 3
    col = pair // 49 % w + pair % 49 % 7 - 3
    inside = (row >= 0) & (row < h) & (col >= 0) & (col < w)
    mask = np.full((h * w, h * w), NEG, dtype=ml_dtypes.bfloat16)
    mask[pair[inside] % (h * w), (row * w + col)[inside]] = 0
    arrays["neighbours"] = mask
    tensors["neighbours"] = nc.dram_tensor("neighbours", mask.shape, BF16, kind="ExternalInput").ap()
    build(nc, tensors)
    r = run_bass_kernel_spmd(nc, [arrays], core_ids=[0])
    return r.results[0]["out_0"]
```
